# Optimizing a Trainium2 kernel written in Bass

```python
import numpy as np
import jax
import jax.numpy as jnp

def _softmax(x, axis=-1):
    return jax.nn.softmax(x, axis=axis)

def _gelu(x):
    return jax.nn.gelu(x, approximate=True)

def _silu(x):
    return jax.nn.silu(x)

def _sigmoid(x):
    return jax.nn.sigmoid(x)

def _layernorm(x, axis=-1, eps=1e-05):
    m = jnp.mean(x, axis=axis, keepdims=True)
    v = jnp.var(x, axis=axis, keepdims=True)
    return (x - m) / jnp.sqrt(v + eps)

def _scatter_add(tgt, idx, src, axis=0):
    return tgt.at[idx].add(src)

def _segment_sum(src, seg, n):
    return jax.ops.segment_sum(src, seg, n)
kernel_name = 'mk_seq_postln_d1_jaxref_r8_486377'

def setup_inputs(seed: int=0):
    np.random.seed(seed)
    _w = jnp.asarray

    def _L0_attn_setup():
        import math
        import jax, jax.numpy as jnp
        import numpy as np
        NH = 16
        NOPE = 128
        ROPE = 64
        VD = 128
        QLR = 192
        IH = 8
        ID = 128
        TOPK = 8
        EPS = 1e-05

        def layernorm(x, w, b):
            mu = jnp.mean(x, axis=-1, keepdims=True)
            var = jnp.mean((x - mu) ** 2, axis=-1, keepdims=True)
            return (x - mu) * jax.lax.rsqrt(var + EPS) * w + b

        def rope_tables(dim, end, base=10000.0):
            freqs = 1.0 / base ** (jnp.arange(0, dim, 2, dtype=jnp.float32) / dim)
            t = jnp.arange(end, dtype=jnp.float32)
            f = jnp.outer(t, freqs)
            return (jnp.cos(f), jnp.sin(f))

        def apply_rope(x, cos, sin):
            xr, xi = (x[..., 0::2], x[..., 1::2])
            c = cos[None, None, :, :]
            s = sin[None, None, :, :]
            or_, oi = (xr * c - xi * s, xr * s + xi * c)
            return jnp.stack([or_, oi], axis=-1).reshape(x.shape)

        def _forward(x, W_cq, q_norm_w, q_norm_b, W_q, W_ckv, kv_norm_w, kv_norm_b, W_kv, W_o, W_ip, W_ig, W_sq, W_sk, W_sv, W_io):
            B, S, H = x.shape
            qc = layernorm(x @ W_cq, q_norm_w, q_norm_b)
            qp = (qc @ W_q).reshape(B, S, NH, NOPE + ROPE).transpose(0, 2, 1, 3)
            q_nope, q_pe = (qp[..., :NOPE], qp[..., NOPE:])
            kvc = (x @ W_ckv).reshape(B, S, NH, ROPE + NOPE).transpose(0, 2, 1, 3)
            k_pe, kv_nope = (kvc[..., :ROPE], kvc[..., ROPE:])
            kv_n = layernorm(kv_nope, kv_norm_w, kv_norm_b)
            kvp = kv_n @ W_kv
            k_nope, v = (kvp[..., :NOPE], kvp[..., NOPE:])
            cos, sin = rope_tables(ROPE, S)
            q_pe = apply_rope(q_pe, cos, sin)
            k_pe = apply_rope(k_pe, cos, sin)
            q = jnp.concatenate([q_nope, q_pe], axis=-1)
            k = jnp.concatenate([k_nope, k_pe], axis=-1)
            scale = 1.0 / math.sqrt(NOPE + ROPE)
            scores = jnp.einsum('bhqd,bhkd->bhqk', q, k) * scale
            causal = jnp.triu(jnp.ones((S, S), dtype=bool), k=1)
            scores = jnp.where(causal[None, None], -jnp.inf, scores)
            probs = jax.nn.softmax(scores.astype(jnp.float32), axis=-1).astype(q.dtype)
            attn = jnp.einsum('bhqk,bhkd->bhqd', probs, v)
            ist = (x @ W_ip).reshape(B, S, IH, ID).transpose(0, 2, 1, 3)
            gate = (x @ W_ig).transpose(0, 2, 1)
            _, top_idx = jax.lax.top_k(gate, TOPK)
            sel = jnp.take_along_axis(ist, top_idx[..., None], axis=2)
            sq, sk, sv = (sel @ W_sq, sel @ W_sk, sel @ W_sv)
            ss = jnp.einsum('bhqd,bhkd->bhqk', sq, sk) / math.sqrt(ID)
            sp = jax.nn.softmax(ss.astype(jnp.float32), axis=-1).astype(sq.dtype)
            so = jnp.einsum('bhqk,bhkd->bhqd', sp, sv)
            sparse_out = so @ W_io
            io = sparse_out.mean(axis=2)[:, :, None, :VD]
            io = jnp.broadcast_to(io, (B, IH, S, VD))
            io = jnp.repeat(io, NH // IH, axis=1)
            attn = attn + io
            out = attn.transpose(0, 2, 1, 3).reshape(B, S, NH * VD) @ W_o
            return out
        key = jax.random.key(seed)
        ks = jax.random.split(key, 16)
        H = 256
        B, S = (2, 256)
        w = lambda k, shp: jax.random.normal(k, shp, dtype=jnp.float32) * 0.02
        return {'x': jax.random.normal(ks[0], (B, S, H), dtype=jnp.float32), 'W_cq': w(ks[1], (H, QLR)), 'q_norm_w': jnp.ones((QLR,), jnp.float32), 'q_norm_b': jnp.zeros((QLR,), jnp.float32), 'W_q': w(ks[2], (QLR, NH * (NOPE + ROPE))), 'W_ckv': w(ks[3], (H, NH * (NOPE + ROPE))), 'kv_norm_w': jnp.ones((NOPE,), jnp.float32), 'kv_norm_b': jnp.zeros((NOPE,), jnp.float32), 'W_kv': w(ks[4], (NOPE, NOPE + VD)), 'W_o': w(ks[5], (NH * VD, H)), 'W_ip': w(ks[6], (H, IH * ID)), 'W_ig': w(ks[7], (H, IH)), 'W_sq': w(ks[8], (ID, ID)), 'W_sk': w(ks[9], (ID, ID)), 'W_sv': w(ks[10], (ID, ID)), 'W_io': w(ks[11], (ID, H))}
    _L0_attn_in = _L0_attn_setup()

    def _L0_ffn_setup():
        import jax, jax.numpy as jnp
        import numpy as np
        D_MODEL = 256
        D_EXPERT = 1024
        EPS = 1e-08

        def ternary_quant(w):
            scale = jnp.mean(jnp.abs(w)) + EPS
            q = jnp.clip(jnp.round(w / scale), -1.0, 1.0) * scale
            return w + jax.lax.stop_gradient(q - w)
        key = jax.random.key(seed)
        k_x, k_up, k_gate, k_down = jax.random.split(key, 4)
        std_in = 1.0 / np.sqrt(D_MODEL)
        std_exp = 1.0 / np.sqrt(D_EXPERT)
        return {'x': jax.random.normal(k_x, (4, 256, D_MODEL), dtype=jnp.float32), 'W_up': jax.random.normal(k_up, (D_EXPERT, D_MODEL), dtype=jnp.float32) * std_in, 'W_gate': jax.random.normal(k_gate, (D_EXPERT, D_MODEL), dtype=jnp.float32) * std_in, 'W_down': jax.random.normal(k_down, (D_MODEL, D_EXPERT), dtype=jnp.float32) * std_exp}
    _L0_ffn_in = _L0_ffn_setup()
    _d = {'L0_attn_x': _L0_attn_in['x'], 'L0_attn_W_cq': _L0_attn_in['W_cq'], 'L0_attn_q_norm_w': _L0_attn_in['q_norm_w'], 'L0_attn_q_norm_b': _L0_attn_in['q_norm_b'], 'L0_attn_W_q': _L0_attn_in['W_q'], 'L0_attn_W_ckv': _L0_attn_in['W_ckv'], 'L0_attn_kv_norm_w': _L0_attn_in['kv_norm_w'], 'L0_attn_kv_norm_b': _L0_attn_in['kv_norm_b'], 'L0_attn_W_kv': _L0_attn_in['W_kv'], 'L0_attn_W_o': _L0_attn_in['W_o'], 'L0_attn_W_ip': _L0_attn_in['W_ip'], 'L0_attn_W_ig': _L0_attn_in['W_ig'], 'L0_attn_W_sq': _L0_attn_in['W_sq'], 'L0_attn_W_sk': _L0_attn_in['W_sk'], 'L0_attn_W_sv': _L0_attn_in['W_sv'], 'L0_attn_W_io': _L0_attn_in['W_io'], 'L0_ffn_W_up': _L0_ffn_in['W_up'], 'L0_ffn_W_gate': _L0_ffn_in['W_gate'], 'L0_ffn_W_down': _L0_ffn_in['W_down']}
    _x0 = _d['L0_attn_x']
    _d['L0_attn_x'] = jax.random.normal(jax.random.fold_in(jax.random.key(seed), 1), (1, 1024, 256), dtype=_x0.dtype)
    del _x0
    return _d

def reference(L0_attn_x, L0_attn_W_cq, L0_attn_q_norm_w, L0_attn_q_norm_b, L0_attn_W_q, L0_attn_W_ckv, L0_attn_kv_norm_w, L0_attn_kv_norm_b, L0_attn_W_kv, L0_attn_W_o, L0_attn_W_ip, L0_attn_W_ig, L0_attn_W_sq, L0_attn_W_sk, L0_attn_W_sv, L0_attn_W_io, L0_ffn_W_up, L0_ffn_W_gate, L0_ffn_W_down):

    def _L0_attn_ref(x, W_cq, q_norm_w, q_norm_b, W_q, W_ckv, kv_norm_w, kv_norm_b, W_kv, W_o, W_ip, W_ig, W_sq, W_sk, W_sv, W_io):
        import math
        import jax, jax.numpy as jnp
        import numpy as np
        NH = 16
        NOPE = 128
        ROPE = 64
        VD = 128
        QLR = 192
        IH = 8
        ID = 128
        TOPK = 8
        EPS = 1e-05

        def layernorm(x, w, b):
            mu = jnp.mean(x, axis=-1, keepdims=True)
            var = jnp.mean((x - mu) ** 2, axis=-1, keepdims=True)
            return (x - mu) * jax.lax.rsqrt(var + EPS) * w + b

        def rope_tables(dim, end, base=10000.0):
            freqs = 1.0 / base ** (jnp.arange(0, dim, 2, dtype=jnp.float32) / dim)
            t = jnp.arange(end, dtype=jnp.float32)
            f = jnp.outer(t, freqs)
            return (jnp.cos(f), jnp.sin(f))

        def apply_rope(x, cos, sin):
            xr, xi = (x[..., 0::2], x[..., 1::2])
            c = cos[None, None, :, :]
            s = sin[None, None, :, :]
            or_, oi = (xr * c - xi * s, xr * s + xi * c)
            return jnp.stack([or_, oi], axis=-1).reshape(x.shape)

        def _forward(x, W_cq, q_norm_w, q_norm_b, W_q, W_ckv, kv_norm_w, kv_norm_b, W_kv, W_o, W_ip, W_ig, W_sq, W_sk, W_sv, W_io):
            B, S, H = x.shape
            qc = layernorm(x @ W_cq, q_norm_w, q_norm_b)
            qp = (qc @ W_q).reshape(B, S, NH, NOPE + ROPE).transpose(0, 2, 1, 3)
            q_nope, q_pe = (qp[..., :NOPE], qp[..., NOPE:])
            kvc = (x @ W_ckv).reshape(B, S, NH, ROPE + NOPE).transpose(0, 2, 1, 3)
            k_pe, kv_nope = (kvc[..., :ROPE], kvc[..., ROPE:])
            kv_n = layernorm(kv_nope, kv_norm_w, kv_norm_b)
            kvp = kv_n @ W_kv
            k_nope, v = (kvp[..., :NOPE], kvp[..., NOPE:])
            cos, sin = rope_tables(ROPE, S)
            q_pe = apply_rope(q_pe, cos, sin)
            k_pe = apply_rope(k_pe, cos, sin)
            q = jnp.concatenate([q_nope, q_pe], axis=-1)
            k = jnp.concatenate([k_nope, k_pe], axis=-1)
            scale = 1.0 / math.sqrt(NOPE + ROPE)
            scores = jnp.einsum('bhqd,bhkd->bhqk', q, k) * scale
            causal = jnp.triu(jnp.ones((S, S), dtype=bool), k=1)
            scores = jnp.where(causal[None, None], -jnp.inf, scores)
            probs = jax.nn.softmax(scores.astype(jnp.float32), axis=-1).astype(q.dtype)
            attn = jnp.einsum('bhqk,bhkd->bhqd', probs, v)
            ist = (x @ W_ip).reshape(B, S, IH, ID).transpose(0, 2, 1, 3)
            gate = (x @ W_ig).transpose(0, 2, 1)
            _, top_idx = jax.lax.top_k(gate, TOPK)
            sel = jnp.take_along_axis(ist, top_idx[..., None], axis=2)
            sq, sk, sv = (sel @ W_sq, sel @ W_sk, sel @ W_sv)
            ss = jnp.einsum('bhqd,bhkd->bhqk', sq, sk) / math.sqrt(ID)
            sp = jax.nn.softmax(ss.astype(jnp.float32), axis=-1).astype(sq.dtype)
            so = jnp.einsum('bhqk,bhkd->bhqd', sp, sv)
            sparse_out = so @ W_io
            io = sparse_out.mean(axis=2)[:, :, None, :VD]
            io = jnp.broadcast_to(io, (B, IH, S, VD))
            io = jnp.repeat(io, NH // IH, axis=1)
            attn = attn + io
            out = attn.transpose(0, 2, 1, 3).reshape(B, S, NH * VD) @ W_o
            return out
        return _forward(x, W_cq, q_norm_w, q_norm_b, W_q, W_ckv, kv_norm_w, kv_norm_b, W_kv, W_o, W_ip, W_ig, W_sq, W_sk, W_sv, W_io)

    def _L0_ffn_ref(x, W_up, W_gate, W_down):
        import jax, jax.numpy as jnp
        import numpy as np
        D_MODEL = 256
        D_EXPERT = 1024
        EPS = 1e-08

        def ternary_quant(w):
            scale = jnp.mean(jnp.abs(w)) + EPS
            q = jnp.clip(jnp.round(w / scale), -1.0, 1.0) * scale
            return w + jax.lax.stop_gradient(q - w)
        wu = ternary_quant(W_up)
        wg = ternary_quant(W_gate)
        wd = ternary_quant(W_down)
        up = jnp.einsum('bsd,ed->bse', x, wu)
        gate = jnp.einsum('bsd,ed->bse', x, wg)
        hidden = jax.nn.silu(up) * gate
        return jnp.einsum('bse,de->bsd', hidden, wd)
    x = L0_attn_x
    x = _layernorm(x + _L0_attn_ref(x, L0_attn_W_cq, L0_attn_q_norm_w, L0_attn_q_norm_b, L0_attn_W_q, L0_attn_W_ckv, L0_attn_kv_norm_w, L0_attn_kv_norm_b, L0_attn_W_kv, L0_attn_W_o, L0_attn_W_ip, L0_attn_W_ig, L0_attn_W_sq, L0_attn_W_sk, L0_attn_W_sv, L0_attn_W_io), axis=-1)
    x = _layernorm(x + _L0_ffn_ref(x, L0_ffn_W_up, L0_ffn_W_gate, L0_ffn_W_down), axis=-1)
    return x

_drawn_inputs = setup_inputs


def setup_inputs(seed=0):
    import zlib

    import numpy as np

    out = dict(_drawn_inputs(seed))
    spreads = {'L0_attn_q_norm_w': (1.0, 0.6),
     'L0_attn_q_norm_b': (0.0, 2.0),
     'L0_attn_kv_norm_w': (1.0, 0.6),
     'L0_attn_kv_norm_b': (0.0, 2.0)}
    factors = {'L0_attn_W_cq': 23.904,
     'L0_attn_W_q': 22.509,
     'L0_attn_W_ckv': 9.192,
     'L0_attn_W_ip': 8.0,
     'L0_attn_W_ig': 8.0,
     'L0_attn_W_sq': 8.0,
     'L0_attn_W_sk': 8.0,
     'L0_attn_W_sv': 8.0,
     'L0_attn_W_io': 8.0}
    for name, (base, spread) in spreads.items():
        noise = np.random.default_rng([zlib.crc32(name.encode()), seed]).standard_normal(out[name].shape)
        drawn = base * np.exp(spread * noise) if base else spread * noise
        out[name] = jnp.asarray(drawn.astype(out[name].dtype))
    for name, factor in factors.items():
        out[name] = (out[name] * factor).astype(out[name].dtype)
    return out
```

```python
import concourse.bass as bass
from concourse import mybir
from contextlib import ExitStack

F32 = mybir.dt.float32
F32R = mybir.dt.float32r
BF16 = mybir.dt.bfloat16
U32 = mybir.dt.uint32
ALU = mybir.AluOpType
ACT = mybir.ActivationFunctionType
AX = mybir.AxisListType

S = 1024
D = 256
NH = 16
NP = NH // 2
NOPE = 128
ROPE = 64
HD = NOPE + ROPE
QL = 192
IH = 8
TOPK = 8
E = 1024
T = S // 128
K = D // 128
QLT = QL - 128
SCALE = float(HD) ** -0.5
SCALE_SIDE = float(128) ** -0.5
EPS = 1e-5
LOW = -3.0e38

CHUNKS = [(i + 4) // 4 for i in range(T)]
CH0 = [sum(CHUNKS[:i]) for i in range(T + 1)]
NCH = CH0[T]


def attention_and_mlp(nc, x, W_cq, q_norm_w, q_norm_b, W_q, W_ckv, kv_norm_w, kv_norm_b, W_kv, W_o,
                      W_ip, W_ig, W_sq, W_sk, W_sv, W_io, W_up, W_gate, W_down,
                      c_ident, c_cos, c_sin, c_tok, c_blk, c_off, c_mean, out):
    top = ExitStack()
    with top:
        stack = [top]

        def sb(name, shape, dt=F32):
            return stack[-1].enter_context(nc.sbuf_tensor(name, shape, dt))

        def sem(name):
            return top.enter_context(nc.semaphore(name))

        SC = [top.enter_context(nc.psum_tensor(f"SC{i}", [128, 1024], F32)) for i in range(2)]
        J = [top.enter_context(nc.psum_tensor(f"J{i}", [128, 512], F32)) for i in range(2)]
        TP = [top.enter_context(nc.psum_tensor(f"TP{i}", [128, 512], F32)) for i in range(2)]

        acc = sb("acc", [128, T, D])
        ident = sb("ident", [128, 128])
        mhalf = sb("mhalf", [128, 16])
        epst = sb("epst", [128, 16])
        held = sem("held")

        def wait(eng, s, v):
            if isinstance(v, int) and v <= 0:
                return
            eng.wait_ge(s, v)

        def hold(eng, s, v):
            wait(eng, s, v)
            eng.sem_inc(held, 1)

        attn = ExitStack()
        stack.append(attn)
        xTh, xTl = sb("xTh", [128, K, S], F32R), sb("xTl", [128, K, S], F32R)
        qch, qcl = sb("qch", [128, S], F32R), sb("qcl", [128, S], F32R)
        qcs = sb("qcs", [128, S], F32R)
        mask = sb("mask", [128, S], BF16)
        cos2, sin2 = sb("cos2", [128, T, ROPE]), sb("sin2", [128, T, ROPE])
        kvw, kvb = sb("kvw", [128, 1]), sb("kvb", [128, 1])
        Wkh, Wkl = sb("Wkh", [128, 2 * NOPE], F32R), sb("Wkl", [128, 2 * NOPE], F32R)
        ioT = sb("ioT", [128, IH])
        iocol = sb("iocol", [128, 2])
        r_kv = sb("r_kv", [128, K, 2 * HD])
        Wckh, Wckl = sb("Wckh", [128, K, 2 * HD], F32R), sb("Wckl", [128, K, 2 * HD], F32R)
        r_qp = sb("r_qp", [128, 2, 2, ROPE])
        Wqph, Wqpl = sb("Wqph", [128, 2, 2, ROPE], F32R), sb("Wqpl", [128, 2, 2, ROPE], F32R)
        r_qn = sb("r_qn", [128, 2, NOPE])
        Wqnh = [sb(f"Wqnh{b}", [128, 2, NOPE], F32R) for b in range(2)]
        Wqnl = [sb(f"Wqnl{b}", [128, 2, NOPE], F32R) for b in range(2)]
        r_o = sb("r_o", [128, D])
        Woh = [sb(f"Woh{b}", [128, D], F32R) for b in range(2)]
        Wol = [sb(f"Wol{b}", [128, D], F32R) for b in range(2)]
        kvraw = sb("kvraw", [128, T, 2 * HD])
        qraw = sb("qraw", [128, T, 2, ROPE])
        ropes = sb("ropes", [128, T, 2, ROPE])
        Rk = sb("Rk", [128, T, 2, 2, ROPE])
        Rq = sb("Rq", [128, T, 2, 2, ROPE])
        bst = sb("bst", [128, T, 2, 6])
        mv = sb("mv", [128, 2 * T, 2])
        veps = sb("veps", [128, 2 * T])
        rstd = sb("rstd", [128, 2 * T])
        kvTh, kvTl = sb("kvTh", [128, S], F32R), sb("kvTl", [128, S], F32R)
        tmp = [sb(f"tmp{c}", [128, 512]) for c in range(2)]
        KNh = [sb(f"KNh{b}", [128, S], F32R) for b in range(2)]
        KNl = [sb(f"KNl{b}", [128, S], F32R) for b in range(2)]
        QNh = [sb(f"QNh{b}", [128, S], F32R) for b in range(2)]
        QNl = [sb(f"QNl{b}", [128, S], F32R) for b in range(2)]
        QS = [sb(f"QS{b}", [128, S], F32R) for b in range(2)]
        KD = [sb(f"KD{b}", [128, S], F32R) for b in range(2)]
        KL = sb("KL", [128, S], F32R)
        Vh, Vl = sb("Vh", [128, T, NOPE], F32R), sb("Vl", [128, T, NOPE], F32R)
        mx = sb("mx", [128, 1])
        nm, sm, rs = sb("nm", [128, 2]), sb("sm", [128, 2]), sb("rs", [128, 2])
        Pb = [sb(f"Pb{i}", [128, S]) for i in range(2)]
        PTh, PTl = sb("PTh", [128, T, 256], F32R), sb("PTl", [128, T, 256], F32R)
        ATh = [sb(f"ATh{i}", [128, 256], F32R) for i in range(2)]
        ATl = [sb(f"ATl{i}", [128, 256], F32R) for i in range(2)]

        wip = Rq[:, :, :, :, :].rearrange("p t h a d -> p (t h a d)").rearrange("p (k n) -> p k n", k=K)
        r_cq = Pb[0][:, 0:400].rearrange("p (k n) -> p k n", k=K)
        r_wkv = Pb[0][:, 512:768]
        Wcqh = KNh[1][:, 0:400].rearrange("p (k n) -> p k n", k=K)
        Wcql = KNl[1][:, 0:400].rearrange("p (k n) -> p k n", k=K)
        qcn = Rk[:, :, :, :, :].rearrange("p t h a d -> p t (h a d)")
        gts = Pb[0][:, 768:768 + 64].rearrange("p (t h) -> p t h", t=T)
        qst = Pb[0][:, 832:832 + 48].rearrange("p (t s) -> p t s", t=T)
        qmv = Pb[0][:, 880:896].rearrange("p (t s) -> p t s", t=T)
        wside = Pb[1][:, 0:512].rearrange("p (k n) -> p k n", k=4)
        qnwb = sb("qnwb", [128, 4])
        gT = qraw[0:8, :, :, :].rearrange("p t h n -> p (t h n)")
        m8 = sb("m8", [8, 8])
        i8 = sb("i8", [8, 8], U32)
        i8f = sb("i8f", [8, 8])
        i8d = sb("i8d", [8, 64])
        ones8 = sb("ones8", [8, 128])
        blk = sb("blk", [8, 64])
        tokid = sb("tokid", [128, T])
        off64 = sb("off64", [64, 64])
        mean8 = sb("mean8", [64, 8])
        idxb = sb("idxb", [128, 64])
        oneh = Pb[1][:, 512:1024].rearrange("p (t n) -> p t n", t=T)
        selT = Pb[0][:, 896:1024].rearrange("p (k n) -> p k n", k=K)
        istT = sb("istT", [128, 64])
        sqT, skT = sb("sqT", [128, 64]), sb("skT", [128, 64])
        svs = sb("svs", [64, 128])
        sp_s = sb("sp_s", [64, 64])
        smx = sb("smx", [64, 4])
        pms = sb("pms", [64, 8])
        soT = sb("soT", [128, 8])

        ld_x, ld_c, ld_w0, ld_side = sem("ld_x"), sem("ld_c"), sem("ld_w0"), sem("ld_side")
        ld_kv, ld_qp, ld_qn, ld_o = sem("ld_kv"), sem("ld_qp"), sem("ld_qn"), sem("ld_o")
        const_ready = sem("const_ready")
        hi_w, w0_ready = sem("hi_w"), sem("w0_ready")
        wkv_hi, wkv_ready = sem("wkv_hi"), sem("wkv_ready")
        wqp_hi, wqp_ready = sem("wqp_hi"), sem("wqp_ready")
        wqn_hi, wqn_ready = sem("wqn_hi"), sem("wqn_ready")
        wo_hi, wo_split = sem("wo_hi"), sem("wo_split")
        ready = {k: sem(f"{k}_ready") for k in
                 ("xt", "qc", "qm", "kv", "qp", "kt", "kp", "qt", "kn", "qn", "v", "pv", "wo", "side")}
        hi = {k: sem(f"{k}_hi") for k in ("xt", "kp", "qt", "kn", "qn", "pv")}
        done = {k: sem(f"{k}_done") for k in
                ("xt", "qc", "qm", "kv", "qp", "kt", "kp", "qt", "kn", "qn", "v", "pv", "wo", "side")}
        qc_stat, qc_aggr, qc_veps, qc_rstd, qc_norm = (sem("qc_stat"), sem("qc_aggr"), sem("qc_veps"),
                                                       sem("qc_rstd"), sem("qc_norm"))
        qc_dup = sem("qc_dup")
        qm_part = sem("qm_part")
        qc_split = sem("qc_split")
        bn_done, aggr_done, veps_done, rstd_done, kvn_done = (sem("bn_done"), sem("aggr_done"),
                                                              sem("veps_done"), sem("rstd_done"),
                                                              sem("kvn_done"))
        rk_mul, rk_ready = sem("rk_mul"), sem("rk_ready")
        rq_mul, rq_ready = sem("rq_mul"), sem("rq_ready")
        kt_lo, v_lo = sem("kt_lo"), sem("v_lo")
        sc_ready = sem("sc_ready")
        mx_ready, nm_ready = sem("mx_ready"), sem("nm_ready")
        exp_done = sem("exp_done")
        rs_ready, p_ready = sem("rs_ready"), sem("p_ready")
        tp_ready = sem("tp_ready")
        pt_hi, pt_lo = sem("pt_hi"), sem("pt_lo")
        io_ready = sem("io_ready")
        side_dve = sem("side_dve")
        side_exp = sem("side_exp")

        PER = {"xt": 4, "qc": T, "qm": 4, "kv": T, "qp": 2, "kt": 2, "kp": 2, "qt": 2, "kn": 2, "qn": 2,
               "v": 2, "pv": 4, "wo": 4, "side": 11}

        def count(kind, unit, c):
            return PER[kind] * unit + c + 1

        PAIR_KINDS = ("kv", "qp", "kvn", "ropek", "ropeq", "wkv", "wqp")

        def unit(kind, off, p):
            return p + off if kind in PAIR_KINDS else 2 * p + off

        def head_steps(b, first, last):
            h, n = b, b + 1
            tail = not (first and b == 0)
            build = not (last and b == 1)
            s = []

            def add(*steps):
                s.extend(steps)

            add(("qk", h, 0), ("norm", h, 0))
            if tail:
                add(("t", h - 1, 7), ("wo", h - 1, 2))
            add(("v", h, 0), ("v", h, 1)) if not tail else None
            add(("qk", h, 1))
            if tail:
                add(("pv", h - 1, 3), ("v", h, 0))
            add(("norm", h, 1), ("t", h, 0))
            add(("qk", h, 2))
            if tail:
                add(("v", h, 1), ("wo", h - 1, 3))
            add(("io", h, 0), ("norm", h, 2), ("t", h, 1))
            if build:
                add(("wqn", n, 0))
            add(("wosp", n, 0)) if not (last and b == 1) else None
            add(("qk", h, 3))
            if build:
                add(("kt", n, 0), ("kt", n, 1))
            add(("norm", h, 3), ("pv", h, 0), ("t", h, 2))
            kv = [] if (last or b == 1) else [("kv", 1, t) for t in range(T)]
            if b == 1 and not last:
                add(("qp", 1, 0), ("qp", 1, 1), ("ropeq", 1, 0), ("wqp", 2, 0))
            add(("qk", h, 4))
            if build:
                add(("kp", n, 0), ("kp", n, 1))
            add(*kv[0:1])
            add(("norm", h, 4), ("wo", h, 0), ("t", h, 3))
            add(("qk", h, 5))
            add(*kv[1:2])
            if build:
                add(("kn", n, 0), ("kn", n, 1))
            add(*kv[2:4])
            add(("norm", h, 5), ("pv", h, 1), ("t", h, 4))
            add(("qk", h, 6))
            add(*kv[4:6])
            if build:
                add(("qn", n, 0))
            add(("norm", h, 6), ("wo", h, 1), ("t", h, 5))
            add(("qk", h, 7))
            if build:
                add(("qn", n, 1))
            add(*kv[6:8])
            if kv:
                add(("kvn", 1, 0), ("ropek", 1, 0))
            if build:
                add(("qt", n, 0), ("qt", n, 1))
            if kv:
                add(("wkv", 2, 0))
            add(("norm", h, 7), ("pv", h, 2), ("t", h, 6))
            return s

        def pair_steps(first=False, last=False):
            return head_steps(0, first, last) + head_steps(1, first, last)

        SIDE = [("side", 0, c) for c in range(11)]
        PROLOGUE = ([("xt", 0, c) for c in range(4)] + [("qc", 0, t) for t in range(T)] +
                    [("wkv", 0, 0)] + SIDE[0:2] + [("kv", 0, 0), ("kv", 0, 1)] + SIDE[2:3] +
                    [("kv", 0, 2)] + SIDE[3:4] + [("kv", 0, 3)] + SIDE[4:5] +
                    [("wqp", 0, 0), ("kv", 0, 4)] + SIDE[5:6] + [("kv", 0, 5)] + SIDE[6:7] + [("kv", 0, 6)] + SIDE[7:8] +
                    [("kv", 0, 7)] + [("qm", 0, c) for c in range(4)] +
                    [("kvn", 0, 0), ("wqn", 0, 0), ("ropek", 0, 0)] +
                    [("qp", 0, c) for c in range(2)] + SIDE[8:9] + [("ropeq", 0, 0), ("wkv", 1, 0), ("wqp", 1, 0), ("wosp", 0, 0)] +
                    [("kt", 0, 0), ("kt", 0, 1), ("qn", 0, 0), ("qn", 0, 1)] + SIDE[9:10] + [("kn", 0, 0), ("kn", 0, 1)] +
                    SIDE[10:] + [("kp", 0, 0), ("kp", 0, 1), ("qt", 0, 0), ("qt", 0, 1)])
        EPILOGUE = [("t", NH - 1, 7), ("wo", NH - 1, 2), ("pv", NH - 1, 3), ("wo", NH - 1, 3)]

        BANKED = tuple(PER)

        def banked(steps):
            return [s for s in steps if s[0] in BANKED]

        FIRST, MID, LAST = pair_steps(first=True), pair_steps(), pair_steps(last=True)
        for part in (PROLOGUE, MID):
            if len(banked(part)) % 2:
                part.append(("skip", 0, 0))

        if len(banked(FIRST)) % 2:
            FIRST.insert(0, ("skip", 0, 0))
        BANKED_ALL = BANKED + ("skip",)

        def numbered(steps, start=0):
            n, res = start, []
            for s in steps:
                if s[0] in BANKED_ALL:
                    res.append((*s, n % 2))
                    n += 1
                else:
                    res.append((*s, None))
            return res

        def half(c):
            return slice(512 * c, 512 * c + 512)

        def tile(t):
            return slice(128 * t, 128 * t + 128)

        block = top.enter_context(ExitStack())
        blk1 = block.enter_context(nc.Block())

        @blk1.sync
        def _(sp):
            sp.dma_start(acc[:, :, :], x.rearrange("(t p) d -> p t d", p=128)).then_inc(ld_x, 16)
            sp.dma_start(ident[:, :], c_ident).then_inc(ld_x, 16)
            cq = W_cq.rearrange("(k p) n -> p k n", p=128)
            sp.dma_start(r_cq[:, :, 0:QL], cq).then_inc(ld_w0, 16)
            sp.dma_start(r_cq[:, :, QL:QL + IH], W_ig.rearrange("(k p) n -> p k n", p=128)).then_inc(ld_w0, 16)
            sp.dma_start(r_wkv, W_kv).then_inc(ld_w0, 16)

            ckv = W_ckv.rearrange("(k p) n -> p k n", p=128)
            wq2 = W_q.rearrange("r (h n) -> r h n", n=HD)

            def load(kind, u):
                if kind == "wkv":
                    wait(sp, wkv_ready, u)
                    sp.dma_start(r_kv[:, :, :], ckv[:, :, bass.ds(u * (2 * HD), 2 * HD)]).then_inc(ld_kv, 16)
                if kind == "wqp":
                    wait(sp, wqp_ready, u)
                    cols = wq2[:, bass.ds(u * 2, 2), NOPE:HD]
                    sp.dma_start(r_qp[:, 0, :, :], cols[0:128]).then_inc(ld_qp, 16)
                    for r in range(2):
                        sp.dma_start(r_qp[64 * r:64 * r + 64, 1, :, :], cols[128:QL]).then_inc(ld_qp, 16)
                if kind == "wqn":
                    wait(sp, wqn_ready, u)
                    cols = W_q[:, bass.ds(u * HD, NOPE)]
                    sp.dma_start(r_qn[:, 0, :], cols[0:128]).then_inc(ld_qn, 16)
                    for r in range(2):
                        sp.dma_start(r_qn[64 * r:64 * r + 64, 1, :], cols[128:QL]).then_inc(ld_qn, 16)
                if kind == "wosp":
                    wait(sp, wo_split, u)
                    sp.dma_start(r_o[:, :], W_o[bass.ds(u * NOPE, NOPE), :]).then_inc(ld_o, 16)

            for kind in ("wkv", "wqp", "wqn", "wosp"):
                load(kind, 0)
            sp.dma_start(qnwb[:, 0:1], q_norm_w[0:128].rearrange("(p a) -> p a", a=1)).then_inc(ld_c, 16)
            sp.dma_start(qnwb[:, 1:2], q_norm_b[0:128].rearrange("(p a) -> p a", a=1)).then_inc(ld_c, 16)
            for r in range(2):
                rows = slice(64 * r, 64 * r + 64)
                sp.dma_start(qnwb[rows, 2:3], q_norm_w[128:QL].rearrange("(p a) -> p a", a=1)).then_inc(ld_c, 16)
                sp.dma_start(qnwb[rows, 3:4], q_norm_b[128:QL].rearrange("(p a) -> p a", a=1)).then_inc(ld_c, 16)
            sp.dma_start(kvw[:, :], kv_norm_w.rearrange("(p a) -> p a", a=1)).then_inc(ld_c, 16)
            sp.dma_start(kvb[:, :], kv_norm_b.rearrange("(p a) -> p a", a=1)).then_inc(ld_c, 16)
            sp.dma_start(cos2[:, :, :], c_cos.rearrange("(t p) d -> p t d", p=128)).then_inc(ld_c, 16)
            sp.dma_start(sin2[:, :, :], c_sin.rearrange("(t p) d -> p t d", p=128)).then_inc(ld_c, 16)
            for dst, src in ((blk[:, :], c_blk), (tokid[:, :], c_tok), (off64[:, :], c_off), (mean8[:, :], c_mean),
                             (wip, W_ip.rearrange("(k p) n -> p k n", p=128)), (wside[:, 0, :], W_sq),
                             (wside[:, 1, :], W_sk), (wside[:, 2, :], W_sv), (wside[:, 3, :], W_io[:, 0:128])):
                sp.dma_start(dst, src).then_inc(ld_side, 16)
            load("wkv", 1)
            load("wqp", 1)

            def run(steps, p):
                for kind, off, c in steps:
                    if kind in ("wqn", "wosp"):
                        load(kind, unit(kind, off, p))
                    if kind in ("wkv", "wqp"):
                        if isinstance(p, int) and p + off >= NP:
                            continue
                        load(kind, unit(kind, off, p))

            run(FIRST, 0)
            with sp.Fori(1, NP - 2) as p:
                run(MID, p)
            run(MID, NP - 2)
            run(LAST, NP - 1)

        LD_C, LD_SIDE, LD_W0 = 16 * 10, 16 * 9, 16 * 3

        @blk1.gpsimd
        def _(gp):
            gp.memset(mhalf[:, :], -0.5)
            gp.memset(epst[:, :], EPS)
            gp.memset(ones8[:, :], 1.0).then_inc(const_ready, 1)
            gp.memset(mask[:, :], 0.0).then_inc(const_ready, 1)
            gp.wait_ge(const_ready, 2)
            gp.affine_select(out=mask[:, S - 128:S], in_=mask[:, S - 128:S], compare_op=ALU.is_ge, fill=-1e30, base=0,
                             pattern=[[-1, 128]], channel_multiplier=1).then_inc(const_ready, 1)
            gp.wait_ge(ld_w0, LD_W0)
            gp.tensor_copy(Wcqh[:, :, :], r_cq)
            gp.tensor_copy(Wkh[:, :], r_wkv).then_inc(hi_w, 1)
            gp.wait_ge(hi_w, 1)
            gp.tensor_tensor(Wcql[:, :, :], r_cq, Wcqh[:, :, :].bitcast(F32), ALU.subtract)
            gp.tensor_tensor(Wkl[:, :], r_wkv, Wkh[:, :].bitcast(F32), ALU.subtract).then_inc(w0_ready, 1)

            def split(loaded, n_loaded, raw, wh, wl, wh_done, wl_done, used, n_used, u):
                hold(gp, loaded, n_loaded)
                hold(gp, used, n_used)
                gp.tensor_copy(wh, raw).then_inc(wh_done, 1)
                gp.wait_ge(wh_done, u + 1)
                gp.tensor_tensor(wl, raw, wh.bitcast(F32), ALU.subtract).then_inc(wl_done, 1)

            def rope(src, raw_sem, raw_n, dst, used, n_used, mul, rdy, u, first, other, other_n):
                hold(gp, raw_sem, raw_n)
                if isinstance(u, int) and u == 0:
                    hold(gp, *first)
                else:
                    hold(gp, used, n_used)
                if not (isinstance(other_n, int) and other_n == 0):
                    gp.wait_ge(other, other_n)
                cosb = cos2[:, :, :].rearrange("p t (a d) -> p t a d", a=1).to_broadcast([128, T, 2, ROPE])
                for e in range(2):
                    s = sin2[:, :, e::2].rearrange("p t (a d) -> p t a d", a=1).to_broadcast([128, T, 2, ROPE // 2])
                    ins = gp.tensor_tensor(ropes[:, :, :, e::2], src[:, :, :, 1 - e::2], s, ALU.mult)
                ins.then_inc(mul, 1)
                gp.wait_ge(mul, 2 * u + 1)
                gp.tensor_tensor(src, src, cosb, ALU.mult).then_inc(mul, 1)
                gp.wait_ge(mul, 2 * u + 2)
                for hh in range(2):
                    a = src[:, :, hh, :].rearrange("p t (a d) -> p t a d", a=1).to_broadcast([128, T, 2, ROPE])
                    b = ropes[:, :, hh, :].rearrange("p t (a d) -> p t a d", a=1).to_broadcast([128, T, 2, ROPE])
                    ins = gp.tensor_tensor(dst[:, :, hh, :, :], a, b, ALU.add)
                ins.then_inc(rdy, 1)

            def inv_std(stats, v, r, s_in, n_in, s_mid, s_out, n):
                hold(gp, s_in, n_in)
                gp.tensor_tensor(v, stats, epst[:, 0:v.shape[1]], ALU.add).then_inc(s_mid, 1)
                gp.wait_ge(s_mid, n)
                gp.tensor_tensor(r, v, mhalf[:, 0:v.shape[1]], ALU.pow).then_inc(s_out, 1)

            def run(steps, p):
                for kind, off, c, bank in steps:
                    u = unit(kind, off, p)
                    if kind == "wkv" or kind == "wqp":
                        if isinstance(u, int) and u >= NP:
                            continue
                    if kind == "wkv":
                        split(ld_kv, 16 * u + 16, r_kv[:, :, :], Wckh[:, :, :], Wckl[:, :, :], wkv_hi, wkv_ready,
                              ready["kv"], T * u, u)
                    if kind == "wqp":
                        split(ld_qp, 48 * u + 48, r_qp[:, :, :, :], Wqph[:, :, :, :], Wqpl[:, :, :, :], wqp_hi, wqp_ready,
                              ready["qp"], 2 * u, u)
                    if kind == "wqn":
                        b = off % 2
                        split(ld_qn, 48 * u + 48, r_qn[:, :, :], Wqnh[b][:, :, :], Wqnl[b][:, :, :], wqn_hi, wqn_ready,
                              ready["qn"], 2 * (u - 1), u)
                    if kind == "wosp":
                        b = off % 2
                        split(ld_o, 16 * u + 16, r_o[:, :], Woh[b][:, :], Wol[b][:, :], wo_hi, wo_split,
                              ready["wo"], 4 * (u - 1), u)
                    if kind == "qm" and c == 0:
                        inv_std(qmv[:, :, 1], veps[:, 0:T], rstd[:, 0:T], qc_aggr, 1, qc_veps, qc_rstd, 1)
                    if kind == "kvn":
                        if isinstance(u, int) and u == 0:
                            hold(gp, qc_norm, 1)
                        inv_std(mv[:, :, 1], veps[:, :], rstd[:, :], aggr_done, u + 1, veps_done, rstd_done, u + 1)
                    if kind == "ropek":
                        src = kvraw[:, :, :].rearrange("p t (h n) -> p t h n", h=2)[:, :, :, 0:ROPE]
                        rope(src, done["kv"], T * (u + 1), Rk, ready["kp"], 4 * u, rk_mul, rk_ready, u, (done["qm"], 4), rq_ready, u)
                    if kind == "ropeq":
                        rope(qraw[:, :, :, :], done["qp"], 2 * (u + 1), Rq, ready["qt"], 4 * u, rq_mul, rq_ready, u, (done["side"], 5), rk_ready, u + 1)
                    if kind == "kt":
                        gp.wait_ge(done["kt"], count("kt", u, c))
                        gp.tensor_tensor(kvTl[:, half(c)], tmp[c][:, :], kvTh[:, half(c)].bitcast(F32),
                                         ALU.subtract).then_inc(kt_lo, 1)
                    if kind == "v":
                        gp.wait_ge(done["v"], count("v", u, c))
                        gp.tensor_tensor(Vl[:, 4 * c:4 * c + 4, :], tmp[c][:, :].rearrange("p (t n) -> p t n", t=4),
                                         Vh[:, 4 * c:4 * c + 4, :].bitcast(F32), ALU.subtract).then_inc(v_lo, 1)

            gp.wait_ge(ld_c, LD_C)
            run(numbered(PROLOGUE), 0)
            run(numbered(FIRST), 0)
            with gp.Fori(1, NP - 2) as p:
                run(numbered(MID), p)
            run(numbered(MID), NP - 2)
            run(numbered(LAST), NP - 1)

        @blk1.tensor
        def _(pe):
            mm = pe.matmul

            def three(o, wh, wl, xh, xl, start, stop):
                mm(o, lhsT=wh, rhs=xh, start=start, stop=False)
                mm(o, lhsT=wh, rhs=xl, start=False, stop=False)
                return mm(o, lhsT=wl, rhs=xh, start=False, stop=stop)

            def qk(h, b, i):
                if i == 0:
                    pe.wait_ge(done["qn"], count("qn", h, 1))
                    pe.wait_ge(done["kn"], count("kn", h, 1))
                    pe.wait_ge(done["kp"], count("kp", h, 1))
                    pe.wait_ge(done["qt"], count("qt", h, 1))
                wait(pe, exp_done, T * h + i - 1)
                o, q, r = SC[i % 2], tile(i), slice(64 * b, 64 * b + 64)
                for c in range(CHUNKS[i]):
                    k = slice(512 * c, min(512 * c + 512, 128 * (i + 1)))
                    mm(o[:, k], lhsT=QNh[b][:, q], rhs=KNh[b][:, k], start=True, stop=False)
                    mm(o[:, k], lhsT=QNh[b][:, q], rhs=KNl[b][:, k], start=False, stop=False)
                    mm(o[:, k], lhsT=QNl[b][:, q], rhs=KNh[b][:, k], start=False, stop=False)
                    mm(o[:, k], lhsT=QS[b][:, q], rhs=KD[b][:, k], start=False, stop=False)
                    last = mm(o[:, k], lhsT=QS[b][r, q], rhs=KL[r, k], start=False, stop=True)
                last.then_inc(sc_ready, 1)

            def tr(h, i):
                pe.wait_ge(p_ready, T * h + i + 1)
                for c in range(CHUNKS[i]):
                    n = CH0[i] + c
                    wait(pe, pt_lo, NCH * h + n - 1)
                    for j in range(4 * c, min(4 * c + 4, i + 1)):
                        last = pe.transpose(TP[n % 2][:, tile(j - 4 * c)], Pb[i % 2][:, tile(j)], ident[:, :])
                    last.then_inc(tp_ready, 1)

            def pv(h, b, g, o):
                if g == 0:
                    pe.wait_ge(v_lo, 2 * h + 2)
                pe.wait_ge(pt_lo, NCH * h + CH0[2 * g + 2])
                for j in range(2 * g + 2):
                    q = slice(0, 256) if j <= 2 * g else slice(128, 256)
                    last = three(o[:, q], Vh[:, j, :], Vl[:, j, :], PTh[:, j, q], PTl[:, j, q], j == 0, j == 2 * g + 1)
                return last

            def side(c, o):
                w = done["side"]
                if c == 0 or c == 1:
                    if c == 0:
                        pe.wait_ge(done["qc"], T)
                    for t in range(4):
                        last = pe.transpose(o[0:8, tile(t)], gts[:, 4 * c + t, :], ident[:, :])
                    return last
                if c == 2:
                    pe.wait_ge(side_dve, 4)
                    return mm(o[:, 0:64], lhsT=ones8[:, :], rhs=i8d[:, :], start=True, stop=True)
                if c == 3:
                    pe.wait_ge(side_dve, 5)
                    for k in range(K):
                        for t in range(T):
                            last = mm(o[:, 64 * k:64 * k + 64], lhsT=acc[:, t, tile(k)], rhs=oneh[:, t, :],
                                      start=t == 0, stop=t == T - 1)
                    return last
                pe.wait_ge(w, c)
                if c == 4:
                    for h in range(IH):
                        for k in range(K):
                            last = mm(o[:, 8 * h:8 * h + 8], lhsT=wip[:, k, tile(h)], rhs=selT[:, k, 8 * h:8 * h + 8],
                                      start=k == 0, stop=k == K - 1)
                    return last
                if c == 5:
                    mm(o[:, 0:64], lhsT=wside[:, 0, :], rhs=istT[:, :], start=True, stop=True)
                    return mm(o[:, 64:128], lhsT=wside[:, 1, :], rhs=istT[:, :], start=True, stop=True)
                if c == 6:
                    return mm(o[0:64, 0:128], lhsT=istT[:, :], rhs=wside[:, 2, :], start=True, stop=True)
                if c == 7:
                    return mm(o[0:64, 0:64], lhsT=sqT[:, :], rhs=skT[:, :], start=True, stop=True)
                if c == 8:
                    pe.wait_ge(side_dve, 9)
                    return mm(o[0:64, 0:8], lhsT=sp_s[:, :], rhs=mean8[:, :], start=True, stop=True)
                if c == 9:
                    return mm(o[:, 0:8], lhsT=svs[:, :], rhs=pms[:, :], start=True, stop=True)
                return mm(o[:, 0:8], lhsT=wside[:, 3, :], rhs=soT[:, :], start=True, stop=True)

            def use(kind, off, c, bank, p):
                u, o = unit(kind, off, p), J[bank]
                b = off % 2
                if kind == "xt":
                    if c == 0:
                        pe.wait_ge(ld_x, 32)
                    for t in range(4):
                        last = pe.transpose(o[:, tile(t)], acc[:, 4 * (c % 2) + t, tile(c // 2)], ident[:, :])
                if kind == "qc":
                    if c == 0:
                        pe.wait_ge(w0_ready, 1)
                        pe.wait_ge(done["xt"], 4)
                    for k in range(K):
                        last = three(o[:, 0:200], xTh[:, k, tile(c)], xTl[:, k, tile(c)], Wcqh[:, k, :], Wcql[:, k, :],
                                     k == 0, k == K - 1)
                if kind == "qm":
                    if c == 0:
                        pe.wait_ge(qc_norm, 1)
                    for t in range(4):
                        src = qcn[:, 4 * (c % 2) + t, 128 * (c // 2):128 * (c // 2) + 128]
                        last = pe.transpose(o[:, tile(t)], src, ident[:, :])
                if kind == "kv":
                    if c == 0:
                        pe.wait_ge(wkv_ready, u + 1)
                    for k in range(K):
                        last = three(o[:, 0:2 * HD], xTh[:, k, tile(c)], xTl[:, k, tile(c)], Wckh[:, k, :], Wckl[:, k, :],
                                     k == 0, k == K - 1)
                if kind == "qp":
                    if c == 0:
                        pe.wait_ge(wqp_ready, u + 1)
                        if isinstance(u, int) and u == 0:
                            pe.wait_ge(qc_split, 4)
                    for t in range(4):
                        tok = tile(4 * c + t)
                        w = [Wqph[:, r, :, :].rearrange("p h n -> p (h n)") for r in range(2)]
                        wl = [Wqpl[:, r, :, :].rearrange("p h n -> p (h n)") for r in range(2)]
                        ot = o[:, tile(t)]
                        three(ot, qch[:, tok], qcl[:, tok], w[0], wl[0], True, False)
                        mm(ot, lhsT=qcs[:, tok], rhs=w[1], start=False, stop=False)
                        last = mm(ot, lhsT=qcs[:, tok], rhs=wl[1], start=False, stop=True)
                if kind == "kt":
                    if c == 0:
                        pe.wait_ge(kvn_done, (u - b if isinstance(u, int) else p * 2 + (off - b)) // 2 + 1
                                   if isinstance(u, int) else p + (off - b) // 2 + 1)
                    for t in range(4):
                        last = pe.transpose(o[:, tile(t)], kvraw[:, 4 * c + t, b * HD + ROPE:b * HD + HD], ident[:, :])
                if kind == "kp" or kind == "qt":
                    src, rdy = (Rk, rk_ready) if kind == "kp" else (Rq, rq_ready)
                    if c == 0:
                        pe.wait_ge(rdy, p + off // 2 + 1)
                    for t in range(4):
                        a = src[:, 4 * c + t, b, :, :].rearrange("p a d -> p (a d)")
                        last = pe.transpose(o[:, tile(t)], a, ident[:, :])
                if kind == "kn":
                    pe.wait_ge(kt_lo, count("kt", u, c))
                    last = three(o[:, :], Wkh[:, 0:NOPE], Wkl[:, 0:NOPE], kvTh[:, half(c)], kvTl[:, half(c)], True, True)
                if kind == "qn":
                    if c == 0:
                        pe.wait_ge(wqn_ready, u + 1)
                    three(o[:, :], Wqnh[b][:, 0, :], Wqnl[b][:, 0, :], qch[:, half(c)], qcl[:, half(c)], True, False)
                    mm(o[:, :], lhsT=Wqnh[b][:, 1, :], rhs=qcs[:, half(c)], start=False, stop=False)
                    last = mm(o[:, :], lhsT=Wqnl[b][:, 1, :], rhs=qcs[:, half(c)], start=False, stop=True)
                if kind == "v":
                    pe.wait_ge(kt_lo, count("kt", u, 1))
                    for t in range(4):
                        tok = tile(4 * c + t)
                        last = three(o[:, tile(t)], kvTh[:, tok], kvTl[:, tok], Wkh[:, NOPE:], Wkl[:, NOPE:], True, True)
                if kind == "pv":
                    last = pv(u, b, c, o)
                if kind == "wo":
                    pe.wait_ge(done["pv"], count("pv", u, c))
                    if c == 0:
                        pe.wait_ge(wo_split, u + 1)
                    for t in range(2):
                        last = three(o[:, 256 * t:256 * t + 256], ATh[c % 2][:, tile(t)], ATl[c % 2][:, tile(t)],
                                     Woh[b][:, :], Wol[b][:, :], True, True)
                if kind == "side":
                    if c == 0:
                        pe.wait_ge(ld_side, LD_SIDE)
                    last = side(c, o)
                last.then_inc(ready[kind], 1)

            def run(steps, p, before):
                prev = list(before)
                for kind, off, c, bank in steps:
                    if kind == "qk":
                        qk(unit(kind, off, p), off % 2, c)
                    elif kind == "t":
                        tr(unit(kind, off, p), c)
                    elif kind in BANKED_ALL:
                        free = prev[-2]
                        if free is not None and kind != "skip":
                            pe.wait_ge(done[free[0]], count(*free))
                        if kind == "skip":
                            prev.append(prev[-2])
                        else:
                            use(kind, off, c, bank, p)
                            prev.append((kind, unit(kind, off, p), c))
                return prev[-2:]

            def at(uses, p):
                return [(k, unit(k, off, p), c) for k, off, c in uses]

            def last_two(steps):
                prev = [None, None]
                for s in steps:
                    if s[0] in BANKED:
                        prev.append(s)
                    elif s[0] == "skip":
                        prev.append(prev[-2])
                return prev[-2:]

            run(numbered(PROLOGUE), 0, [None, None])
            run(numbered(FIRST), 0, at(last_two(PROLOGUE), 0))
            assert last_two(FIRST) == last_two(MID)
            with pe.Fori(1, NP - 1) as p:
                run(numbered(MID), p, at(last_two(MID), p - 1))
            run(numbered(LAST), NP - 1, at(last_two(MID), NP - 2))
            run([(*s[:1], s[1], s[2], n) for s, n in zip(EPILOGUE, (None, 0, 1, 0))] if len(banked(LAST)) % 2 == 0 else
                [(*s[:1], s[1], s[2], n) for s, n in zip(EPILOGUE, (None, 1, 0, 1))], 0,
                at(last_two(LAST), NP - 1))

        EPI_BANKS = (None, 0, 1, 0) if len(banked(LAST)) % 2 == 0 else (None, 1, 0, 1)
        EPI = [(*s, n) for s, n in zip(EPILOGUE, EPI_BANKS)]

        @blk1.scalar
        def _(act):
            def copy(o, i):
                return act.activation(o, i, ACT.Copy)

            def run(steps, p):
                for kind, off, c, bank in steps:
                    u, b = unit(kind, off, p), off % 2
                    o = J[bank] if bank is not None else None
                    if kind == "qk":
                        i = c
                        act.wait_ge(nm_ready, T * u + i + 1)
                        wait(act, tp_ready, NCH * u + (CH0[i - 1] if i >= 2 else (CH0[i + 7] - NCH)))
                        if isinstance(u, int) and u == 0 and i == 0:
                            act.wait_ge(done["side"], 11)
                        w = slice(0, 128 * (i + 1))
                        act.activation(Pb[i % 2][:, w], SC[i % 2][:, w], ACT.Exp, bias=nm[:, i % 2:i % 2 + 1],
                                       scale=SCALE, accum_out=sm[:, i % 2:i % 2 + 1]).then_inc(exp_done, 1)
                    if kind == "t":
                        for k in range(CHUNKS[c]):
                            n = CH0[c] + k
                            nb = min(4, c + 1 - 4 * k)
                            act.wait_ge(tp_ready, NCH * u + n + 1)
                            dst = PTh[:, 4 * k:4 * k + nb, tile(c % 2)]
                            copy(dst, TP[n % 2][:, 0:128 * nb].rearrange("p (j q) -> p j q", j=nb)).then_inc(pt_hi, 1)
                    if kind in ready and kind != "side":
                        act.wait_ge(ready[kind], count(kind, u, c))
                    if kind == "xt":
                        copy(xTh[:, c // 2, half(c % 2)], o[:, :]).then_inc(hi["xt"], 1)
                    if kind == "qc":
                        copy(qcn[:, c, 0:QL], o[:, 0:QL])
                        copy(gts[:, c, :], o[:, QL:QL + IH]).then_inc(done["qc"], 1)
                    if kind == "qm":
                        if c == 0:
                            act.wait_ge(ld_c, LD_C)
                        if c >= 2:
                            act.wait_ge(qc_split, c - 1)
                        w, bb = (0, 1) if c < 2 else (2, 3)
                        act.activation(tmp[c % 2][:, :], o[:, :], ACT.Identity, bias=qnwb[:, bb:bb + 1],
                                       scale=qnwb[:, w:w + 1]).then_inc(done["qm"], 1)
                    if kind == "kv":
                        if c == 0:
                            wait(act, rk_ready, u)
                        copy(kvraw[:, c, :], o[:, 0:2 * HD]).then_inc(done["kv"], 1)
                    if kind == "qp":
                        if c == 0 and isinstance(u, int) and u == 0:
                            act.wait_ge(side_dve, 2)
                        elif c == 0:
                            act.wait_ge(rq_ready, u)
                        copy(qraw[:, 4 * c:4 * c + 4, :, :].rearrange("p t h n -> p (t h n)"), o[:, :]).then_inc(done["qp"], 1)
                    if kind == "kt":
                        if isinstance(u, int) and u == 0:
                            act.wait_ge(qc_split, 4)
                        else:
                            act.wait_ge(v_lo, 2 * u + c - 1)
                        act.activation(kvTh[:, half(c)], o[:, :], ACT.Identity, bias=kvb[:, 0:1], scale=kvw[:, 0:1])
                        act.activation(tmp[c][:, :], o[:, :], ACT.Identity, bias=kvb[:, 0:1],
                                       scale=kvw[:, 0:1]).then_inc(done["kt"], 1)
                    if kind == "kp":
                        copy(KD[b][:, half(c)], o[:, :]).then_inc(hi["kp"], 1)
                    if kind == "qt":
                        copy(QS[b][:, half(c)], o[:, :]).then_inc(hi["qt"], 1)
                    if kind == "kn":
                        copy(KNh[b][:, half(c)], o[:, :]).then_inc(hi["kn"], 1)
                    if kind == "qn":
                        copy(QNh[b][:, half(c)], o[:, :]).then_inc(hi["qn"], 1)
                    if kind == "v":
                        act.wait_ge(kt_lo, count("kt", u, c))
                        copy(Vh[:, 4 * c:4 * c + 4, :].rearrange("p t n -> p (t n)"), o[:, :])
                        copy(tmp[c][:, :], o[:, :]).then_inc(done["v"], 1)
                    if kind == "pv":
                        if c == 0:
                            act.wait_ge(io_ready, u + 1)
                        wait(act, ready["wo"], 4 * u + c - 1)
                        act.activation(ATh[c % 2][:, :], o[:, 0:256], ACT.Identity,
                                       bias=iocol[:, b:b + 1]).then_inc(hi["pv"], 1)
                    if kind == "side" and c == 7:
                        act.wait_ge(side_dve, 7)
                        act.activation(sp_s[:, :], o[0:64, 0:64], ACT.Exp, bias=smx[:, 1:2], scale=SCALE_SIDE,
                                       accum_out=smx[:, 2:3]).then_inc(side_exp, 1)

            run(numbered(PROLOGUE), 0)
            run(numbered(FIRST), 0)
            with act.Fori(1, NP - 1) as p:
                run(numbered(MID), p)
            run(numbered(LAST), NP - 1)
            run(EPI, 0)

        @blk1.vector
        def _(dve):
            def lo(kind, u, c, o, i, h):
                dve.wait_ge(hi[kind], count(kind, u, c))
                dve.tensor_tensor(o, i, h.bitcast(F32), ALU.subtract).then_inc(done[kind], 1)

            def side(c, o):
                n = count("side", 0, c)
                dve.wait_ge(ready["side"], n)
                cp = dve.tensor_copy
                d = done["side"]
                if c in (0, 1):
                    cp(gT[:, half(c)], o[0:8, :]).then_inc(d, 1)
                if c == 1:
                    dve.wait_ge(d, 2)
                    dve.max(m8[:, :], gT).then_inc(side_dve, 1)
                    dve.wait_ge(side_dve, 1)
                    dve.max_index(i8[:, :], m8[:, :], gT).then_inc(side_dve, 1)
                    dve.wait_ge(side_dve, 2)
                    cp(i8f[:, :], i8[:, :]).then_inc(side_dve, 1)
                    dve.wait_ge(side_dve, 3)
                    a = i8f[:, :].rearrange("p (a k) -> p a k", a=1).to_broadcast([8, 8, 8])
                    dve.wait_ge(ld_side, LD_SIDE)
                    dve.tensor_tensor(i8d[:, :].rearrange("p (h k) -> p h k", h=8), a,
                                      blk[:, :].rearrange("p (h k) -> p h k", h=8), ALU.mult).then_inc(side_dve, 1)
                if c == 2:
                    cp(idxb[:, :], o[:, 0:64]).then_inc(d, 1)
                    dve.wait_ge(d, 3)
                    a = idxb[:, :].rearrange("p (a n) -> p a n", a=1).to_broadcast([128, T, 64])
                    bb = tokid[:, :].rearrange("p (t a) -> p t a", a=1).to_broadcast([128, T, 64])
                    dve.tensor_tensor(oneh[:, :, :], a, bb, ALU.is_equal).then_inc(side_dve, 1)
                if c == 3:
                    cp(selT[:, :, :].rearrange("p k n -> p (k n)"), o[:, 0:128]).then_inc(d, 1)
                if c == 4:
                    cp(istT[:, :], o[:, 0:64]).then_inc(d, 1)
                if c == 5:
                    cp(sqT[:, :], o[:, 0:64])
                    cp(skT[:, :], o[:, 64:128]).then_inc(d, 1)
                if c == 6:
                    cp(svs[:, :], o[0:64, 0:128]).then_inc(d, 1)
                if c == 7:
                    dve.tensor_tensor_reduce(out=o[0:64, 0:64], in0=o[0:64, 0:64], in1=off64[:, :], scale=1.0, scalar=LOW,
                                             op0=ALU.add, op1=ALU.max, accum_out=smx[:, 0:1]).then_inc(side_dve, 1)
                    dve.wait_ge(side_dve, 6)
                    dve.tensor_scalar(smx[:, 1:2], smx[:, 0:1], -SCALE_SIDE, None, ALU.mult).then_inc(side_dve, 1)
                    dve.wait_ge(side_exp, 1)
                    dve.reciprocal(smx[:, 3:4], smx[:, 2:3]).then_inc(side_dve, 1)
                    dve.wait_ge(side_dve, 8)
                    dve.tensor_scalar(sp_s[:, :], sp_s[:, :], smx[:, 3:4], None, ALU.mult).then_inc(side_dve, 1)
                    dve.wait_ge(side_dve, 9)
                    dve.sem_inc(d, 1)
                if c == 8:
                    cp(pms[:, :], o[0:64, 0:8]).then_inc(d, 1)
                if c == 9:
                    cp(soT[:, :], o[:, 0:8]).then_inc(d, 1)
                if c == 10:
                    cp(ioT[:, :], o[:, 0:8]).then_inc(d, 1)

            def run(steps, p):
                for kind, off, c, bank in steps:
                    u, b = unit(kind, off, p), off % 2
                    o = J[bank] if bank is not None else None
                    if kind == "qk":
                        i = c
                        w = slice(0, 128 * (i + 1))
                        hold(dve, sc_ready, T * u + i + 1)
                        dve.tensor_tensor_reduce(out=SC[i % 2][:, w], in0=SC[i % 2][:, w], in1=mask[:, 128 * (7 - i):S],
                                                 scale=1.0, scalar=LOW, op0=ALU.add, op1=ALU.max,
                                                 accum_out=mx[:, 0:1]).then_inc(mx_ready, 1)
                        dve.wait_ge(mx_ready, T * u + i + 1)
                        dve.tensor_scalar(nm[:, i % 2:i % 2 + 1], mx[:, 0:1], -SCALE, None, ALU.mult).then_inc(nm_ready, 1)
                    if kind == "norm":
                        i = c
                        w = slice(0, 128 * (i + 1))
                        dve.wait_ge(exp_done, T * u + i + 1)
                        dve.reciprocal(rs[:, i % 2:i % 2 + 1], sm[:, i % 2:i % 2 + 1]).then_inc(rs_ready, 1)
                        dve.wait_ge(rs_ready, T * u + i + 1)
                        dve.tensor_scalar(Pb[i % 2][:, w], Pb[i % 2][:, w], rs[:, i % 2:i % 2 + 1], None,
                                          ALU.mult).then_inc(p_ready, 1)
                    if kind == "t":
                        for k in range(CHUNKS[c]):
                            n = CH0[c] + k
                            nb = min(4, c + 1 - 4 * k)
                            dve.wait_ge(pt_hi, NCH * u + n + 1)
                            dst = (slice(None), slice(4 * k, 4 * k + nb), tile(c % 2))
                            dve.tensor_tensor(PTl[dst], TP[n % 2][:, 0:128 * nb].rearrange("p (j q) -> p j q", j=nb),
                                              PTh[dst].bitcast(F32), ALU.subtract).then_inc(pt_lo, 1)
                    if kind == "xt":
                        d = (slice(None), c // 2, half(c % 2))
                        lo("xt", 0, c, xTl[d], o[:, :], xTh[d])
                    if kind == "qc":
                        dve.wait_ge(done["qc"], c + 1)
                        dve.bn_stats(qst[:, c, :], qcn[:, c, 0:QL]).then_inc(qc_stat, 1)
                        if c == T - 1:
                            dve.wait_ge(qc_stat, T)
                            for t in range(T):
                                ins = dve.bn_aggr(qmv[:, t, :], qst[:, t, :])
                            ins.then_inc(qc_aggr, 1)
                    if kind == "qm":
                        if c == 0:
                            dve.wait_ge(qc_rstd, 1)
                            dve.wait_ge(qc_aggr, 1)
                            for t in range(T):
                                a = (qcn[:, t, 128:QL], qmv[:, t, 0:1], rstd[:, t:t + 1], ALU.subtract, ALU.mult)
                                ins = dve.tensor_scalar(qcn[:, t, QL:256], *a)
                            ins.then_inc(qc_dup, 1)
                            dve.wait_ge(qc_dup, 1)
                            for t in range(T):
                                a = (qcn[:, t, 0:QL], qmv[:, t, 0:1], rstd[:, t:t + 1], ALU.subtract, ALU.mult)
                                ins = dve.tensor_scalar(qcn[:, t, 0:QL], *a)
                            ins.then_inc(qc_norm, 1)
                        dve.wait_ge(done["qm"], c + 1)
                        q = half(c % 2)
                        dst = (qch if c < 2 else qcs)[:, q]
                        dve.tensor_copy(dst, tmp[c % 2][:, :]).then_inc(qm_part, 1)
                        dve.wait_ge(qm_part, c + 1)
                        if c < 2:
                            dve.tensor_tensor(qcl[:, q], tmp[c][:, :], qch[:, q].bitcast(F32),
                                              ALU.subtract).then_inc(qc_split, 1)
                        else:
                            dve.tensor_tensor(qcs[64:128, q], tmp[c % 2][64:128, :], qcs[64:128, q].bitcast(F32),
                                              ALU.subtract).then_inc(qc_split, 1)
                    if kind == "kv":
                        dve.wait_ge(done["kv"], count("kv", u, c))
                        for hh in range(2):
                            ins = dve.bn_stats(bst[:, c, hh, :], kvraw[:, c, hh * HD + ROPE:hh * HD + HD])
                        ins.then_inc(bn_done, 1)
                    if kind == "kvn":
                        hold(dve, bn_done, T * (u + 1))
                        for t in range(T):
                            for hh in range(2):
                                ins = dve.bn_aggr(mv[:, 2 * t + hh, :], bst[:, t, hh, :])
                        ins.then_inc(aggr_done, 1)
                        dve.wait_ge(rstd_done, u + 1)
                        for t in range(T):
                            for hh in range(2):
                                v = kvraw[:, t, hh * HD + ROPE:hh * HD + HD]
                                n = 2 * t + hh
                                ins = dve.tensor_scalar(v, v, mv[:, n, 0:1], rstd[:, n:n + 1], ALU.subtract, ALU.mult)
                        ins.then_inc(kvn_done, 1)
                    if kind == "kn":
                        lo("kn", u, c, KNl[b][:, half(c)], o[:, :], KNh[b][:, half(c)])
                    if kind == "qn":
                        lo("qn", u, c, QNl[b][:, half(c)], o[:, :], QNh[b][:, half(c)])
                    if kind == "kp":
                        r = slice(64 * b, 64 * b + 64)
                        lo("kp", u, c, KL[r, half(c)], o[r, :], KD[b][r, half(c)])
                    if kind == "qt":
                        r = slice(64 * (1 - b), 64 * (1 - b) + 64)
                        lo("qt", u, c, QS[b][r, half(c)], o[r, :], QS[b][r, half(c)])
                    if kind == "io":
                        if isinstance(p, int):
                            if p == 0:
                                dve.wait_ge(done["side"], 11)
                            dve.tensor_copy(iocol[:, b:b + 1], ioT[:, p:p + 1]).then_inc(io_ready, 1)
                        else:
                            dve.tensor_copy(iocol[:, b:b + 1], ioT[:, bass.ds(p, 1)]).then_inc(io_ready, 1)
                    if kind == "pv":
                        if c == 0:
                            hold(dve, io_ready, u + 1)
                        dve.wait_ge(hi["pv"], count("pv", u, c))
                        dve.scalar_tensor_tensor(ATl[c % 2][:, :], o[:, 0:256], iocol[:, b:b + 1],
                                                 ATh[c % 2][:, :].bitcast(F32), ALU.add,
                                                 ALU.subtract).then_inc(done["pv"], 1)
                    if kind == "wo":
                        dve.wait_ge(ready["wo"], count("wo", u, c))
                        a = acc[:, 2 * c:2 * c + 2, :].rearrange("p t d -> p (t d)")
                        dve.tensor_tensor(a, o[:, :], a, ALU.add).then_inc(done["wo"], 1)
                    if kind == "side":
                        side(c, o)

            run(numbered(PROLOGUE), 0)
            run(numbered(FIRST), 0)
            with dve.Fori(1, NP - 1) as p:
                run(numbered(MID), p)
            run(numbered(LAST), NP - 1)
            run(EPI, 0)

        block.close()
        stack.pop()
        attn.close()

        mlp(nc, top, SC, J, TP, acc, ident, mhalf, epst, W_up, W_gate, W_down, out)


def mlp(nc, top, SC, J, TP, acc, ident, mhalf, epst, W_up, W_gate, W_down, out):
    def sb(name, shape, dt=F32):
        return top.enter_context(nc.sbuf_tensor(name, shape, dt))

    def sem(name):
        return top.enter_context(nc.semaphore(name))

    ET = E // 128
    raw = [sb(f"raw_{n}", [128, 2048]) for n in range(3)]
    low = sb("low", [128, 2048])
    tern = [sb(f"tern_{n}", [128, 2048]) for n in range(3)]
    ternT = [sb("upT", [128, K, E], F32R), sb("gateT", [128, K, E], F32R), sb("downT", [128, ET, D], F32R)]
    asum = sb("asum", [128, 4])
    onesf = sb("onesf", [128, 128])
    scl = sb("scl", [128, 4])
    thr = sb("thr", [128, 4])
    nthr = sb("nthr", [128, 4])
    hTh, hTl = sb("hTh", [128, K, S], F32R), sb("hTl", [128, K, S], F32R)
    sg = [sb(f"sg{i}", [128, 512]) for i in range(2)]
    tt = [sb(f"tt{i}", [128, 512]) for i in range(2)]
    hid = [sb(f"hid{i}", [128, 512]) for i in range(2)]
    Hh, Hl = sb("Hh", [128, ET, 512], F32R), sb("Hl", [128, ET, 512], F32R)
    st, mvl = sb("st", [128, T, 6]), sb("mvl", [128, T, 2])
    ve, rsd = sb("ve", [128, T]), sb("rsd", [128, T])
    st2, mv2 = sb("st2", [128, T, 6]), sb("mv2", [128, T, 2])
    ve2, rsd2 = sb("ve2", [128, T]), sb("rsd2", [128, T])
    yo = sb("yo", [128, T, D])

    ld = [sem(f"ld_mlp{n}") for n in range(3)]
    ones_ready, abs_done, tot_ready, scl_ready, thr_ready = (sem("ones_ready"), sem("abs_done"), sem("tot_ready"),
                                                             sem("scl_ready"), sem("thr_ready"))
    low_done, tern_ready = sem("low_done"), sem("tern_ready")
    st_done, ag_done, ve_done, rsd_ready, ln_done = (sem("st_done"), sem("ag_done"), sem("ve_done"),
                                                     sem("rsd_ready"), sem("ln_done"))
    wt_ready, wt_done = sem("wt_ready"), sem("wt_done")
    ht_ready, ht_hi, ht_done = sem("ht_ready"), sem("ht_hi"), sem("ht_done")
    ug_ready, sg_done, tt_done, hid_done, hh_done, hl_done = (sem("ug_ready"), sem("sg_done"), sem("tt_done"),
                                                              sem("hid_done"), sem("hh_done"), sem("hl_done"))
    dn_ready, y_done, y_st, y_ag, y_ve, y_rsd, y_ln, stored = (sem("dn_ready"), sem("y_done"), sem("y_st"), sem("y_ag"),
                                                               sem("y_ve"), sem("y_rsd"), sem("y_ln"), sem("stored"))

    def tile(t):
        return slice(128 * t, 128 * t + 128)

    N_W = 3 * 2048 // 512
    W_BANKS = [J[0], J[1], TP[0], TP[1]]
    UG = [(SC[0][:, 0:512], SC[0][:, 512:1024]), (SC[1][:, 0:512], SC[1][:, 512:1024])]
    DN = [J[0], J[1]]

    with nc.Block() as blk2:
        @blk2.sync
        def _(sp):
            for n, w in enumerate((W_up, W_gate, W_down)):
                v = w.rearrange("(t p) d -> p t d", p=128)
                sp.dma_start(raw[n][:, :].rearrange("p (t d) -> p t d", t=v.shape[1]), v).then_inc(ld[n], 16)
            for c in range(2):
                sp.wait_ge(y_ln, c + 1)
                sp.dma_start(out[512 * c:512 * c + 512, :].rearrange("(t p) d -> p t d", p=128),
                             yo[:, 4 * c:4 * c + 4, :]).then_inc(stored, 16)
            sp.wait_ge(stored, 32)

        @blk2.gpsimd
        def _(gp):
            gp.memset(asum[:, 3:4], 0.0)
            gp.memset(onesf[:, :], 1.0).then_inc(ones_ready, 1)
            gp.wait_ge(ag_done, 1)
            gp.tensor_tensor(ve[:, :], mvl[:, :, 1], epst[:, 0:T], ALU.add).then_inc(ve_done, 1)
            gp.wait_ge(ve_done, 1)
            gp.tensor_tensor(rsd[:, :], ve[:, :], mhalf[:, 0:T], ALU.pow).then_inc(rsd_ready, 1)
            for c in range(2):
                for e in range(ET):
                    n = c * ET + e
                    gp.wait_ge(hh_done, n + 1)
                    gp.tensor_tensor(Hl[:, e, :], hid[n % 2][:, :], Hh[:, e, :].bitcast(F32),
                                     ALU.subtract).then_inc(hl_done, 1)
                if c == 1:
                    pass
                gp.wait_ge(y_ag, c + 1)
                q = slice(4 * c, 4 * c + 4)
                gp.tensor_tensor(ve2[:, q], mv2[:, q, 1], epst[:, 0:4], ALU.add).then_inc(y_ve, 1)
                gp.wait_ge(y_ve, c + 1)
                gp.tensor_tensor(rsd2[:, q], ve2[:, q], mhalf[:, 0:4], ALU.pow).then_inc(y_rsd, 1)

        @blk2.tensor
        def _(pe):
            mm = pe.matmul
            pe.wait_ge(ones_ready, 1)
            pe.wait_ge(abs_done, 3)
            mm(SC[0][:, 0:4], lhsT=onesf[:, :], rhs=asum[:, :], start=True, stop=True).then_inc(tot_ready, 1)
            pe.wait_ge(ln_done, 1)
            for c in range(4):
                if c >= 2:
                    pe.wait_ge(ht_done, c - 1)
                for t in range(4):
                    last = pe.transpose(UG[1][c % 2][:, tile(t)], acc[:, 4 * (c % 2) + t, tile(c // 2)], ident[:, :])
                last.then_inc(ht_ready, 1)
            for n in range(N_W):
                w, q = n // 4, n % 4
                if q == 0:
                    pe.wait_ge(tern_ready, w + 1)
                if n >= 4:
                    pe.wait_ge(wt_done, n - 3)
                o = W_BANKS[n % 4]
                for m in range(4):
                    if w < 2:
                        src = tern[w][:, D * (4 * (q % 2) + m) + 128 * (q // 2):][:, 0:128]
                    else:
                        src = tern[w][:, E * (m % 2) + 128 * (2 * q + m // 2):][:, 0:128]
                    last = pe.transpose(o[:, tile(m)], src, ident[:, :])
                last.then_inc(wt_ready, 1)
            pe.wait_ge(wt_done, N_W)
            pe.wait_ge(ht_done, 4)
            for c in range(2):
                tok = slice(512 * c, 512 * c + 512)
                for e in range(ET):
                    n = c * ET + e
                    if n >= 2:
                        pe.wait_ge(hid_done, n - 1)
                    for w in range(2):
                        for k in range(K):
                            mm(UG[n % 2][w], lhsT=ternT[w][:, k, tile(e)], rhs=hTh[:, k, tok], start=k == 0, stop=False)
                            last = mm(UG[n % 2][w], lhsT=ternT[w][:, k, tile(e)], rhs=hTl[:, k, tok], start=False,
                                      stop=k == K - 1)
                    last.then_inc(ug_ready, 1)
                pe.wait_ge(hl_done, ET * (c + 1))
                for t in range(4):
                    if c == 1 and t % 2 == 0:
                        pe.wait_ge(y_done, t // 2 + 1)
                    for e in range(ET):
                        o = DN[t // 2][:, 256 * (t % 2):256 * (t % 2) + 256]
                        mm(o, lhsT=Hh[:, e, tile(t)], rhs=ternT[2][:, e, :], start=e == 0, stop=False)
                        last = mm(o, lhsT=Hl[:, e, tile(t)], rhs=ternT[2][:, e, :], start=False, stop=e == ET - 1)
                    if t % 2 == 1:
                        last.then_inc(dn_ready, 1)

        @blk2.scalar
        def _(act):
            for n in range(3):
                act.wait_ge(ld[n], 16)
                act.activation(tern[n][:, :], raw[n][:, :], ACT.Abs, accum_out=asum[:, n:n + 1]).then_inc(abs_done, 1)
            for c in range(4):
                act.wait_ge(ht_ready, c + 1)
                act.activation(hTh[:, c // 2, 512 * (c % 2):512 * (c % 2) + 512], UG[1][c % 2], ACT.Copy).then_inc(ht_hi, 1)
            for n in range(N_W):
                w, q = n // 4, n % 4
                act.wait_ge(wt_ready, n + 1)
                o = W_BANKS[n % 4]
                if w < 2:
                    dst = ternT[w][:, q // 2, 512 * (q % 2):512 * (q % 2) + 512]
                else:
                    dst = ternT[2][:, 2 * q:2 * q + 2, :].rearrange("p e d -> p (e d)")
                act.activation(dst, o[:, :], ACT.Copy).then_inc(wt_done, 1)
            for c in range(2):
                for e in range(ET):
                    n = c * ET + e
                    act.wait_ge(ug_ready, n + 1)
                    act.wait_ge(scl_ready, 1)
                    if n >= 2:
                        act.wait_ge(tt_done, n - 1)
                    act.activation(sg[n % 2][:, :], UG[n % 2][0], ACT.Sigmoid, scale=scl[:, 0:1]).then_inc(sg_done, 1)
                    act.wait_ge(hid_done, n + 1)
                    if c == 1 and e == 0:
                        act.wait_ge(dn_ready, 2)
                    act.activation(Hh[:, e, :], hid[n % 2][:, :], ACT.Copy).then_inc(hh_done, 1)

        @blk2.vector
        def _(dve):
            for t in range(T):
                dve.bn_stats(st[:, t, :], acc[:, t, :]).then_inc(st_done, 1)
            dve.wait_ge(st_done, T)
            for t in range(T):
                ins = dve.bn_aggr(mvl[:, t, :], st[:, t, :])
            ins.then_inc(ag_done, 1)
            dve.wait_ge(rsd_ready, 1)
            dve.wait_ge(ag_done, 1)
            for t in range(T):
                ins = dve.tensor_scalar(acc[:, t, :], acc[:, t, :], mvl[:, t, 0:1], rsd[:, t:t + 1], ALU.subtract, ALU.mult)
            ins.then_inc(ln_done, 1)
            dve.wait_ge(tot_ready, 1)
            dve.tensor_scalar(scl[:, :], SC[0][:, 0:4], 1.0 / (D * E), 1e-8, ALU.mult, ALU.add).then_inc(scl_ready, 1)
            dve.wait_ge(scl_ready, 1)
            dve.tensor_scalar(thr[:, :], scl[:, :], 0.5, None, ALU.mult)
            dve.tensor_scalar(nthr[:, :], scl[:, :], -0.5, None, ALU.mult).then_inc(thr_ready, 1)
            dve.wait_ge(thr_ready, 1)
            dve.wait_ge(abs_done, 3)
            for n in range(3):
                if n:
                    dve.wait_ge(tern_ready, n)
                dve.tensor_scalar(low[:, :], raw[n][:, :], nthr[:, n:n + 1], None, ALU.is_lt).then_inc(low_done, 1)
                dve.wait_ge(low_done, n + 1)
                dve.scalar_tensor_tensor(tern[n][:, :], raw[n][:, :], thr[:, n:n + 1], low[:, :], ALU.is_gt,
                                         ALU.subtract).then_inc(tern_ready, 1)
                if n == 0:
                    for c in range(4):
                        dve.wait_ge(ht_hi, c + 1)
                        d = (slice(None), c // 2, slice(512 * (c % 2), 512 * (c % 2) + 512))
                        dve.tensor_tensor(hTl[d], UG[1][c % 2], hTh[d].bitcast(F32), ALU.subtract).then_inc(ht_done, 1)
            for c in range(2):
                for e in range(ET):
                    n = c * ET + e
                    dve.wait_ge(sg_done, n + 1)
                    dve.scalar_tensor_tensor(tt[n % 2][:, :], UG[n % 2][0], scl[:, 0:1], sg[n % 2][:, :], ALU.mult,
                                             ALU.mult).then_inc(tt_done, 1)
                    dve.wait_ge(tt_done, n + 1)
                    if n >= 2:
                        dve.wait_ge(hl_done, n - 1)
                    dve.scalar_tensor_tensor(hid[n % 2][:, :], UG[n % 2][1], scl[:, 1:2], tt[n % 2][:, :], ALU.mult,
                                             ALU.mult).then_inc(hid_done, 1)
                for i in range(2):
                    t0 = 4 * c + 2 * i
                    dve.wait_ge(dn_ready, 2 * c + i + 1)
                    a = acc[:, t0:t0 + 2, :].rearrange("p t d -> p (t d)")
                    y = yo[:, t0:t0 + 2, :].rearrange("p t d -> p (t d)")
                    dve.scalar_tensor_tensor(y, DN[i][:, :], scl[:, 2:3], a, ALU.mult, ALU.add).then_inc(y_done, 1)
                dve.wait_ge(y_done, 2 * c + 2)
                for t in range(4 * c, 4 * c + 4):
                    dve.bn_stats(st2[:, t, :], yo[:, t, :]).then_inc(y_st, 1)
                dve.wait_ge(y_st, 4 * c + 4)
                for t in range(4 * c, 4 * c + 4):
                    ins = dve.bn_aggr(mv2[:, t, :], st2[:, t, :])
                ins.then_inc(y_ag, 1)
                dve.wait_ge(y_rsd, c + 1)
                dve.wait_ge(y_ag, c + 1)
                for t in range(4 * c, 4 * c + 4):
                    ins = dve.tensor_scalar(yo[:, t, :], yo[:, t, :], mv2[:, t, 0:1], rsd2[:, t:t + 1], ALU.subtract,
                                            ALU.mult)
                ins.then_inc(y_ln, 1)


INPUTS = ["L0_attn_x", "L0_attn_W_cq", "L0_attn_q_norm_w", "L0_attn_q_norm_b", "L0_attn_W_q", "L0_attn_W_ckv",
          "L0_attn_kv_norm_w", "L0_attn_kv_norm_b", "L0_attn_W_kv", "L0_attn_W_o", "L0_attn_W_ip", "L0_attn_W_ig",
          "L0_attn_W_sq", "L0_attn_W_sk", "L0_attn_W_sv", "L0_attn_W_io", "L0_ffn_W_up", "L0_ffn_W_gate",
          "L0_ffn_W_down"]


def constants():
    import numpy as np
    freqs = (1.0 / np.power(np.float32(10000.0), np.arange(0, ROPE, 2, dtype=np.float32) / np.float32(ROPE))).astype(np.float32)
    f = np.outer(np.arange(S, dtype=np.float32), freqs).astype(np.float32)
    cos, sin = np.cos(f).astype(np.float32), np.sin(f).astype(np.float32)
    col = np.arange(64)
    return {
        "c_ident": np.eye(128, dtype=np.float32),
        "c_cos": np.repeat(cos, 2, axis=1),
        "c_sin": np.stack([-sin, sin], axis=-1).reshape(S, ROPE),
        "c_tok": (np.arange(128)[:, None] + 128 * np.arange(T)[None, :]).astype(np.float32),
        "c_blk": (np.arange(8)[:, None] == col[None, :] // TOPK).astype(np.float32),
        "c_off": np.where(col[:, None] // TOPK == col[None, :] // TOPK, 0.0, -1e30).astype(np.float32),
        "c_mean": ((col[:, None] // TOPK == np.arange(8)[None, :]) / TOPK).astype(np.float32),
    }


def kernel(**inputs):
    import numpy as np
    import concourse.bacc as bacc
    from concourse.bass_utils import run_bass_kernel_spmd

    nc = bacc.Bacc("TRN2", target_bir_lowering=False, num_devices=1)
    arrays, args = {}, []
    for name in INPUTS:
        a = np.ascontiguousarray(inputs[name])
        if name == "L0_attn_x":
            a = a.reshape(S, D)
        arrays[f"in_{name}"] = a
    for name, a in constants().items():
        arrays[f"in_{name}"] = np.ascontiguousarray(a)
    for name, a in arrays.items():
        args.append(nc.dram_tensor(name, a.shape, mybir.dt.from_np(a.dtype), kind="ExternalInput").ap())
    args.append(nc.dram_tensor("out", (S, D), F32, kind="ExternalOutput").ap())
    attention_and_mlp(nc, *args)
    r = run_bass_kernel_spmd(nc, [arrays], core_ids=[0])
    return r.results[0]["out"].reshape(1, S, D)
```

```python
import concourse.bass as bass
from concourse import mybir
from contextlib import ExitStack

F32 = mybir.dt.float32
F32R = mybir.dt.float32r
BF16 = mybir.dt.bfloat16
U32 = mybir.dt.uint32
ALU = mybir.AluOpType
ACT = mybir.ActivationFunctionType
AX = mybir.AxisListType

S = 1024
D = 256
NH = 16
NP = NH // 2
NOPE = 128
ROPE = 64
HD = NOPE + ROPE
QL = 192
IH = 8
TOPK = 8
E = 1024
T = S // 128
K = D // 128
QLT = QL - 128
SCALE = float(HD) ** -0.5
SCALE_SIDE = float(128) ** -0.5
EPS = 1e-5
LOW = -3.0e38
NB = 4

CHUNKS = [(i + 4) // 4 for i in range(T)]
CH0 = [sum(CHUNKS[:i]) for i in range(T + 1)]
NCH = CH0[T]
TILE_OF = [i for i in range(T) for _ in range(CHUNKS[i])]


def attention_and_mlp(nc, x, W_cq, q_norm_w, q_norm_b, W_q, W_ckv, kv_norm_w, kv_norm_b, W_kv, W_o,
                      W_ip, W_ig, W_sq, W_sk, W_sv, W_io, W_up, W_gate, W_down,
                      c_ident, c_cos, c_sin, c_tok, c_blk, c_off, c_mean, out):
    top = ExitStack()
    with top:
        stack = [top]

        def sb(name, shape, dt=F32):
            return stack[-1].enter_context(nc.sbuf_tensor(name, shape, dt))

        def sem(name):
            return top.enter_context(nc.semaphore(name))

        SC = [top.enter_context(nc.psum_tensor(f"SC{i}", [128, 1024], F32)) for i in range(2)]
        J = [top.enter_context(nc.psum_tensor(f"J{i}", [128, 512], F32)) for i in range(NB)]

        acc = sb("acc", [128, T, D])
        ident = sb("ident", [128, 128])
        mhalf = sb("mhalf", [128, 16])
        epst = sb("epst", [128, 16])
        held = sem("held")

        def wait(eng, s, v):
            if isinstance(v, int) and v <= 0:
                return
            eng.wait_ge(s, v)

        def hold(eng, s, v):
            wait(eng, s, v)
            eng.sem_inc(held, 1)

        attn = ExitStack()
        stack.append(attn)
        xTh, xTl = sb("xTh", [128, K, S], F32R), sb("xTl", [128, K, S], F32R)
        qch, qcl = sb("qch", [128, S], F32R), sb("qcl", [128, S], F32R)
        qcs = sb("qcs", [128, S], F32R)
        mask = sb("mask", [128, S], BF16)
        cos2, sin2 = sb("cos2", [128, T, ROPE]), sb("sin2", [128, T, ROPE])
        kvw, kvb = sb("kvw", [128, 1]), sb("kvb", [128, 1])
        Wkh, Wkl = sb("Wkh", [128, 2 * NOPE], F32R), sb("Wkl", [128, 2 * NOPE], F32R)
        kvbias = sb("kvbias", [128, 2])
        ioT = sb("ioT", [128, IH])
        iocol = sb("iocol", [128, 2])
        r_kv = sb("r_kv", [128, K, 2 * HD])
        Wckh, Wckl = sb("Wckh", [128, K, 2 * HD], F32R), sb("Wckl", [128, K, 2 * HD], F32R)
        r_qp = sb("r_qp", [128, 2, 2, ROPE])
        Wqph, Wqpl = sb("Wqph", [128, 2, 2, ROPE], F32R), sb("Wqpl", [128, 2, 2, ROPE], F32R)
        r_qn = sb("r_qn", [128, 2, NOPE])
        Wqnh = [sb(f"Wqnh{b}", [128, 2, NOPE], F32R) for b in range(2)]
        Wqnl = [sb(f"Wqnl{b}", [128, 2, NOPE], F32R) for b in range(2)]
        r_o = sb("r_o", [128, D])
        Woh = [sb(f"Woh{b}", [128, D], F32R) for b in range(2)]
        Wol = [sb(f"Wol{b}", [128, D], F32R) for b in range(2)]
        kvraw = sb("kvraw", [128, T, 2 * HD])
        qraw = sb("qraw", [128, T, 2, ROPE])
        ropes = sb("ropes", [128, T, 2, ROPE])
        Rk = sb("Rk", [128, T, 2, 2, ROPE])
        Rq = sb("Rq", [128, T, 2, 2, ROPE])
        bst = sb("bst", [128, T, 2, 6])
        mv = sb("mv", [128, 2 * T, 2])
        veps = sb("veps", [128, 2 * T])
        rstd = sb("rstd", [128, 2 * T])
        kvTh, kvTl = sb("kvTh", [128, S], F32R), sb("kvTl", [128, S], F32R)
        tmp = [sb(f"tmp{c}", [128, 512]) for c in range(2)]
        KNh = [sb(f"KNh{b}", [128, S], F32R) for b in range(2)]
        KNl = [sb(f"KNl{b}", [128, S], F32R) for b in range(2)]
        QNh = [sb(f"QNh{b}", [128, S], F32R) for b in range(2)]
        QNl = [sb(f"QNl{b}", [128, S], F32R) for b in range(2)]
        QS = [sb(f"QS{b}", [128, S], F32R) for b in range(2)]
        KD = [sb(f"KD{b}", [128, S], F32R) for b in range(2)]
        KL = sb("KL", [128, S], F32R)
        Vh, Vl = sb("Vh", [128, T, NOPE], F32R), sb("Vl", [128, T, NOPE], F32R)
        mx = sb("mx", [128, 1])
        nm, sm, rs = sb("nm", [128, 2]), sb("sm", [128, 2]), sb("rs", [128, 2])
        Pb = [sb(f"Pb{i}", [128, S]) for i in range(2)]
        PTh, PTl = sb("PTh", [128, T, 256], F32R), sb("PTl", [128, T, 256], F32R)
        ATh = [sb(f"ATh{i}", [128, 256], F32R) for i in range(2)]
        ATl = [sb(f"ATl{i}", [128, 256], F32R) for i in range(2)]

        wip = Rq[:, :, :, :, :].rearrange("p t h a d -> p (t h a d)").rearrange("p (k n) -> p k n", k=K)
        r_cq = Pb[0][:, 0:400].rearrange("p (k n) -> p k n", k=K)
        r_wkv = Pb[0][:, 512:768]
        s_wkv = ropes[:, 0:2, :, :].rearrange("p t h n -> p (t h n)")
        Wcqh = KNh[1][:, 0:400].rearrange("p (k n) -> p k n", k=K)
        Wcql = KNl[1][:, 0:400].rearrange("p (k n) -> p k n", k=K)
        qcn = Rk[:, :, :, :, :].rearrange("p t h a d -> p t (h a d)")
        gts = Pb[0][:, 768:768 + 64].rearrange("p (t h) -> p t h", t=T)
        qst = Pb[0][:, 832:832 + 48].rearrange("p (t s) -> p t s", t=T)
        qmv = Pb[0][:, 880:896].rearrange("p (t s) -> p t s", t=T)
        wside = Pb[1][:, 0:512].rearrange("p (k n) -> p k n", k=4)
        qnwb = sb("qnwb", [128, 4])
        gT = qraw[0:8, :, :, :].rearrange("p t h n -> p (t h n)")
        m8 = sb("m8", [8, 8])
        i8 = sb("i8", [8, 8], U32)
        i8f = sb("i8f", [8, 8])
        i8d = sb("i8d", [8, 64])
        ones8 = sb("ones8", [8, 128])
        blk = sb("blk", [8, 64])
        tokid = sb("tokid", [128, T])
        off64 = sb("off64", [64, 64])
        mean8 = sb("mean8", [64, 8])
        idxb = sb("idxb", [128, 64])
        oneh = Pb[1][:, 512:1024].rearrange("p (t n) -> p t n", t=T)
        selT = Pb[0][:, 896:1024].rearrange("p (k n) -> p k n", k=K)
        istT = sb("istT", [128, 64])
        sqT, skT = sb("sqT", [128, 64]), sb("skT", [128, 64])
        svs = sb("svs", [64, 128])
        sp_s = sb("sp_s", [64, 64])
        smx = sb("smx", [64, 4])
        pms = sb("pms", [64, 8])
        soT = sb("soT", [128, 8])

        ld_x, ld_c, ld_w0, ld_side = sem("ld_x"), sem("ld_c"), sem("ld_w0"), sem("ld_side")
        ld_kv, ld_qp, ld_qn, ld_o = sem("ld_kv"), sem("ld_qp"), sem("ld_qn"), sem("ld_o")
        const_ready = sem("const_ready")
        hi_w, w0_ready = sem("hi_w"), sem("w0_ready")
        wkv_hi, wkv_ready = sem("wkv_hi"), sem("wkv_ready")
        wqp_hi, wqp_ready = sem("wqp_hi"), sem("wqp_ready")
        wqn_hi, wqn_ready = sem("wqn_hi"), sem("wqn_ready")
        wo_hi, wo_split = sem("wo_hi"), sem("wo_split")
        ready = {k: sem(f"{k}_ready") for k in
                 ("xt", "qc", "qm", "kv", "qp", "kt", "kp", "qt", "kn", "qn", "v", "pv", "wo", "side", "tc", "wb")}
        hi = {k: sem(f"{k}_hi") for k in ("xt", "kt", "kp", "qt", "kn", "qn", "v", "pv", "tc")}
        done = {k: sem(f"{k}_done") for k in
                ("xt", "qc", "qm", "kv", "qp", "kt", "kp", "qt", "kn", "qn", "v", "pv", "wo", "side", "tc",
                 "wb")}
        qc_stat, qc_aggr, qc_veps, qc_rstd, qc_norm = (sem("qc_stat"), sem("qc_aggr"), sem("qc_veps"),
                                                       sem("qc_rstd"), sem("qc_norm"))
        qc_dup = sem("qc_dup")
        qm_part = sem("qm_part")
        qc_split = sem("qc_split")
        bn_done, aggr_done, veps_done, rstd_done, kvn_done = (sem("bn_done"), sem("aggr_done"),
                                                              sem("veps_done"), sem("rstd_done"),
                                                              sem("kvn_done"))
        rk_mul, rk_ready = sem("rk_mul"), sem("rk_ready")
        rq_mul, rq_ready = sem("rq_mul"), sem("rq_ready")
        wkv_scaled = sem("wkv_scaled")
        sc_ready = sem("sc_ready")
        mx_ready, nm_ready = sem("mx_ready"), sem("nm_ready")
        exp_done = sem("exp_done")
        rs_ready, p_ready = sem("rs_ready"), sem("p_ready")
        tp_ready, pt_lo = ready["tc"], done["tc"]
        io_ready = sem("io_ready")
        side_dve = sem("side_dve")
        side_exp = sem("side_exp")

        PER = {"xt": 4, "qc": T, "qm": 4, "kv": T, "qp": 2, "kt": 2, "kp": 2, "qt": 2, "kn": 2, "qn": 2,
               "v": 2, "pv": 4, "wo": 4, "side": 11, "tc": NCH, "wb": 1}

        def count(kind, unit, c):
            return PER[kind] * unit + c + 1

        PAIR_KINDS = ("kv", "qp", "kvn", "kvn2", "ropek", "ropeq", "wkv", "wqp")

        def unit(kind, off, p):
            return p + off if kind in PAIR_KINDS else 2 * p + off

        def t(h, i):
            return [("tc", h, n) for n in range(CH0[i], CH0[i + 1])]

        def head_steps(b, first, last):
            h, n, m = b, b + 1, b - 1
            tail = not (first and b == 0)
            more = not last
            slots = [[] for _ in range(T)]

            def add(i, cond, *steps):
                if cond:
                    slots[i].extend(steps)

            add(0, tail, *t(m, 7), ("wo", m, 2))
            add(1, tail, ("pv", m, 3))
            add(1, True, *t(h, 0), ("v", h, 0), ("v", h, 1))
            if b == 0:
                add(0, True, ("qn", n, 0))
                add(0, more, ("wkv", 1, 0))
                add(2, True, *t(h, 1))
                add(2, tail, ("wo", m, 3))
                add(2, True, ("io", h, 0), ("qn", n, 1), ("kt", n, 0), ("kt", n, 1))
                add(3, True, ("kp", n, 0), ("pv", h, 0), *t(h, 2), ("kn", n, 0), ("wosp", n, 0))
                add(4, True, ("kp", n, 1), *t(h, 3), ("wo", h, 0), ("kn", n, 1))
                add(4, more, ("kv", 1, 0), ("wqp", 1, 0))
                add(5, more, ("kv", 1, 1))
                add(5, True, ("pv", h, 1), *t(h, 4), ("qt", n, 0))
                add(5, more, ("kv", 1, 2), ("wqn", h + 2, 0))
                add(6, more, ("kv", 1, 3))
                add(6, True, *t(h, 5), ("wo", h, 1), ("qt", n, 1))
                add(6, more, ("kv", 1, 4), ("kv", 1, 5))
                add(7, more, ("kv", 1, 6), ("kv", 1, 7))
                add(7, True, ("pv", h, 2), *t(h, 6))
            else:
                add(0, more, ("qp", 1, 0), ("kvn", 1, 0), ("ropek", 1, 0))
                add(1, more, ("qn", n, 0), ("kvn2", 1, 0))
                add(2, True, *t(h, 1), ("wo", m, 3), ("io", h, 0))
                add(2, more, ("qp", 1, 1), ("kvn2", 1, 1), ("ropek", 1, 1))
                add(3, more, ("kt", n, 0))
                add(3, True, ("pv", h, 0), *t(h, 2))
                add(3, more, ("kt", n, 1), ("kvn2", 1, 2), ("ropeq", 1, 0))
                add(4, more, ("kn", n, 0))
                add(4, True, *t(h, 3), ("wo", h, 0))
                add(4, more, ("kn", n, 1), ("kvn2", 1, 3), ("ropeq", 1, 1), ("wosp", n, 0))
                add(5, more, ("kp", n, 0))
                add(5, True, ("pv", h, 1), *t(h, 4))
                add(5, more, ("kp", n, 1), ("wqn", h + 2, 0))
                add(6, more, ("qn", n, 1))
                add(6, True, *t(h, 5), ("wo", h, 1))
                add(6, more, ("qt", n, 0))
                add(7, more, ("qt", n, 1))
                add(7, True, ("pv", h, 2), *t(h, 6))
            exp_at, norm_at = [[2, 2, 2, 2, 2, 2, 2, 2], [2, 2, 2, 2, 2, 2, 2, 2]], [[2, 2, 2, 2, 2, 2, 2, 2], [2, 2, 2, 2, 2, 2, 2, 2]]
            s = []
            for i in range(T):
                n = len(slots[i])
                e, d = min(exp_at[b][i], n), min(norm_at[b][i], n)
                s += [("qk", h, i), *slots[i][:e], ("exp", h, i), *slots[i][e:d], ("norm", h, i), *slots[i][d:]]
            return s

        def pair_steps(first=False, last=False):
            return head_steps(0, first, last) + head_steps(1, first, last)

        SIDE = [("side", 0, c) for c in range(11)]
        PROLOGUE = ([("xt", 0, c) for c in range(4)] + [("qc", 0, t) for t in range(T)] + [("wb", 0, 0)] +
                    [("wkv", 0, 0)] + SIDE[0:2] + [("kv", 0, 0), ("kv", 0, 1)] + SIDE[2:3] +
                    [("kv", 0, 2)] + SIDE[3:4] + [("kv", 0, 3)] + SIDE[4:5] +
                    [("wqp", 0, 0), ("kv", 0, 4)] + SIDE[5:6] + [("kv", 0, 5)] + SIDE[6:7] + [("kv", 0, 6)] + SIDE[7:8] +
                    [("kv", 0, 7)] + [("qm", 0, c) for c in range(4)] +
                    [("kvn", 0, 0), ("wqn", 0, 0), ("ropek", 0, 0), ("ropek", 0, 1)] + [("kvn2", 0, c) for c in range(4)] +
                    [("qp", 0, c) for c in range(2)] + SIDE[8:9] +
                    [("ropeq", 0, 0), ("ropeq", 0, 1), ("wosp", 0, 0), ("wqn", 1, 0)] +
                    [("kt", 0, 0), ("kt", 0, 1), ("qn", 0, 0), ("qn", 0, 1)] + SIDE[9:10] + [("kn", 0, 0), ("kn", 0, 1)] +
                    SIDE[10:] + [("kp", 0, 0), ("kp", 0, 1), ("qt", 0, 0), ("qt", 0, 1)])
        EPILOGUE = [*t(NH - 1, 7), ("wo", NH - 1, 2), ("pv", NH - 1, 3), ("wo", NH - 1, 3)]

        BANKED = tuple(PER)

        def banked(steps):
            return [s for s in steps if s[0] in BANKED or s[0] == "skip"]

        FIRST, MID, LAST = pair_steps(first=True), pair_steps(), pair_steps(last=True)
        PROLOGUE += [("skip", 0, 0)] * (-len(banked(PROLOGUE)) % NB)
        fill = [("skip", 0, 0)] * (-len(banked(MID)) % NB)
        MID += fill
        FIRST += fill
        FIRST[0:0] = [("skip", 0, 0)] * (-len(banked(FIRST)) % NB)
        BANKED_ALL = BANKED + ("skip",)

        def numbered(steps, start=0):
            n, res = start, []
            for s in steps:
                if s[0] in BANKED_ALL:
                    res.append((*s, n % NB))
                    n += 1
                else:
                    res.append((*s, None))
            return res

        EPI = numbered(EPILOGUE, len(banked(LAST)))

        def half(c):
            return slice(512 * c, 512 * c + 512)

        def tile(t):
            return slice(128 * t, 128 * t + 128)

        block = top.enter_context(ExitStack())
        blk1 = block.enter_context(nc.Block())

        @blk1.sync
        def _(sp):
            sp.dma_start(acc[:, :, :], x.rearrange("(t p) d -> p t d", p=128)).then_inc(ld_x, 16)
            sp.dma_start(ident[:, :], c_ident).then_inc(ld_x, 16)
            cq = W_cq.rearrange("(k p) n -> p k n", p=128)
            sp.dma_start(r_cq[:, :, 0:QL], cq).then_inc(ld_w0, 16)
            sp.dma_start(r_cq[:, :, QL:QL + IH], W_ig.rearrange("(k p) n -> p k n", p=128)).then_inc(ld_w0, 16)
            sp.dma_start(r_wkv, W_kv).then_inc(ld_w0, 16)

            ckv = W_ckv.rearrange("(k p) n -> p k n", p=128)
            wq2 = W_q.rearrange("r (h n) -> r h n", n=HD)

            def load(kind, u):
                if kind == "wkv":
                    wait(sp, wkv_ready, u)
                    sp.dma_start(r_kv[:, :, :], ckv[:, :, bass.ds(u * (2 * HD), 2 * HD)]).then_inc(ld_kv, 16)
                if kind == "wqp":
                    wait(sp, wqp_ready, u)
                    cols = wq2[:, bass.ds(u * 2, 2), NOPE:HD]
                    sp.dma_start(r_qp[:, 0, :, :], cols[0:128]).then_inc(ld_qp, 16)
                    for r in range(2):
                        sp.dma_start(r_qp[64 * r:64 * r + 64, 1, :, :], cols[128:QL]).then_inc(ld_qp, 16)
                if kind == "wqn":
                    wait(sp, wqn_ready, u)
                    cols = W_q[:, bass.ds(u * HD, NOPE)]
                    sp.dma_start(r_qn[:, 0, :], cols[0:128]).then_inc(ld_qn, 16)
                    for r in range(2):
                        sp.dma_start(r_qn[64 * r:64 * r + 64, 1, :], cols[128:QL]).then_inc(ld_qn, 16)
                if kind == "wosp":
                    wait(sp, wo_split, u)
                    sp.dma_start(r_o[:, :], W_o[bass.ds(u * NOPE, NOPE), :]).then_inc(ld_o, 16)

            for kind in ("wkv", "wqp", "wqn", "wosp"):
                load(kind, 0)
            sp.dma_start(qnwb[:, 0:1], q_norm_w[0:128].rearrange("(p a) -> p a", a=1)).then_inc(ld_c, 16)
            sp.dma_start(qnwb[:, 1:2], q_norm_b[0:128].rearrange("(p a) -> p a", a=1)).then_inc(ld_c, 16)
            for r in range(2):
                rows = slice(64 * r, 64 * r + 64)
                sp.dma_start(qnwb[rows, 2:3], q_norm_w[128:QL].rearrange("(p a) -> p a", a=1)).then_inc(ld_c, 16)
                sp.dma_start(qnwb[rows, 3:4], q_norm_b[128:QL].rearrange("(p a) -> p a", a=1)).then_inc(ld_c, 16)
            sp.dma_start(kvw[:, :], kv_norm_w.rearrange("(p a) -> p a", a=1)).then_inc(ld_c, 16)
            sp.dma_start(kvb[:, :], kv_norm_b.rearrange("(p a) -> p a", a=1)).then_inc(ld_c, 16)
            sp.dma_start(cos2[:, :, :], c_cos.rearrange("(t p) d -> p t d", p=128)).then_inc(ld_c, 16)
            sp.dma_start(sin2[:, :, :], c_sin.rearrange("(t p) d -> p t d", p=128)).then_inc(ld_c, 16)
            for dst, src in ((blk[:, :], c_blk), (tokid[:, :], c_tok), (off64[:, :], c_off), (mean8[:, :], c_mean),
                             (wip, W_ip.rearrange("(k p) n -> p k n", p=128)), (wside[:, 0, :], W_sq),
                             (wside[:, 1, :], W_sk), (wside[:, 2, :], W_sv), (wside[:, 3, :], W_io[:, 0:128])):
                sp.dma_start(dst, src).then_inc(ld_side, 16)
            load("wqn", 1)

            def run(steps, p):
                for kind, off, c in steps:
                    if kind in ("wkv", "wqp", "wqn", "wosp"):
                        load(kind, unit(kind, off, p))

            run(FIRST, 0)
            with sp.Fori(1, NP - 1) as p:
                run(MID, p)
            run(LAST, NP - 1)

        LD_C, LD_SIDE, LD_W0 = 16 * 10, 16 * 9, 16 * 3

        @blk1.gpsimd
        def _(gp):
            gp.memset(mhalf[:, :], -0.5)
            gp.memset(epst[:, :], EPS)
            gp.memset(ones8[:, :], 1.0).then_inc(const_ready, 1)
            gp.memset(mask[:, :], 0.0).then_inc(const_ready, 1)
            gp.wait_ge(const_ready, 2)
            gp.affine_select(out=mask[:, S - 128:S], in_=mask[:, S - 128:S], compare_op=ALU.is_ge, fill=-1e30, base=0,
                             pattern=[[-1, 128]], channel_multiplier=1).then_inc(const_ready, 1)
            gp.wait_ge(ld_w0, LD_W0)
            gp.tensor_copy(Wcqh[:, :, :], r_cq).then_inc(hi_w, 1)
            gp.wait_ge(hi_w, 1)
            gp.tensor_tensor(Wcql[:, :, :], r_cq, Wcqh[:, :, :].bitcast(F32), ALU.subtract).then_inc(w0_ready, 1)
            gp.wait_ge(ld_c, LD_C)
            gp.tensor_tensor(s_wkv, r_wkv, kvw[:, 0:1].to_broadcast([128, 2 * NOPE]), ALU.mult).then_inc(wkv_scaled, 1)
            gp.wait_ge(wkv_scaled, 1)
            gp.tensor_copy(Wkh[:, :], s_wkv).then_inc(hi_w, 1)
            gp.wait_ge(hi_w, 2)
            gp.tensor_tensor(Wkl[:, :], s_wkv, Wkh[:, :].bitcast(F32), ALU.subtract).then_inc(w0_ready, 1)

            def split(loaded, n_loaded, raw, wh, wl, wh_done, wl_done, used, n_used, u):
                hold(gp, loaded, n_loaded)
                hold(gp, used, n_used)
                gp.tensor_copy(wh, raw).then_inc(wh_done, 1)
                gp.wait_ge(wh_done, u + 1)
                gp.tensor_tensor(wl, raw, wh.bitcast(F32), ALU.subtract).then_inc(wl_done, 1)

            def rope(src, dst, mul, rdy, u, c, waits):
                for w in waits:
                    hold(gp, *w)
                t = slice(4 * c, 4 * c + 4)
                src = src[:, t]
                cosb = cos2[:, t, :].rearrange("p t (a d) -> p t a d", a=1).to_broadcast([128, 4, 2, ROPE])
                for e in range(2):
                    s = sin2[:, t, e::2].rearrange("p t (a d) -> p t a d", a=1).to_broadcast([128, 4, 2, ROPE // 2])
                    ins = gp.tensor_tensor(ropes[:, t, :, e::2], src[:, :, :, 1 - e::2], s, ALU.mult)
                ins.then_inc(mul, 1)
                gp.wait_ge(mul, 4 * u + 2 * c + 1)
                gp.tensor_tensor(src, src, cosb, ALU.mult).then_inc(mul, 1)
                gp.wait_ge(mul, 4 * u + 2 * c + 2)
                for hh in range(2):
                    a = src[:, :, hh, :].rearrange("p t (a d) -> p t a d", a=1).to_broadcast([128, 4, 2, ROPE])
                    b = ropes[:, t, hh, :].rearrange("p t (a d) -> p t a d", a=1).to_broadcast([128, 4, 2, ROPE])
                    ins = gp.tensor_tensor(dst[:, t, hh, :, :], a, b, ALU.add)
                ins.then_inc(rdy, 1)

            def inv_std(stats, v, r, s_in, n_in, s_mid, s_out, n):
                hold(gp, s_in, n_in)
                gp.tensor_tensor(v, stats, epst[:, 0:v.shape[1]], ALU.add).then_inc(s_mid, 1)
                gp.wait_ge(s_mid, n)
                gp.tensor_tensor(r, v, mhalf[:, 0:v.shape[1]], ALU.pow).then_inc(s_out, 1)

            def run(steps, p):
                for kind, off, c, bank in steps:
                    u = unit(kind, off, p)
                    if kind == "wkv":
                        split(ld_kv, 16 * u + 16, r_kv[:, :, :], Wckh[:, :, :], Wckl[:, :, :], wkv_hi, wkv_ready,
                              ready["kv"], T * u, u)
                    if kind == "wqp":
                        split(ld_qp, 48 * u + 48, r_qp[:, :, :, :], Wqph[:, :, :, :], Wqpl[:, :, :, :], wqp_hi, wqp_ready,
                              ready["qp"], 2 * u, u)
                    if kind == "wqn":
                        b = off % 2
                        split(ld_qn, 48 * u + 48, r_qn[:, :, :], Wqnh[b][:, :, :], Wqnl[b][:, :, :], wqn_hi, wqn_ready,
                              ready["qn"], 2 * (u - 1), u)
                    if kind == "wosp":
                        b = off % 2
                        split(ld_o, 16 * u + 16, r_o[:, :], Woh[b][:, :], Wol[b][:, :], wo_hi, wo_split,
                              ready["wo"], 4 * (u - 1), u)
                    if kind == "qm" and c == 0:
                        inv_std(qmv[:, :, 1], veps[:, 0:T], rstd[:, 0:T], qc_aggr, 1, qc_veps, qc_rstd, 1)
                    if kind == "kvn":
                        if isinstance(u, int) and u == 0:
                            hold(gp, qc_norm, 1)
                        inv_std(mv[:, :, 1], veps[:, :], rstd[:, :], aggr_done, u + 1, veps_done, rstd_done, u + 1)
                    if kind == "ropek":
                        src = kvraw[:, :, :].rearrange("p t (h n) -> p t h n", h=2)[:, :, :, 0:ROPE]
                        start = isinstance(u, int) and u == 0
                        waits = [(done["kv"], T * (u + 1)), (done["qm"], 4) if start else (ready["kp"], 4 * u)]
                        rope(src, Rk, rk_mul, rk_ready, u, c, waits + ([] if start else [(rq_ready, 2 * u)]))
                    if kind == "ropeq":
                        start = isinstance(u, int) and u == 0
                        waits = [(done["qp"], 2 * (u + 1)), (done["side"], 5) if start else (ready["qt"], 4 * u)]
                        rope(qraw[:, :, :, :], Rq, rq_mul, rq_ready, u, c, waits + [(rk_ready, 2 * u + 2)])
            run(numbered(PROLOGUE), 0)
            run(numbered(FIRST), 0)
            with gp.Fori(1, NP - 1) as p:
                run(numbered(MID), p)
            run(numbered(LAST), NP - 1)

        @blk1.tensor
        def _(pe):
            mm = pe.matmul

            def three(o, wh, wl, xh, xl, start, stop):
                mm(o, lhsT=wh, rhs=xh, start=start, stop=False)
                mm(o, lhsT=wh, rhs=xl, start=False, stop=False)
                return mm(o, lhsT=wl, rhs=xh, start=False, stop=stop)

            def qk(h, b, i):
                if i == 0:
                    pe.wait_ge(done["qn"], count("qn", h, 1))
                    pe.wait_ge(done["kn"], count("kn", h, 1))
                    pe.wait_ge(done["kp"], count("kp", h, 1))
                    pe.wait_ge(done["qt"], count("qt", h, 1))
                wait(pe, exp_done, T * h + i - 1)
                o, q, r = SC[i % 2], tile(i), slice(64 * b, 64 * b + 64)
                for c in range(CHUNKS[i]):
                    k = slice(512 * c, min(512 * c + 512, 128 * (i + 1)))
                    mm(o[:, k], lhsT=QNh[b][:, q], rhs=KNh[b][:, k], start=True, stop=False)
                    mm(o[:, k], lhsT=QNh[b][:, q], rhs=KNl[b][:, k], start=False, stop=False)
                    mm(o[:, k], lhsT=QNl[b][:, q], rhs=KNh[b][:, k], start=False, stop=False)
                    mm(o[:, k], lhsT=QS[b][:, q], rhs=KD[b][:, k], start=False, stop=False)
                    last = mm(o[:, k], lhsT=QS[b][r, q], rhs=KL[r, k], start=False, stop=True)
                last.then_inc(sc_ready, 1)

            def tr(h, n, o):
                i = TILE_OF[n]
                c = n - CH0[i]
                if c == 0:
                    pe.wait_ge(p_ready, T * h + i + 1)
                for j in range(4 * c, min(4 * c + 4, i + 1)):
                    last = pe.transpose(o[:, tile(j - 4 * c)], Pb[i % 2][:, tile(j)], ident[:, :])
                return last

            def pv(h, b, g, o):
                if g == 0:
                    pe.wait_ge(done["v"], 2 * h + 2)
                pe.wait_ge(pt_lo, NCH * h + CH0[2 * g + 2])
                for j in range(2 * g + 2):
                    q = slice(0, 256) if j <= 2 * g else slice(128, 256)
                    last = three(o[:, q], Vh[:, j, :], Vl[:, j, :], PTh[:, j, q], PTl[:, j, q], j == 0, j == 2 * g + 1)
                return last

            def side(c, o):
                w = done["side"]
                if c == 0 or c == 1:
                    if c == 0:
                        pe.wait_ge(done["qc"], T)
                    for t in range(4):
                        last = pe.transpose(o[0:8, tile(t)], gts[:, 4 * c + t, :], ident[:, :])
                    return last
                if c == 2:
                    pe.wait_ge(side_dve, 4)
                    return mm(o[:, 0:64], lhsT=ones8[:, :], rhs=i8d[:, :], start=True, stop=True)
                if c == 3:
                    pe.wait_ge(side_dve, 5)
                    for k in range(K):
                        for t in range(T):
                            last = mm(o[:, 64 * k:64 * k + 64], lhsT=acc[:, t, tile(k)], rhs=oneh[:, t, :],
                                      start=t == 0, stop=t == T - 1)
                    return last
                pe.wait_ge(w, c)
                if c == 4:
                    for h in range(IH):
                        for k in range(K):
                            last = mm(o[:, 8 * h:8 * h + 8], lhsT=wip[:, k, tile(h)], rhs=selT[:, k, 8 * h:8 * h + 8],
                                      start=k == 0, stop=k == K - 1)
                    return last
                if c == 5:
                    mm(o[:, 0:64], lhsT=wside[:, 0, :], rhs=istT[:, :], start=True, stop=True)
                    return mm(o[:, 64:128], lhsT=wside[:, 1, :], rhs=istT[:, :], start=True, stop=True)
                if c == 6:
                    return mm(o[0:64, 0:128], lhsT=istT[:, :], rhs=wside[:, 2, :], start=True, stop=True)
                if c == 7:
                    return mm(o[0:64, 0:64], lhsT=sqT[:, :], rhs=skT[:, :], start=True, stop=True)
                if c == 8:
                    pe.wait_ge(side_dve, 9)
                    return mm(o[0:64, 0:8], lhsT=sp_s[:, :], rhs=mean8[:, :], start=True, stop=True)
                if c == 9:
                    return mm(o[:, 0:8], lhsT=svs[:, :], rhs=pms[:, :], start=True, stop=True)
                return mm(o[:, 0:8], lhsT=wside[:, 3, :], rhs=soT[:, :], start=True, stop=True)

            def use(kind, off, c, bank, p):
                u, o = unit(kind, off, p), J[bank]
                b = off % 2
                if kind == "xt":
                    if c == 0:
                        pe.wait_ge(ld_x, 32)
                    for t in range(4):
                        last = pe.transpose(o[:, tile(t)], acc[:, 4 * (c % 2) + t, tile(c // 2)], ident[:, :])
                if kind == "qc":
                    if c == 0:
                        pe.wait_ge(w0_ready, 1)
                        pe.wait_ge(done["xt"], 4)
                    for k in range(K):
                        last = three(o[:, 0:200], xTh[:, k, tile(c)], xTl[:, k, tile(c)], Wcqh[:, k, :], Wcql[:, k, :],
                                     k == 0, k == K - 1)
                if kind == "qm":
                    if c == 0:
                        pe.wait_ge(qc_norm, 1)
                    for t in range(4):
                        src = qcn[:, 4 * (c % 2) + t, 128 * (c // 2):128 * (c // 2) + 128]
                        last = pe.transpose(o[:, tile(t)], src, ident[:, :])
                if kind == "kv":
                    if c == 0:
                        pe.wait_ge(wkv_ready, u + 1)
                    for k in range(K):
                        last = three(o[:, 0:2 * HD], xTh[:, k, tile(c)], xTl[:, k, tile(c)], Wckh[:, k, :], Wckl[:, k, :],
                                     k == 0, k == K - 1)
                if kind == "qp":
                    if c == 0:
                        pe.wait_ge(wqp_ready, u + 1)
                        if isinstance(u, int) and u == 0:
                            pe.wait_ge(qc_split, 4)
                    for t in range(4):
                        tok = tile(4 * c + t)
                        w = [Wqph[:, r, :, :].rearrange("p h n -> p (h n)") for r in range(2)]
                        wl = [Wqpl[:, r, :, :].rearrange("p h n -> p (h n)") for r in range(2)]
                        ot = o[:, tile(t)]
                        three(ot, qch[:, tok], qcl[:, tok], w[0], wl[0], True, False)
                        mm(ot, lhsT=qcs[:, tok], rhs=w[1], start=False, stop=False)
                        last = mm(ot, lhsT=qcs[:, tok], rhs=wl[1], start=False, stop=True)
                if kind == "kt":
                    pe.wait_ge(kvn_done, 4 * (p + off // 2) + 2 * b + c + 1)
                    for t in range(4):
                        last = pe.transpose(o[:, tile(t)], kvraw[:, 4 * c + t, b * HD + ROPE:b * HD + HD], ident[:, :])
                if kind == "kp" or kind == "qt":
                    src, rdy = (Rk, rk_ready) if kind == "kp" else (Rq, rq_ready)
                    if c == 0:
                        pe.wait_ge(rdy, 2 * (p + off // 2) + 2)
                    for t in range(4):
                        a = src[:, 4 * c + t, b, :, :].rearrange("p a d -> p (a d)")
                        last = pe.transpose(o[:, tile(t)], a, ident[:, :])
                if kind == "kn":
                    if isinstance(u, int) and u == 0 and c == 0:
                        pe.wait_ge(w0_ready, 2)
                    pe.wait_ge(done["kt"], count("kt", u, c))
                    last = three(o[:, :], Wkh[:, 0:NOPE], Wkl[:, 0:NOPE], kvTh[:, half(c)], kvTl[:, half(c)], True, True)
                if kind == "qn":
                    if c == 0:
                        pe.wait_ge(wqn_ready, u + 1)
                    three(o[:, :], Wqnh[b][:, 0, :], Wqnl[b][:, 0, :], qch[:, half(c)], qcl[:, half(c)], True, False)
                    mm(o[:, :], lhsT=Wqnh[b][:, 1, :], rhs=qcs[:, half(c)], start=False, stop=False)
                    last = mm(o[:, :], lhsT=Wqnl[b][:, 1, :], rhs=qcs[:, half(c)], start=False, stop=True)
                if kind == "v":
                    pe.wait_ge(done["kt"], count("kt", u, 1))
                    for t in range(4):
                        tok = tile(4 * c + t)
                        last = three(o[:, tile(t)], kvTh[:, tok], kvTl[:, tok], Wkh[:, NOPE:], Wkl[:, NOPE:], True, True)
                if kind == "wb":
                    pe.wait_ge(ld_c, LD_C)
                    pe.wait_ge(ld_w0, LD_W0)
                    mm(o[:, 0:1], lhsT=r_wkv[:, 0:NOPE], rhs=kvb[:, :], start=True, stop=True)
                    last = mm(o[:, 1:2], lhsT=r_wkv[:, NOPE:], rhs=kvb[:, :], start=True, stop=True)
                if kind == "tc":
                    last = tr(u, c, o)
                if kind == "pv":
                    last = pv(u, b, c, o)
                if kind == "wo":
                    pe.wait_ge(done["pv"], count("pv", u, c))
                    if c == 0:
                        pe.wait_ge(wo_split, u + 1)
                    for t in range(2):
                        last = three(o[:, 256 * t:256 * t + 256], ATh[c % 2][:, tile(t)], ATl[c % 2][:, tile(t)],
                                     Woh[b][:, :], Wol[b][:, :], True, True)
                if kind == "side":
                    if c == 0:
                        pe.wait_ge(ld_side, LD_SIDE)
                    last = side(c, o)
                last.then_inc(ready[kind], 1)

            def run(steps, p, before):
                prev = list(before)
                for kind, off, c, bank in steps:
                    if kind == "qk":
                        qk(unit(kind, off, p), off % 2, c)
                    elif kind in BANKED_ALL:
                        free = prev[-NB]
                        if free is not None and kind != "skip":
                            pe.wait_ge(done[free[0]], count(*free))
                        if kind == "skip":
                            prev.append(prev[-NB])
                        else:
                            use(kind, off, c, bank, p)
                            prev.append((kind, unit(kind, off, p), c))
                return prev[-NB:]

            def at(uses, p):
                return [(k, unit(k, off, p), c) for k, off, c in uses]

            def last_uses(steps):
                prev = [None] * NB
                for s in steps:
                    if s[0] in BANKED:
                        prev.append(s)
                    elif s[0] == "skip":
                        prev.append(prev[-NB])
                return prev[-NB:]

            run(numbered(PROLOGUE), 0, [None] * NB)
            run(numbered(FIRST), 0, at(last_uses(PROLOGUE), 0))
            assert last_uses(FIRST) == last_uses(MID)
            with pe.Fori(1, NP - 1) as p:
                run(numbered(MID), p, at(last_uses(MID), p - 1))
            run(numbered(LAST), NP - 1, at(last_uses(MID), NP - 2))
            run(EPI, 0, at(last_uses(LAST), NP - 1))

        @blk1.scalar
        def _(act):
            def copy(o, i):
                return act.activation(o, i, ACT.Copy)

            def run(steps, p):
                for kind, off, c, bank in steps:
                    u, b = unit(kind, off, p), off % 2
                    o = J[bank] if bank is not None else None
                    if kind == "exp":
                        i = c
                        act.wait_ge(nm_ready, T * u + i + 1)
                        wait(act, tp_ready, NCH * u + (CH0[i - 1] if i >= 2 else (CH0[i + 7] - NCH)))
                        if isinstance(u, int) and u == 0 and i == 0:
                            act.wait_ge(done["side"], 11)
                        w = slice(0, 128 * (i + 1))
                        act.activation(Pb[i % 2][:, w], SC[i % 2][:, w], ACT.Exp, bias=nm[:, i % 2:i % 2 + 1],
                                       scale=SCALE, accum_out=sm[:, i % 2:i % 2 + 1]).then_inc(exp_done, 1)
                    if kind in ready and kind not in ("side", "wb"):
                        act.wait_ge(ready[kind], count(kind, u, c))
                    if kind == "tc":
                        i = TILE_OF[c]
                        k = 4 * (c - CH0[i])
                        nb = min(4, i + 1 - k)
                        copy(PTh[:, k:k + nb, tile(i % 2)],
                             o[:, 0:128 * nb].rearrange("p (j q) -> p j q", j=nb)).then_inc(hi["tc"], 1)
                    if kind == "xt":
                        copy(xTh[:, c // 2, half(c % 2)], o[:, :]).then_inc(hi["xt"], 1)
                    if kind == "qc":
                        copy(qcn[:, c, 0:QL], o[:, 0:QL])
                        copy(gts[:, c, :], o[:, QL:QL + IH]).then_inc(done["qc"], 1)
                    if kind == "qm":
                        if c == 0:
                            act.wait_ge(ld_c, LD_C)
                        if c >= 2:
                            act.wait_ge(qc_split, c - 1)
                        w, bb = (0, 1) if c < 2 else (2, 3)
                        act.activation(tmp[c % 2][:, :], o[:, :], ACT.Identity, bias=qnwb[:, bb:bb + 1],
                                       scale=qnwb[:, w:w + 1]).then_inc(done["qm"], 1)
                    if kind == "kv":
                        if c == 0:
                            wait(act, rk_ready, 2 * u)
                        copy(kvraw[:, c, :], o[:, 0:2 * HD]).then_inc(done["kv"], 1)
                    if kind == "qp":
                        if c == 0 and isinstance(u, int) and u == 0:
                            act.wait_ge(side_dve, 2)
                        elif c == 0:
                            act.wait_ge(rq_ready, 2 * u)
                        copy(qraw[:, 4 * c:4 * c + 4, :, :].rearrange("p t h n -> p (t h n)"), o[:, :]).then_inc(done["qp"], 1)
                    if kind == "kt":
                        copy(kvTh[:, half(c)], o[:, :]).then_inc(hi["kt"], 1)
                    if kind == "kp":
                        copy(KD[b][:, half(c)], o[:, :]).then_inc(hi["kp"], 1)
                    if kind == "qt":
                        copy(QS[b][:, half(c)], o[:, :]).then_inc(hi["qt"], 1)
                    if kind == "kn":
                        if isinstance(u, int) and u == 0 and c == 0:
                            act.wait_ge(done["wb"], 1)
                        act.activation(KNh[b][:, half(c)], o[:, :], ACT.Identity, bias=kvbias[:, 0:1]).then_inc(hi["kn"], 1)
                    if kind == "qn":
                        copy(QNh[b][:, half(c)], o[:, :]).then_inc(hi["qn"], 1)
                    if kind == "v":
                        copy(Vh[:, 4 * c:4 * c + 4, :].rearrange("p t n -> p (t n)"), o[:, :]).then_inc(hi["v"], 1)
                    if kind == "pv":
                        if c == 0:
                            act.wait_ge(io_ready, u + 1)
                        wait(act, ready["wo"], 4 * u + c - 1)
                        act.activation(ATh[c % 2][:, :], o[:, 0:256], ACT.Identity,
                                       bias=iocol[:, b:b + 1]).then_inc(hi["pv"], 1)
                    if kind == "side" and c == 7:
                        act.wait_ge(side_dve, 7)
                        act.activation(sp_s[:, :], o[0:64, 0:64], ACT.Exp, bias=smx[:, 1:2], scale=SCALE_SIDE,
                                       accum_out=smx[:, 2:3]).then_inc(side_exp, 1)

            run(numbered(PROLOGUE), 0)
            run(numbered(FIRST), 0)
            with act.Fori(1, NP - 1) as p:
                run(numbered(MID), p)
            run(numbered(LAST), NP - 1)
            run(EPI, 0)

        @blk1.vector
        def _(dve):
            def lo(kind, u, c, o, i, h):
                dve.wait_ge(hi[kind], count(kind, u, c))
                dve.tensor_tensor(o, i, h.bitcast(F32), ALU.subtract).then_inc(done[kind], 1)

            def side(c, o):
                n = count("side", 0, c)
                dve.wait_ge(ready["side"], n)
                cp = dve.tensor_copy
                d = done["side"]
                if c in (0, 1):
                    cp(gT[:, half(c)], o[0:8, :]).then_inc(d, 1)
                if c == 1:
                    dve.wait_ge(d, 2)
                    dve.max(m8[:, :], gT).then_inc(side_dve, 1)
                    dve.wait_ge(side_dve, 1)
                    dve.max_index(i8[:, :], m8[:, :], gT).then_inc(side_dve, 1)
                    dve.wait_ge(side_dve, 2)
                    cp(i8f[:, :], i8[:, :]).then_inc(side_dve, 1)
                    dve.wait_ge(side_dve, 3)
                    a = i8f[:, :].rearrange("p (a k) -> p a k", a=1).to_broadcast([8, 8, 8])
                    dve.wait_ge(ld_side, LD_SIDE)
                    dve.tensor_tensor(i8d[:, :].rearrange("p (h k) -> p h k", h=8), a,
                                      blk[:, :].rearrange("p (h k) -> p h k", h=8), ALU.mult).then_inc(side_dve, 1)
                if c == 2:
                    cp(idxb[:, :], o[:, 0:64]).then_inc(d, 1)
                    dve.wait_ge(d, 3)
                    a = idxb[:, :].rearrange("p (a n) -> p a n", a=1).to_broadcast([128, T, 64])
                    bb = tokid[:, :].rearrange("p (t a) -> p t a", a=1).to_broadcast([128, T, 64])
                    dve.tensor_tensor(oneh[:, :, :], a, bb, ALU.is_equal).then_inc(side_dve, 1)
                if c == 3:
                    cp(selT[:, :, :].rearrange("p k n -> p (k n)"), o[:, 0:128]).then_inc(d, 1)
                if c == 4:
                    cp(istT[:, :], o[:, 0:64]).then_inc(d, 1)
                if c == 5:
                    cp(sqT[:, :], o[:, 0:64])
                    cp(skT[:, :], o[:, 64:128]).then_inc(d, 1)
                if c == 6:
                    cp(svs[:, :], o[0:64, 0:128]).then_inc(d, 1)
                if c == 7:
                    dve.tensor_tensor_reduce(out=o[0:64, 0:64], in0=o[0:64, 0:64], in1=off64[:, :], scale=1.0, scalar=LOW,
                                             op0=ALU.add, op1=ALU.max, accum_out=smx[:, 0:1]).then_inc(side_dve, 1)
                    dve.wait_ge(side_dve, 6)
                    dve.tensor_scalar(smx[:, 1:2], smx[:, 0:1], -SCALE_SIDE, None, ALU.mult).then_inc(side_dve, 1)
                    dve.wait_ge(side_exp, 1)
                    dve.reciprocal(smx[:, 3:4], smx[:, 2:3]).then_inc(side_dve, 1)
                    dve.wait_ge(side_dve, 8)
                    dve.tensor_scalar(sp_s[:, :], sp_s[:, :], smx[:, 3:4], None, ALU.mult).then_inc(side_dve, 1)
                    dve.wait_ge(side_dve, 9)
                    dve.sem_inc(d, 1)
                if c == 8:
                    cp(pms[:, :], o[0:64, 0:8]).then_inc(d, 1)
                if c == 9:
                    cp(soT[:, :], o[:, 0:8]).then_inc(d, 1)
                if c == 10:
                    dve.wait_ge(done["wb"], 1)
                    dve.tensor_scalar(ioT[:, :], o[:, 0:8], kvbias[:, 1:2], None, ALU.add).then_inc(d, 1)

            def run(steps, p):
                for kind, off, c, bank in steps:
                    u, b = unit(kind, off, p), off % 2
                    o = J[bank] if bank is not None else None
                    if kind == "qk":
                        i = c
                        w = slice(0, 128 * (i + 1))
                        hold(dve, sc_ready, T * u + i + 1)
                        dve.tensor_tensor_reduce(out=SC[i % 2][:, w], in0=SC[i % 2][:, w], in1=mask[:, 128 * (7 - i):S],
                                                 scale=1.0, scalar=LOW, op0=ALU.add, op1=ALU.max,
                                                 accum_out=mx[:, 0:1]).then_inc(mx_ready, 1)
                        dve.wait_ge(mx_ready, T * u + i + 1)
                        dve.tensor_scalar(nm[:, i % 2:i % 2 + 1], mx[:, 0:1], -SCALE, None, ALU.mult).then_inc(nm_ready, 1)
                    if kind == "norm":
                        i = c
                        w = slice(0, 128 * (i + 1))
                        dve.wait_ge(exp_done, T * u + i + 1)
                        dve.reciprocal(rs[:, i % 2:i % 2 + 1], sm[:, i % 2:i % 2 + 1]).then_inc(rs_ready, 1)
                        dve.wait_ge(rs_ready, T * u + i + 1)
                        dve.tensor_scalar(Pb[i % 2][:, w], Pb[i % 2][:, w], rs[:, i % 2:i % 2 + 1], None,
                                          ALU.mult).then_inc(p_ready, 1)
                    if kind == "tc":
                        i = TILE_OF[c]
                        k = 4 * (c - CH0[i])
                        nb = min(4, i + 1 - k)
                        dst = (slice(None), slice(k, k + nb), tile(i % 2))
                        lo("tc", u, c, PTl[dst], o[:, 0:128 * nb].rearrange("p (j q) -> p j q", j=nb), PTh[dst])
                    if kind == "xt":
                        d = (slice(None), c // 2, half(c % 2))
                        lo("xt", 0, c, xTl[d], o[:, :], xTh[d])
                    if kind == "qc":
                        dve.wait_ge(done["qc"], c + 1)
                        dve.bn_stats(qst[:, c, :], qcn[:, c, 0:QL]).then_inc(qc_stat, 1)
                        if c == T - 1:
                            dve.wait_ge(qc_stat, T)
                            for t in range(T):
                                ins = dve.bn_aggr(qmv[:, t, :], qst[:, t, :])
                            ins.then_inc(qc_aggr, 1)
                    if kind == "qm":
                        if c == 0:
                            dve.wait_ge(qc_rstd, 1)
                            dve.wait_ge(qc_aggr, 1)
                            for t in range(T):
                                a = (qcn[:, t, 128:QL], qmv[:, t, 0:1], rstd[:, t:t + 1], ALU.subtract, ALU.mult)
                                ins = dve.tensor_scalar(qcn[:, t, QL:256], *a)
                            ins.then_inc(qc_dup, 1)
                            dve.wait_ge(qc_dup, 1)
                            for t in range(T):
                                a = (qcn[:, t, 0:QL], qmv[:, t, 0:1], rstd[:, t:t + 1], ALU.subtract, ALU.mult)
                                ins = dve.tensor_scalar(qcn[:, t, 0:QL], *a)
                            ins.then_inc(qc_norm, 1)
                        dve.wait_ge(done["qm"], c + 1)
                        q = half(c % 2)
                        dst = (qch if c < 2 else qcs)[:, q]
                        dve.tensor_copy(dst, tmp[c % 2][:, :]).then_inc(qm_part, 1)
                        dve.wait_ge(qm_part, c + 1)
                        if c < 2:
                            dve.tensor_tensor(qcl[:, q], tmp[c][:, :], qch[:, q].bitcast(F32),
                                              ALU.subtract).then_inc(qc_split, 1)
                        else:
                            dve.tensor_tensor(qcs[64:128, q], tmp[c % 2][64:128, :], qcs[64:128, q].bitcast(F32),
                                              ALU.subtract).then_inc(qc_split, 1)
                    if kind == "kv":
                        dve.wait_ge(done["kv"], count("kv", u, c))
                        for hh in range(2):
                            ins = dve.bn_stats(bst[:, c, hh, :], kvraw[:, c, hh * HD + ROPE:hh * HD + HD])
                        ins.then_inc(bn_done, 1)
                    if kind == "kvn":
                        hold(dve, bn_done, T * (u + 1))
                        for t in range(T):
                            for hh in range(2):
                                ins = dve.bn_aggr(mv[:, 2 * t + hh, :], bst[:, t, hh, :])
                        ins.then_inc(aggr_done, 1)
                    if kind == "kvn2":
                        dve.wait_ge(rstd_done, u + 1)
                        hh = c // 2
                        for t in range(4 * (c % 2), 4 * (c % 2) + 4):
                            v = kvraw[:, t, hh * HD + ROPE:hh * HD + HD]
                            n = 2 * t + hh
                            ins = dve.tensor_scalar(v, v, mv[:, n, 0:1], rstd[:, n:n + 1], ALU.subtract, ALU.mult)
                        ins.then_inc(kvn_done, 1)
                    if kind == "wb":
                        dve.wait_ge(ready["wb"], 1)
                        dve.tensor_copy(kvbias[:, :], o[:, 0:2]).then_inc(done["wb"], 1)
                    if kind == "kt":
                        lo("kt", u, c, kvTl[:, half(c)], o[:, :], kvTh[:, half(c)])
                    if kind == "v":
                        lo("v", u, c, Vl[:, 4 * c:4 * c + 4, :].rearrange("p t n -> p (t n)"), o[:, :],
                           Vh[:, 4 * c:4 * c + 4, :].rearrange("p t n -> p (t n)"))
                    if kind == "kn":
                        if isinstance(u, int) and u == 0 and c == 0:
                            dve.wait_ge(done["wb"], 1)
                        dve.wait_ge(hi["kn"], count("kn", u, c))
                        dve.scalar_tensor_tensor(KNl[b][:, half(c)], o[:, :], kvbias[:, 0:1], KNh[b][:, half(c)].bitcast(F32),
                                                 ALU.add, ALU.subtract).then_inc(done["kn"], 1)
                    if kind == "qn":
                        lo("qn", u, c, QNl[b][:, half(c)], o[:, :], QNh[b][:, half(c)])
                    if kind == "kp":
                        r = slice(64 * b, 64 * b + 64)
                        lo("kp", u, c, KL[r, half(c)], o[r, :], KD[b][r, half(c)])
                    if kind == "qt":
                        r = slice(64 * (1 - b), 64 * (1 - b) + 64)
                        lo("qt", u, c, QS[b][r, half(c)], o[r, :], QS[b][r, half(c)])
                    if kind == "io":
                        if isinstance(p, int):
                            if p == 0:
                                dve.wait_ge(done["side"], 11)
                            dve.tensor_copy(iocol[:, b:b + 1], ioT[:, p:p + 1]).then_inc(io_ready, 1)
                        else:
                            dve.tensor_copy(iocol[:, b:b + 1], ioT[:, bass.ds(p, 1)]).then_inc(io_ready, 1)
                    if kind == "pv":
                        if c == 0:
                            hold(dve, io_ready, u + 1)
                        dve.wait_ge(hi["pv"], count("pv", u, c))
                        dve.scalar_tensor_tensor(ATl[c % 2][:, :], o[:, 0:256], iocol[:, b:b + 1],
                                                 ATh[c % 2][:, :].bitcast(F32), ALU.add,
                                                 ALU.subtract).then_inc(done["pv"], 1)
                    if kind == "wo":
                        dve.wait_ge(ready["wo"], count("wo", u, c))
                        a = acc[:, 2 * c:2 * c + 2, :].rearrange("p t d -> p (t d)")
                        dve.tensor_tensor(a, o[:, :], a, ALU.add).then_inc(done["wo"], 1)
                    if kind == "side":
                        side(c, o)

            run(numbered(PROLOGUE), 0)
            run(numbered(FIRST), 0)
            with dve.Fori(1, NP - 1) as p:
                run(numbered(MID), p)
            run(numbered(LAST), NP - 1)
            run(EPI, 0)

        block.close()
        stack.pop()
        attn.close()

        mlp(nc, top, SC, J, acc, ident, mhalf, epst, W_up, W_gate, W_down, out)


def mlp(nc, top, SC, J, acc, ident, mhalf, epst, W_up, W_gate, W_down, out):
    def sb(name, shape, dt=F32):
        return top.enter_context(nc.sbuf_tensor(name, shape, dt))

    def sem(name):
        return top.enter_context(nc.semaphore(name))

    ET = E // 128
    raw = [sb(f"raw_{n}", [128, 2048]) for n in range(3)]
    low = sb("low", [128, 2048])
    tern = [sb(f"tern_{n}", [128, 2048]) for n in range(3)]
    ternT = [sb("upT", [128, K, E], F32R), sb("gateT", [128, K, E], F32R), sb("downT", [128, ET, D], F32R)]
    asum = sb("asum", [128, 4])
    onesf = sb("onesf", [128, 128])
    scl = sb("scl", [128, 4])
    thr = sb("thr", [128, 4])
    nthr = sb("nthr", [128, 4])
    hTh, hTl = sb("hTh", [128, K, S], F32R), sb("hTl", [128, K, S], F32R)
    sg = [sb(f"sg{i}", [128, 512]) for i in range(2)]
    tt = [sb(f"tt{i}", [128, 512]) for i in range(2)]
    hid = [sb(f"hid{i}", [128, 512]) for i in range(2)]
    Hh, Hl = sb("Hh", [128, ET, 512], F32R), sb("Hl", [128, ET, 512], F32R)
    st, mvl = sb("st", [128, T, 6]), sb("mvl", [128, T, 2])
    ve, rsd = sb("ve", [128, T]), sb("rsd", [128, T])
    st2, mv2 = sb("st2", [128, T, 6]), sb("mv2", [128, T, 2])
    ve2, rsd2 = sb("ve2", [128, T]), sb("rsd2", [128, T])
    yo = sb("yo", [128, T, D])

    ld = [sem(f"ld_mlp{n}") for n in range(3)]
    ones_ready, abs_done, tot_ready, scl_ready, thr_ready = (sem("ones_ready"), sem("abs_done"), sem("tot_ready"),
                                                             sem("scl_ready"), sem("thr_ready"))
    low_done, tern_ready = sem("low_done"), sem("tern_ready")
    st_done, ag_done, ve_done, rsd_ready, ln_done = (sem("st_done"), sem("ag_done"), sem("ve_done"),
                                                     sem("rsd_ready"), sem("ln_done"))
    wt_ready, wt_done = sem("wt_ready"), sem("wt_done")
    ht_ready, ht_hi, ht_done = sem("ht_ready"), sem("ht_hi"), sem("ht_done")
    ug_ready, sg_done, tt_done, hid_done, hh_done, hl_done = (sem("ug_ready"), sem("sg_done"), sem("tt_done"),
                                                              sem("hid_done"), sem("hh_done"), sem("hl_done"))
    dn_ready, y_done, y_st, y_ag, y_ve, y_rsd, y_ln, stored = (sem("dn_ready"), sem("y_done"), sem("y_st"), sem("y_ag"),
                                                               sem("y_ve"), sem("y_rsd"), sem("y_ln"), sem("stored"))

    def tile(t):
        return slice(128 * t, 128 * t + 128)

    N_W = 3 * 2048 // 512
    W_BANKS = J
    UG = [(SC[0][:, 0:512], SC[0][:, 512:1024]), (SC[1][:, 0:512], SC[1][:, 512:1024])]
    DN = [J[0], J[1]]

    with nc.Block() as blk2:
        @blk2.sync
        def _(sp):
            for n, w in enumerate((W_up, W_gate, W_down)):
                v = w.rearrange("(t p) d -> p t d", p=128)
                sp.dma_start(raw[n][:, :].rearrange("p (t d) -> p t d", t=v.shape[1]), v).then_inc(ld[n], 16)
            for c in range(2):
                sp.wait_ge(y_ln, c + 1)
                sp.dma_start(out[512 * c:512 * c + 512, :].rearrange("(t p) d -> p t d", p=128),
                             yo[:, 4 * c:4 * c + 4, :]).then_inc(stored, 16)
            sp.wait_ge(stored, 32)

        @blk2.gpsimd
        def _(gp):
            gp.memset(asum[:, 3:4], 0.0)
            gp.memset(onesf[:, :], 1.0).then_inc(ones_ready, 1)
            gp.wait_ge(ag_done, 1)
            gp.tensor_tensor(ve[:, :], mvl[:, :, 1], epst[:, 0:T], ALU.add).then_inc(ve_done, 1)
            gp.wait_ge(ve_done, 1)
            gp.tensor_tensor(rsd[:, :], ve[:, :], mhalf[:, 0:T], ALU.pow).then_inc(rsd_ready, 1)
            for c in range(2):
                for e in range(ET):
                    n = c * ET + e
                    gp.wait_ge(hh_done, n + 1)
                    gp.tensor_tensor(Hl[:, e, :], hid[n % 2][:, :], Hh[:, e, :].bitcast(F32),
                                     ALU.subtract).then_inc(hl_done, 1)
                if c == 1:
                    pass
                gp.wait_ge(y_ag, c + 1)
                q = slice(4 * c, 4 * c + 4)
                gp.tensor_tensor(ve2[:, q], mv2[:, q, 1], epst[:, 0:4], ALU.add).then_inc(y_ve, 1)
                gp.wait_ge(y_ve, c + 1)
                gp.tensor_tensor(rsd2[:, q], ve2[:, q], mhalf[:, 0:4], ALU.pow).then_inc(y_rsd, 1)

        @blk2.tensor
        def _(pe):
            mm = pe.matmul
            pe.wait_ge(ones_ready, 1)
            pe.wait_ge(abs_done, 3)
            mm(SC[0][:, 0:4], lhsT=onesf[:, :], rhs=asum[:, :], start=True, stop=True).then_inc(tot_ready, 1)
            pe.wait_ge(ln_done, 1)
            for c in range(4):
                if c >= 2:
                    pe.wait_ge(ht_done, c - 1)
                for t in range(4):
                    last = pe.transpose(UG[1][c % 2][:, tile(t)], acc[:, 4 * (c % 2) + t, tile(c // 2)], ident[:, :])
                last.then_inc(ht_ready, 1)
            for n in range(N_W):
                w, q = n // 4, n % 4
                if q == 0:
                    pe.wait_ge(tern_ready, w + 1)
                if n >= 4:
                    pe.wait_ge(wt_done, n - 3)
                o = W_BANKS[n % 4]
                for m in range(4):
                    if w < 2:
                        src = tern[w][:, D * (4 * (q % 2) + m) + 128 * (q // 2):][:, 0:128]
                    else:
                        src = tern[w][:, E * (m % 2) + 128 * (2 * q + m // 2):][:, 0:128]
                    last = pe.transpose(o[:, tile(m)], src, ident[:, :])
                last.then_inc(wt_ready, 1)
            pe.wait_ge(wt_done, N_W)
            pe.wait_ge(ht_done, 4)
            for c in range(2):
                tok = slice(512 * c, 512 * c + 512)
                for e in range(ET):
                    n = c * ET + e
                    if n >= 2:
                        pe.wait_ge(hid_done, n - 1)
                    for w in range(2):
                        for k in range(K):
                            mm(UG[n % 2][w], lhsT=ternT[w][:, k, tile(e)], rhs=hTh[:, k, tok], start=k == 0, stop=False)
                            last = mm(UG[n % 2][w], lhsT=ternT[w][:, k, tile(e)], rhs=hTl[:, k, tok], start=False,
                                      stop=k == K - 1)
                    last.then_inc(ug_ready, 1)
                pe.wait_ge(hl_done, ET * (c + 1))
                for t in range(4):
                    if c == 1 and t % 2 == 0:
                        pe.wait_ge(y_done, t // 2 + 1)
                    for e in range(ET):
                        o = DN[t // 2][:, 256 * (t % 2):256 * (t % 2) + 256]
                        mm(o, lhsT=Hh[:, e, tile(t)], rhs=ternT[2][:, e, :], start=e == 0, stop=False)
                        last = mm(o, lhsT=Hl[:, e, tile(t)], rhs=ternT[2][:, e, :], start=False, stop=e == ET - 1)
                    if t % 2 == 1:
                        last.then_inc(dn_ready, 1)

        @blk2.scalar
        def _(act):
            for n in range(3):
                act.wait_ge(ld[n], 16)
                act.activation(tern[n][:, :], raw[n][:, :], ACT.Abs, accum_out=asum[:, n:n + 1]).then_inc(abs_done, 1)
            for c in range(4):
                act.wait_ge(ht_ready, c + 1)
                act.activation(hTh[:, c // 2, 512 * (c % 2):512 * (c % 2) + 512], UG[1][c % 2], ACT.Copy).then_inc(ht_hi, 1)
            for n in range(N_W):
                w, q = n // 4, n % 4
                act.wait_ge(wt_ready, n + 1)
                o = W_BANKS[n % 4]
                if w < 2:
                    dst = ternT[w][:, q // 2, 512 * (q % 2):512 * (q % 2) + 512]
                else:
                    dst = ternT[2][:, 2 * q:2 * q + 2, :].rearrange("p e d -> p (e d)")
                act.activation(dst, o[:, :], ACT.Copy).then_inc(wt_done, 1)
            for c in range(2):
                for e in range(ET):
                    n = c * ET + e
                    act.wait_ge(ug_ready, n + 1)
                    act.wait_ge(scl_ready, 1)
                    if n >= 2:
                        act.wait_ge(tt_done, n - 1)
                    act.activation(sg[n % 2][:, :], UG[n % 2][0], ACT.Sigmoid, scale=scl[:, 0:1]).then_inc(sg_done, 1)
                    act.wait_ge(hid_done, n + 1)
                    if c == 1 and e == 0:
                        act.wait_ge(dn_ready, 2)
                    act.activation(Hh[:, e, :], hid[n % 2][:, :], ACT.Copy).then_inc(hh_done, 1)

        @blk2.vector
        def _(dve):
            for t in range(T):
                dve.bn_stats(st[:, t, :], acc[:, t, :]).then_inc(st_done, 1)
            dve.wait_ge(st_done, T)
            for t in range(T):
                ins = dve.bn_aggr(mvl[:, t, :], st[:, t, :])
            ins.then_inc(ag_done, 1)
            dve.wait_ge(rsd_ready, 1)
            dve.wait_ge(ag_done, 1)
            for t in range(T):
                ins = dve.tensor_scalar(acc[:, t, :], acc[:, t, :], mvl[:, t, 0:1], rsd[:, t:t + 1], ALU.subtract, ALU.mult)
            ins.then_inc(ln_done, 1)
            dve.wait_ge(tot_ready, 1)
            dve.tensor_scalar(scl[:, :], SC[0][:, 0:4], 1.0 / (D * E), 1e-8, ALU.mult, ALU.add).then_inc(scl_ready, 1)
            dve.wait_ge(scl_ready, 1)
            dve.tensor_scalar(thr[:, :], scl[:, :], 0.5, None, ALU.mult)
            dve.tensor_scalar(nthr[:, :], scl[:, :], -0.5, None, ALU.mult).then_inc(thr_ready, 1)
            dve.wait_ge(thr_ready, 1)
            dve.wait_ge(abs_done, 3)
            for n in range(3):
                if n:
                    dve.wait_ge(tern_ready, n)
                dve.tensor_scalar(low[:, :], raw[n][:, :], nthr[:, n:n + 1], None, ALU.is_lt).then_inc(low_done, 1)
                dve.wait_ge(low_done, n + 1)
                dve.scalar_tensor_tensor(tern[n][:, :], raw[n][:, :], thr[:, n:n + 1], low[:, :], ALU.is_gt,
                                         ALU.subtract).then_inc(tern_ready, 1)
                if n == 0:
                    for c in range(4):
                        dve.wait_ge(ht_hi, c + 1)
                        d = (slice(None), c // 2, slice(512 * (c % 2), 512 * (c % 2) + 512))
                        dve.tensor_tensor(hTl[d], UG[1][c % 2], hTh[d].bitcast(F32), ALU.subtract).then_inc(ht_done, 1)
            for c in range(2):
                for e in range(ET):
                    n = c * ET + e
                    dve.wait_ge(sg_done, n + 1)
                    dve.scalar_tensor_tensor(tt[n % 2][:, :], UG[n % 2][0], scl[:, 0:1], sg[n % 2][:, :], ALU.mult,
                                             ALU.mult).then_inc(tt_done, 1)
                    dve.wait_ge(tt_done, n + 1)
                    if n >= 2:
                        dve.wait_ge(hl_done, n - 1)
                    dve.scalar_tensor_tensor(hid[n % 2][:, :], UG[n % 2][1], scl[:, 1:2], tt[n % 2][:, :], ALU.mult,
                                             ALU.mult).then_inc(hid_done, 1)
                for i in range(2):
                    t0 = 4 * c + 2 * i
                    dve.wait_ge(dn_ready, 2 * c + i + 1)
                    a = acc[:, t0:t0 + 2, :].rearrange("p t d -> p (t d)")
                    y = yo[:, t0:t0 + 2, :].rearrange("p t d -> p (t d)")
                    dve.scalar_tensor_tensor(y, DN[i][:, :], scl[:, 2:3], a, ALU.mult, ALU.add).then_inc(y_done, 1)
                dve.wait_ge(y_done, 2 * c + 2)
                for t in range(4 * c, 4 * c + 4):
                    dve.bn_stats(st2[:, t, :], yo[:, t, :]).then_inc(y_st, 1)
                dve.wait_ge(y_st, 4 * c + 4)
                for t in range(4 * c, 4 * c + 4):
                    ins = dve.bn_aggr(mv2[:, t, :], st2[:, t, :])
                ins.then_inc(y_ag, 1)
                dve.wait_ge(y_rsd, c + 1)
                dve.wait_ge(y_ag, c + 1)
                for t in range(4 * c, 4 * c + 4):
                    ins = dve.tensor_scalar(yo[:, t, :], yo[:, t, :], mv2[:, t, 0:1], rsd2[:, t:t + 1], ALU.subtract,
                                            ALU.mult)
                ins.then_inc(y_ln, 1)


INPUTS = ["L0_attn_x", "L0_attn_W_cq", "L0_attn_q_norm_w", "L0_attn_q_norm_b", "L0_attn_W_q", "L0_attn_W_ckv",
          "L0_attn_kv_norm_w", "L0_attn_kv_norm_b", "L0_attn_W_kv", "L0_attn_W_o", "L0_attn_W_ip", "L0_attn_W_ig",
          "L0_attn_W_sq", "L0_attn_W_sk", "L0_attn_W_sv", "L0_attn_W_io", "L0_ffn_W_up", "L0_ffn_W_gate",
          "L0_ffn_W_down"]


def constants():
    import numpy as np
    freqs = (1.0 / np.power(np.float32(10000.0), np.arange(0, ROPE, 2, dtype=np.float32) / np.float32(ROPE))).astype(np.float32)
    f = np.outer(np.arange(S, dtype=np.float32), freqs).astype(np.float32)
    cos, sin = np.cos(f).astype(np.float32), np.sin(f).astype(np.float32)
    col = np.arange(64)
    return {
        "c_ident": np.eye(128, dtype=np.float32),
        "c_cos": np.repeat(cos, 2, axis=1),
        "c_sin": np.stack([-sin, sin], axis=-1).reshape(S, ROPE),
        "c_tok": (np.arange(128)[:, None] + 128 * np.arange(T)[None, :]).astype(np.float32),
        "c_blk": (np.arange(8)[:, None] == col[None, :] // TOPK).astype(np.float32),
        "c_off": np.where(col[:, None] // TOPK == col[None, :] // TOPK, 0.0, -1e30).astype(np.float32),
        "c_mean": ((col[:, None] // TOPK == np.arange(8)[None, :]) / TOPK).astype(np.float32),
    }


def kernel(**inputs):
    import numpy as np
    import concourse.bacc as bacc
    from concourse.bass_utils import run_bass_kernel_spmd

    nc = bacc.Bacc("TRN2", target_bir_lowering=False, num_devices=1)
    arrays, args = {}, []
    for name in INPUTS:
        a = np.ascontiguousarray(inputs[name])
        if name == "L0_attn_x":
            a = a.reshape(S, D)
        arrays[f"in_{name}"] = a
    for name, a in constants().items():
        arrays[f"in_{name}"] = np.ascontiguousarray(a)
    for name, a in arrays.items():
        args.append(nc.dram_tensor(name, a.shape, mybir.dt.from_np(a.dtype), kind="ExternalInput").ap())
    args.append(nc.dram_tensor("out", (S, D), F32, kind="ExternalOutput").ap())
    attention_and_mlp(nc, *args)
    r = run_bass_kernel_spmd(nc, [arrays], core_ids=[0])
    return r.results[0]["out"].reshape(1, S, D)
```

```python
import concourse.bass as bass
from concourse import mybir
from contextlib import ExitStack

F32 = mybir.dt.float32
F32R = mybir.dt.float32r
BF16 = mybir.dt.bfloat16
U32 = mybir.dt.uint32
ALU = mybir.AluOpType
ACT = mybir.ActivationFunctionType
AX = mybir.AxisListType

S = 1024
D = 256
NH = 16
NP = NH // 2
NOPE = 128
ROPE = 64
HD = NOPE + ROPE
QL = 192
IH = 8
TOPK = 8
E = 1024
T = S // 128
K = D // 128
QLT = QL - 128
SCALE = float(HD) ** -0.5
SCALE_SIDE = float(128) ** -0.5
EPS = 1e-5
LOW = -3.0e38
NB = 4

CHUNKS = [(i + 4) // 4 for i in range(T)]
CH0 = [sum(CHUNKS[:i]) for i in range(T + 1)]
NCH = CH0[T]
TILE_OF = [i for i in range(T) for _ in range(CHUNKS[i])]


def attention_and_mlp(nc, x, W_cq, q_norm_w, q_norm_b, W_q, W_ckv, kv_norm_w, kv_norm_b, W_kv, W_o,
                      W_ip, W_ig, W_sq, W_sk, W_sv, W_io, W_up, W_gate, W_down,
                      c_ident, c_cos, c_sin, c_tok, c_blk, c_off, c_mean, out):
    top = ExitStack()
    with top:
        stack = [top]

        def sb(name, shape, dt=F32):
            return stack[-1].enter_context(nc.sbuf_tensor(name, shape, dt))

        def sem(name):
            return top.enter_context(nc.semaphore(name))

        SC = [top.enter_context(nc.psum_tensor(f"SC{i}", [128, 1024], F32)) for i in range(2)]
        J = [top.enter_context(nc.psum_tensor(f"J{i}", [128, 512], F32)) for i in range(NB)]

        acc = sb("acc", [128, T, D])
        ident = sb("ident", [128, 128])
        mhalf = sb("mhalf", [128, 16])
        epst = sb("epst", [128, 16])
        xTh, xTl = sb("xTh", [128, K, S], F32R), sb("xTl", [128, K, S], F32R)
        KNh, KNl = [sb("KNh0", [128, S], F32R)], [sb("KNl0", [128, S], F32R)]
        QNh, QNl = [sb("QNh0", [128, S], F32R)], [sb("QNl0", [128, S], F32R)]
        QS = [sb("QS0", [128, S], F32R)]
        KD = [sb("KD0", [128, S], F32R)]
        asum = sb("asum", [128, 6])
        onesf = sb("onesf", [128, 128])
        scl, thr, nthr = sb("scl", [128, 3]), sb("thr", [128, 3]), sb("nthr", [128, 3])
        st, mvl = sb("st", [128, T, 6]), sb("mvl", [128, T, 2])
        ve, rsd = sb("ve", [128, T]), sb("rsd", [128, T])
        held = sem("held")

        def wait(eng, s, v):
            if isinstance(v, int) and v <= 0:
                return
            eng.wait_ge(s, v)

        def hold(eng, s, v):
            wait(eng, s, v)
            eng.sem_inc(held, 1)

        attn = ExitStack()
        stack.append(attn)
        qch, qcl = sb("qch", [128, S], F32R), sb("qcl", [128, S], F32R)
        qcs = sb("qcs", [128, S], F32R)
        mask = sb("mask", [128, S], BF16)
        cos2, sin2 = sb("cos2", [128, T, ROPE]), sb("sin2", [128, T, ROPE])
        kvw, kvb = sb("kvw", [128, 1]), sb("kvb", [128, 1])
        Wkh, Wkl = sb("Wkh", [128, 2 * NOPE], F32R), sb("Wkl", [128, 2 * NOPE], F32R)
        kvbias = sb("kvbias", [128, 2])
        ioT = sb("ioT", [128, IH])
        iobh, iobl = sb("iobh", [128, 128], F32R), sb("iobl", [128, 128], F32R)
        row = sb("row", [128, D])
        r_kv = sb("r_kv", [128, K, 2 * HD])
        Wckh, Wckl = sb("Wckh", [128, K, 2 * HD], F32R), sb("Wckl", [128, K, 2 * HD], F32R)
        r_qp = sb("r_qp", [128, 2, 2, ROPE])
        Wqph, Wqpl = sb("Wqph", [128, 2, 2, ROPE], F32R), sb("Wqpl", [128, 2, 2, ROPE], F32R)
        r_qn = sb("r_qn", [128, 2, NOPE])
        Wqnh = [sb(f"Wqnh{b}", [128, 2, NOPE], F32R) for b in range(2)]
        Wqnl = [sb(f"Wqnl{b}", [128, 2, NOPE], F32R) for b in range(2)]
        r_o = sb("r_o", [128, D])
        Woh = [sb(f"Woh{b}", [128, D], F32R) for b in range(2)]
        Wol = [sb(f"Wol{b}", [128, D], F32R) for b in range(2)]
        kvraw = sb("kvraw", [128, T, 2 * HD])
        qraw = sb("qraw", [128, T, 2, ROPE])
        ropes = sb("ropes", [128, T, 2, ROPE])
        Rk = sb("Rk", [128, T, 2, 2, ROPE])
        Rq = sb("Rq", [128, T, 2, 2, ROPE])
        bst = sb("bst", [128, T, 2, 6])
        mv = sb("mv", [128, 2 * T, 2])
        veps = sb("veps", [128, 2 * T])
        rstd = sb("rstd", [128, 2 * T])
        kvTh, kvTl = sb("kvTh", [128, S], F32R), sb("kvTl", [128, S], F32R)
        KNh.append(sb("KNh1", [128, S], F32R))
        KNl.append(sb("KNl1", [128, S], F32R))
        QNh.append(sb("QNh1", [128, S], F32R))
        QNl.append(sb("QNl1", [128, S], F32R))
        QS.append(sb("QS1", [128, S], F32R))
        KD.append(sb("KD1", [128, S], F32R))
        KL = sb("KL", [128, S], F32R)
        Vh, Vl = sb("Vh", [128, T, NOPE], F32R), sb("Vl", [128, T, NOPE], F32R)
        lows = ropes[:, :, :, :].rearrange("p t h n -> p (t h n)").rearrange("p (c n) -> p c n", c=2)
        low = [lows[:, c, :] for c in range(2)]
        raw = [kvraw[:, :, 0:D], Rk[:, :, :, :, :].rearrange("p t h a d -> p t (h a d)"),
               Rq[:, :, :, :, :].rearrange("p t h a d -> p (t h a d)").rearrange("p (k e) -> p k e", k=K)]
        junk = qraw[:, :, :, :].rearrange("p t h n -> p (t h n)")
        mx = sb("mx", [128, 2])
        nm = sb("nm", [128, 2])
        sm, rs = sb("sm", [128, 2, T]), sb("rs", [128, 2, T])
        Pb = [sb(f"Pb{i}", [128, S]) for i in range(2)]
        PTh, PTl = sb("PTh", [128, T, 256], F32R), sb("PTl", [128, T, 256], F32R)
        ATh = [sb(f"ATh{i}", [128, 256], F32R) for i in range(2)]
        ATl = [sb(f"ATl{i}", [128, 256], F32R) for i in range(2)]

        wip = Rq[:, :, :, :, :].rearrange("p t h a d -> p (t h a d)").rearrange("p (k n) -> p k n", k=K)
        r_cq = Pb[0][:, 0:400].rearrange("p (k n) -> p k n", k=K)
        r_wkv = Pb[0][:, 512:768]
        s_wkv = ropes[:, 0:2, :, :].rearrange("p t h n -> p (t h n)")
        Wcqh = KNh[1][:, 0:400].rearrange("p (k n) -> p k n", k=K)
        Wcql = KNl[1][:, 0:400].rearrange("p (k n) -> p k n", k=K)
        qcm = sb("qcm", [128, T, 128])
        qct = qraw[:, :, :, :].rearrange("p t h n -> p t (h n)")
        gts = Pb[0][:, 768:768 + 64].rearrange("p (t h) -> p t h", t=T)
        qst = Pb[0][:, 832:832 + 48].rearrange("p (t s) -> p t s", t=T)
        qmv = Pb[0][:, 880:896].rearrange("p (t s) -> p t s", t=T)
        wside = Pb[1][:, 0:512].rearrange("p (k n) -> p k n", k=4)
        qnwb = sb("qnwb", [128, 4])
        gT = qraw[0:8, :, :, :].rearrange("p t h n -> p (t h n)")
        m8 = sb("m8", [8, 8])
        i8 = sb("i8", [8, 8], U32)
        i8f = sb("i8f", [8, 8])
        i8d = sb("i8d", [8, 64])
        ones8 = onesf[0:8, :]
        blk = sb("blk", [8, 64])
        tokid = sb("tokid", [128, T])
        off64 = sb("off64", [64, 64])
        mean8 = sb("mean8", [64, 8])
        idxb = Pb[0][:, 400:464]
        oneh = Pb[1][:, 512:1024].rearrange("p (t n) -> p t n", t=T)
        selT = Pb[0][:, 896:1024].rearrange("p (k n) -> p k n", k=K)
        istT, sqT, skT = Pb[0][:, 0:64], Pb[0][:, 64:128], Pb[0][:, 128:192]
        svs = Pb[0][0:64, 192:320]
        sp_s = Pb[0][0:64, 320:384]
        smx = sb("smx", [64, 4])
        pms = sb("pms", [64, 8])
        soT = sb("soT", [128, 8])

        ld_x, ld_c, ld_w0, ld_side = sem("ld_x"), sem("ld_c"), sem("ld_w0"), sem("ld_side")
        ld_kv, ld_qp, ld_qn, ld_o = sem("ld_kv"), sem("ld_qp"), sem("ld_qn"), sem("ld_o")
        const_ready = sem("const_ready")
        hi_w, w0_ready = sem("hi_w"), sem("w0_ready")
        wkv_hi, wkv_ready = sem("wkv_hi"), sem("wkv_ready")
        wqp_hi, wqp_ready = sem("wqp_hi"), sem("wqp_ready")
        wqn_hi, wqn_ready = sem("wqn_hi"), sem("wqn_ready")
        wo_hi, wo_split = sem("wo_hi"), sem("wo_split")
        ready = {k: sem(f"{k}_ready") for k in
                 ("xt", "qc", "qm", "kv", "qp", "kt", "kp", "qt", "kn", "qn", "v", "pv", "wo", "side", "tc", "wb",
                  "rw", "wtot", "wt", "ht")}
        hi = {k: sem(f"{k}_hi") for k in ("xt", "kt", "kp", "qt", "kn", "qn", "v", "pv", "tc", "ht",
                                        "qc", "qm")}
        done = {k: sem(f"{k}_done") for k in
                ("xt", "qc", "qm", "kv", "qp", "kt", "kp", "qt", "kn", "qn", "v", "pv", "wo", "side", "tc",
                 "wb", "rw", "wtot", "wt", "ht")}
        ld_mlp = [sem(f"ld_mlp{n}") for n in range(3)]
        tot_done = sem("tot_done")
        abs_done, scl_ready, thr_ready, low_done, tern_done = (sem("abs_done"), sem("scl_ready"), sem("thr_ready"),
                                                               sem("low_done"), sem("tern_done"))
        ln_st, ln_ag, ln_ve, ln_rsd, ln_done = sem("ln_st"), sem("ln_ag"), sem("ln_ve"), sem("ln_rsd"), sem("ln_done")
        qc_aggr, qc_veps, qc_rstd, qc_norm = (sem("qc_aggr"), sem("qc_veps"),
                                                       sem("qc_rstd"), sem("qc_norm"))
        qm_scaled = sem("qm_scaled")
        bn_done, aggr_done, veps_done, rstd_done, kvn_done = (sem("bn_done"), sem("aggr_done"),
                                                              sem("veps_done"), sem("rstd_done"),
                                                              sem("kvn_done"))
        rk_mul, rk_ready = sem("rk_mul"), sem("rk_ready")
        rq_mul, rq_ready = sem("rq_mul"), sem("rq_ready")
        wkv_scaled = sem("wkv_scaled")
        sc_ready = sem("sc_ready")
        mx_ready, nm_ready = sem("mx_ready"), sem("nm_ready")
        exp_done = sem("exp_done")
        rs_ready = sem("rs_ready")
        tp_ready, pt_lo = ready["tc"], done["tc"]
        io_hi, io_ready = sem("io_hi"), sem("io_ready")
        row_added = sem("row_added")
        side_dve = sem("side_dve")
        side_exp = sem("side_exp")

        PER = {"xt": 4, "qc": T, "qm": 4, "kv": T, "qp": 2, "kt": 2, "kp": 2, "qt": 2, "kn": 2, "qn": 2,
               "v": 2, "pv": 4, "wo": 4, "side": 11, "tc": NCH, "wb": 1, "rw": 1, "wtot": 3, "wt": 12, "ht": 2}

        def count(kind, unit, c):
            return PER[kind] * unit + c + 1

        PAIR_KINDS = ("io", "rw", "kv", "qp", "kvn", "kvn2", "ropek", "ropeq", "wkv", "wqp")

        def unit(kind, off, p):
            if kind in ("wtot", "wt", "ht"):
                return off
            return p + off if kind in PAIR_KINDS else 2 * p + off

        def t(h, i):
            return [("tc", h, n) for n in range(CH0[i], CH0[i + 1])]

        def head_steps(b, first, last):
            h, n, m = b, b + 1, b - 1
            tail = not (first and b == 0)
            more = not last
            slots = [[] for _ in range(T)]

            def add(i, cond, *steps):
                if cond:
                    slots[i].extend(steps)

            def mlp_steps():
                if b == 0:
                    add(2, True, ("wld", 0, 0))
                    add(4, True, ("wld", 0, 1), ("wabs", 0, 0))
                    add(5, True, ("wabs", 0, 1))
                    add(6, True, ("wtot", 0, 0), ("wld", 0, 2), ("tern", 0, 0), ("wabs", 0, 2))
                    add(7, True, ("tern", 0, 1), ("wabs", 0, 3))
                else:
                    add(0, True, ("wtot", 0, 1), ("tern", 0, 2))
                    add(1, True, ("tern", 0, 3), ("wabs", 0, 4))
                    add(2, True, ("wt", 0, 0), ("tern", 0, 4), ("wabs", 0, 5))
                    add(3, True, ("rowadd", 0, 0), ("rowadd", 0, 1), ("wt", 0, 1), ("wt", 0, 2), ("tern", 0, 5), ("tern", 0, 6))
                    add(4, True, ("wtot", 0, 2), ("wt", 0, 3), ("tern", 0, 7), ("rowadd", 0, 2), ("rowadd", 0, 3))
                    add(5, True, ("wt", 0, 4), ("tern", 0, 8), ("ln1", 0, 0))
                    add(6, True, ("wt", 0, 5), ("tern", 0, 9), ("ln1n", 0, 0), ("ln1", 0, 1))
                    add(7, True, ("wt", 0, 6), ("wt", 0, 7), ("tern", 0, 10), ("tern", 0, 11), ("ln1n", 0, 1))

            add(0, tail, *t(m, 7), ("wo", m, 2))
            add(1, tail, ("pv", m, 3))
            add(1, True, *t(h, 0), ("v", h, 0), ("v", h, 1))
            if b == 0:
                add(0, True, ("qn", n, 0), ("kvn2", 0, 2))
                add(0, more, ("wkv", 1, 0))
                add(1, True, ("kvn2", 0, 3))
                add(2, True, *t(h, 1))
                add(2, tail, ("wo", m, 3))
                add(2, True, ("io", 0, 0), ("qn", n, 1), ("kt", n, 0), ("kt", n, 1))
                add(3, True, ("kp", n, 0), ("pv", h, 0), *t(h, 2), ("kn", n, 0), ("wosp", n, 0))
                add(4, True, ("kp", n, 1), *t(h, 3), ("wo", h, 0), ("kn", n, 1))
                add(4, more, ("kv", 1, 0), ("wqp", 1, 0))
                add(5, more, ("kv", 1, 1))
                add(5, True, ("pv", h, 1), *t(h, 4), ("qt", n, 0))
                add(5, more, ("kv", 1, 2), ("wqn", h + 2, 0))
                add(6, more, ("kv", 1, 3))
                add(6, True, *t(h, 5), ("wo", h, 1), ("qt", n, 1))
                add(6, more, ("kv", 1, 4), ("kv", 1, 5))
                add(7, more, ("kv", 1, 6), ("kv", 1, 7))
                add(7, True, ("pv", h, 2), *t(h, 6))
            else:
                add(0, more, ("qp", 1, 0), ("kvn", 1, 0), ("ropek", 1, 0))
                add(1, more, ("qn", n, 0), ("kvn2", 1, 0))
                add(2, True, *t(h, 1), ("rw", 0, 0), ("wo", m, 3))
                add(2, more, ("qp", 1, 1), ("kvn2", 1, 1), ("ropek", 1, 1))
                add(3, more, ("kt", n, 0))
                add(3, True, ("pv", h, 0), *t(h, 2))
                add(3, more, ("kt", n, 1), ("ropeq", 1, 0))
                add(4, more, ("kn", n, 0))
                add(4, True, *t(h, 3), ("wo", h, 0))
                add(4, more, ("kn", n, 1), ("ropeq", 1, 1), ("wosp", n, 0))
                add(5, more, ("kp", n, 0))
                add(5, True, ("pv", h, 1), *t(h, 4))
                add(5, more, ("kp", n, 1), ("wqn", h + 2, 0))
                add(6, more, ("qn", n, 1))
                add(6, True, *t(h, 5), ("wo", h, 1))
                add(6, more, ("qt", n, 0))
                add(7, more, ("qt", n, 1))
                add(7, True, ("pv", h, 2), *t(h, 6))
            if last:
                mlp_steps()
            exp_at = [[2, 2, 2, 2, 2, 2, 2, 2], [2, 2, 2, 2, 2, 2, 2, 2]]
            s = []
            for i in range(T):
                e = min(exp_at[b][i], len(slots[i]))
                s += [("qk", h, i), *slots[i][:e], ("exp", h, i), *slots[i][e:]]
            return s

        def pair_steps(first=False, last=False):
            return head_steps(0, first, last) + head_steps(1, first, last)

        SIDE = [("side", 0, c) for c in range(11)]
        def each(kind, *cs):
            return [(kind, 0, c) for c in cs]

        PROLOGUE = (each("xt", 0, 1, 2, 3) + each("wkv", 0) + each("wqp", 0) + each("wqn", 0) + each("qc", *range(T)) +
                    each("qrs", 0) + each("kv", 0, 1) + each("wb", 0) + each("kv", 2, 3) + each("ropek", 0) +
                    each("qnorm", 0) + each("kv", 4, 5, 6, 7) + each("kvn", 0) + each("ropek", 1) +
                    each("qm", 0, 1, 2, 3) + each("side", 0, 1) + each("kvn2", 0, 1) + each("qn", 0, 1) + each("qp", 0) + each("kt", 0, 1) +
                    each("side", 2) + each("qp", 1) + each("kn", 0, 1) + each("kp", 0) +
                    each("side", 3) + each("kp", 1) + each("side", 4, 5) + each("ropeq", 0) +
                    each("side", 6, 7) + each("ropeq", 1) + each("side", 8) + each("qt", 0) + each("side", 9) +
                    each("qt", 1) + each("side", 10) +
                    each("wosp", 0) + [("wqn", 1, 0)])
        EPILOGUE = [*t(NH - 1, 7), ("ht", 0, 0), ("wo", NH - 1, 2), ("wt", 0, 8), ("wt", 0, 9), ("pv", NH - 1, 3),
                    ("ht", 0, 1), ("wt", 0, 10), ("wt", 0, 11), ("wo", NH - 1, 3)]

        BANKED = tuple(PER)

        def banked(steps):
            return [s for s in steps if s[0] in BANKED or s[0] == "skip"]

        FIRST, MID, LAST = pair_steps(first=True), pair_steps(), pair_steps(last=True)
        PROLOGUE += [("skip", 0, 0)] * (-len(banked(PROLOGUE)) % NB)
        fill = [("skip", 0, 0)] * (-len(banked(MID)) % NB)
        MID += fill
        FIRST += fill
        FIRST[0:0] = [("skip", 0, 0)] * (-len(banked(FIRST)) % NB)
        BANKED_ALL = BANKED + ("skip",)

        def numbered(steps, start=0):
            n, res = start, []
            for s in steps:
                if s[0] in BANKED_ALL:
                    res.append((*s, n % NB))
                    n += 1
                else:
                    res.append((*s, None))
            return res

        EPI = numbered(EPILOGUE, len(banked(LAST)))

        def half(c):
            return slice(512 * c, 512 * c + 512)

        def tile(t):
            return slice(128 * t, 128 * t + 128)

        block = top.enter_context(ExitStack())
        blk1 = block.enter_context(nc.Block())

        @blk1.sync
        def _(sp):
            sp.dma_start(acc[:, :, :], x.rearrange("(t p) d -> p t d", p=128)).then_inc(ld_x, 16)
            sp.dma_start(ident[:, :], c_ident).then_inc(ld_x, 16)
            cq = W_cq.rearrange("(k p) n -> p k n", p=128)
            sp.dma_start(r_cq[:, :, 0:QL], cq).then_inc(ld_w0, 16)
            sp.dma_start(r_cq[:, :, QL:QL + IH], W_ig.rearrange("(k p) n -> p k n", p=128)).then_inc(ld_w0, 16)
            sp.dma_start(r_wkv, W_kv).then_inc(ld_w0, 16)
            sp.dma_start(kvw[:, :], kv_norm_w.rearrange("(p a) -> p a", a=1)).then_inc(ld_w0, 16)
            sp.dma_start(kvb[:, :], kv_norm_b.rearrange("(p a) -> p a", a=1)).then_inc(ld_w0, 16)

            ckv = W_ckv.rearrange("(k p) n -> p k n", p=128)
            wq2 = W_q.rearrange("r (h n) -> r h n", n=HD)

            def load(kind, u):
                if kind == "wkv":
                    wait(sp, wkv_ready, u)
                    sp.dma_start(r_kv[:, :, :], ckv[:, :, bass.ds(u * (2 * HD), 2 * HD)]).then_inc(ld_kv, 16)
                if kind == "wqp":
                    wait(sp, wqp_ready, u)
                    cols = wq2[:, bass.ds(u * 2, 2), NOPE:HD]
                    sp.dma_start(r_qp[:, 0, :, :], cols[0:128]).then_inc(ld_qp, 16)
                    for r in range(2):
                        sp.dma_start(r_qp[64 * r:64 * r + 64, 1, :, :], cols[128:QL]).then_inc(ld_qp, 16)
                if kind == "wqn":
                    wait(sp, wqn_ready, u)
                    cols = W_q[:, bass.ds(u * HD, NOPE)]
                    sp.dma_start(r_qn[:, 0, :], cols[0:128]).then_inc(ld_qn, 16)
                    for r in range(2):
                        sp.dma_start(r_qn[64 * r:64 * r + 64, 1, :], cols[128:QL]).then_inc(ld_qn, 16)
                if kind == "wosp":
                    wait(sp, wo_split, u)
                    sp.dma_start(r_o[:, :], W_o[bass.ds(u * NOPE, NOPE), :]).then_inc(ld_o, 16)

            for kind in ("wkv", "wqp", "wqn", "wosp"):
                load(kind, 0)
            sp.dma_start(qnwb[:, 0:1], q_norm_w[0:128].rearrange("(p a) -> p a", a=1)).then_inc(ld_c, 16)
            sp.dma_start(qnwb[:, 1:2], q_norm_b[0:128].rearrange("(p a) -> p a", a=1)).then_inc(ld_c, 16)
            for r in range(2):
                rows = slice(64 * r, 64 * r + 64)
                sp.dma_start(qnwb[rows, 2:3], q_norm_w[128:QL].rearrange("(p a) -> p a", a=1)).then_inc(ld_c, 16)
                sp.dma_start(qnwb[rows, 3:4], q_norm_b[128:QL].rearrange("(p a) -> p a", a=1)).then_inc(ld_c, 16)
            sp.dma_start(cos2[:, :, :], c_cos.rearrange("(t p) d -> p t d", p=128)).then_inc(ld_c, 16)
            sp.dma_start(sin2[:, :, :], c_sin.rearrange("(t p) d -> p t d", p=128)).then_inc(ld_c, 16)
            for dst, src in ((blk[:, :], c_blk), (tokid[:, :], c_tok), (off64[:, :], c_off), (mean8[:, :], c_mean),
                             (wip, W_ip.rearrange("(k p) n -> p k n", p=128)), (wside[:, 0, :], W_sq),
                             (wside[:, 1, :], W_sk), (wside[:, 2, :], W_sv), (wside[:, 3, :], W_io[:, 0:128])):
                sp.dma_start(dst, src).then_inc(ld_side, 16)
            load("wqn", 1)

            def run(steps, p):
                for kind, off, c in steps:
                    if kind in ("wkv", "wqp", "wqn", "wosp"):
                        load(kind, unit(kind, off, p))
                    if kind == "wld":
                        src = (W_up, W_gate, W_down)[c]
                        over = ("kt", "kp", "qt")[c]
                        sp.wait_ge(ready[over], PER[over] * NH)
                        sp.dma_start(raw[c], src.rearrange("(t p) d -> p t d", p=128)).then_inc(ld_mlp[c], 16)

            run(FIRST, 0)
            with sp.Fori(1, NP - 1) as p:
                run(MID, p)
            run(LAST, NP - 1)

        LD_C, LD_SIDE, LD_W0 = 16 * 8, 16 * 9, 16 * 5

        def rope(eng, src, dst, mul, rdy, u, c, waits):
            for w in waits:
                hold(eng, *w)
            t = slice(4 * c, 4 * c + 4)
            src = src[:, t]
            cosb = cos2[:, t, :].rearrange("p t (a d) -> p t a d", a=1).to_broadcast([128, 4, 2, ROPE])
            for e in range(2):
                s = sin2[:, t, e::2].rearrange("p t (a d) -> p t a d", a=1).to_broadcast([128, 4, 2, ROPE // 2])
                ins = eng.tensor_tensor(ropes[:, t, :, e::2], src[:, :, :, 1 - e::2], s, ALU.mult)
            ins.then_inc(mul, 1)
            eng.wait_ge(mul, 4 * u + 2 * c + 1)
            eng.tensor_tensor(src, src, cosb, ALU.mult).then_inc(mul, 1)
            eng.wait_ge(mul, 4 * u + 2 * c + 2)
            for hh in range(2):
                a = src[:, :, hh, :].rearrange("p t (a d) -> p t a d", a=1).to_broadcast([128, 4, 2, ROPE])
                b = ropes[:, t, hh, :].rearrange("p t (a d) -> p t a d", a=1).to_broadcast([128, 4, 2, ROPE])
                ins = eng.tensor_tensor(dst[:, t, hh, :, :], a, b, ALU.add)
            ins.then_inc(rdy, 1)

        def rope_q(eng, u, c):
            start = isinstance(u, int) and u == 0
            waits = [(done["qp"], 2 * u + c + 1), (done["side"], 5) if start else (ready["qt"], 4 * u)]
            rope(eng, qraw[:, :, :, :], Rq, rq_mul, rq_ready, u, c, waits + [(rk_ready, 2 * u + 2)])

        @blk1.gpsimd
        def _(gp):
            gp.memset(mhalf[:, :], -0.5)
            gp.memset(epst[:, :], EPS)
            gp.memset(onesf[:, :], 1.0)
            gp.memset(row[:, :], 0.0).then_inc(const_ready, 1)
            gp.memset(mask[:, :], 0.0).then_inc(const_ready, 1)
            gp.wait_ge(const_ready, 2)
            gp.affine_select(out=mask[:, S - 128:S], in_=mask[:, S - 128:S], compare_op=ALU.is_ge, fill=-1e30, base=0,
                             pattern=[[-1, 128]], channel_multiplier=1).then_inc(const_ready, 1)
            gp.wait_ge(ld_w0, LD_W0)
            gp.tensor_copy(Wcqh[:, :, :], r_cq).then_inc(hi_w, 1)
            gp.wait_ge(hi_w, 1)
            gp.tensor_tensor(Wcql[:, :, :], r_cq, Wcqh[:, :, :].bitcast(F32), ALU.subtract).then_inc(w0_ready, 1)
            gp.tensor_tensor(s_wkv, r_wkv, kvw[:, 0:1].to_broadcast([128, 2 * NOPE]), ALU.mult).then_inc(wkv_scaled, 1)
            gp.wait_ge(wkv_scaled, 1)
            gp.tensor_copy(Wkh[:, :], s_wkv).then_inc(hi_w, 1)
            gp.wait_ge(hi_w, 2)
            gp.tensor_tensor(Wkl[:, :], s_wkv, Wkh[:, :].bitcast(F32), ALU.subtract).then_inc(w0_ready, 1)

            def split(loaded, n_loaded, raw, wh, wl, wh_done, wl_done, used, n_used, u):
                hold(gp, loaded, n_loaded)
                hold(gp, used, n_used)
                gp.tensor_copy(wh, raw).then_inc(wh_done, 1)
                gp.wait_ge(wh_done, u + 1)
                gp.tensor_tensor(wl, raw, wh.bitcast(F32), ALU.subtract).then_inc(wl_done, 1)

            def inv_std(stats, v, r, s_in, n_in, s_mid, s_out, n):
                hold(gp, s_in, n_in)
                gp.tensor_tensor(v, stats, epst[:, 0:v.shape[1]], ALU.add).then_inc(s_mid, 1)
                gp.wait_ge(s_mid, n)
                gp.tensor_tensor(r, v, mhalf[:, 0:v.shape[1]], ALU.pow).then_inc(s_out, 1)

            def run(steps, p):
                for kind, off, c, bank in steps:
                    u = unit(kind, off, p)
                    if kind == "wkv":
                        split(ld_kv, 16 * u + 16, r_kv[:, :, :], Wckh[:, :, :], Wckl[:, :, :], wkv_hi, wkv_ready,
                              ready["kv"], T * u, u)
                    if kind == "wqp":
                        split(ld_qp, 48 * u + 48, r_qp[:, :, :, :], Wqph[:, :, :, :], Wqpl[:, :, :, :], wqp_hi, wqp_ready,
                              ready["qp"], 2 * u, u)
                    if kind == "wqn":
                        b = off % 2
                        split(ld_qn, 48 * u + 48, r_qn[:, :, :], Wqnh[b][:, :, :], Wqnl[b][:, :, :], wqn_hi, wqn_ready,
                              ready["qn"], 2 * (u - 1), u)
                    if kind == "wosp":
                        b = off % 2
                        split(ld_o, 16 * u + 16, r_o[:, :], Woh[b][:, :], Wol[b][:, :], wo_hi, wo_split,
                              ready["wo"], 4 * (u - 1), u)
                    if kind == "ln1":
                        q = slice(2 * c, 2 * c + 2)
                        inv_std(mvl[:, q, 1], ve[:, q], rsd[:, q], ln_ag, c + 1, ln_ve, ln_rsd, c + 1)
                    if kind == "qrs":
                        inv_std(qmv[:, :, 1], ve[:, :], rsd[:, :], qc_aggr, 1, qc_veps, qc_rstd, 1)
                    if kind == "kvn":
                        inv_std(mv[:, :, 1], veps[:, :], rstd[:, :], aggr_done, u + 1, veps_done, rstd_done, u + 1)
                    if kind == "ropek":
                        src = kvraw[:, :, :].rearrange("p t (h n) -> p t h n", h=2)[:, :, :, 0:ROPE]
                        start = isinstance(u, int) and u == 0
                        if start and c == 0:
                            gp.wait_ge(ld_c, LD_C)
                        waits = [(done["kv"], T * u + 4 * c + 4), (w0_ready, 2) if start else (ready["kp"], 4 * u)]
                        rope(gp, src, Rk, rk_mul, rk_ready, u, c, waits + ([] if start else [(rq_ready, 2 * u)]))
                    if kind == "ropeq" and not (isinstance(u, int) and u == 0):
                        rope_q(gp, u, c)

            run(numbered(PROLOGUE), 0)
            run(numbered(FIRST), 0)
            with gp.Fori(1, NP - 1) as p:
                run(numbered(MID), p)
            run(numbered(LAST), NP - 1)
            run(EPI, 0)

        @blk1.tensor
        def _(pe):
            mm = pe.matmul

            def three(o, wh, wl, xh, xl, start, stop):
                mm(o, lhsT=wh, rhs=xh, start=start, stop=False)
                mm(o, lhsT=wh, rhs=xl, start=False, stop=False)
                return mm(o, lhsT=wl, rhs=xh, start=False, stop=stop)

            def qk(h, b, i):
                if i == 0:
                    pe.wait_ge(done["qn"], count("qn", h, 1))
                    pe.wait_ge(done["kn"], count("kn", h, 1))
                    pe.wait_ge(done["kp"], count("kp", h, 1))
                    pe.wait_ge(done["qt"], count("qt", h, 1))
                wait(pe, exp_done, T * h + i - 1)
                o, q, r = SC[i % 2], tile(i), slice(64 * b, 64 * b + 64)
                for c in range(CHUNKS[i]):
                    k = slice(512 * c, min(512 * c + 512, 128 * (i + 1)))
                    mm(o[:, k], lhsT=QNh[b][:, q], rhs=KNh[b][:, k], start=True, stop=False)
                    mm(o[:, k], lhsT=QNh[b][:, q], rhs=KNl[b][:, k], start=False, stop=False)
                    mm(o[:, k], lhsT=QNl[b][:, q], rhs=KNh[b][:, k], start=False, stop=False)
                    mm(o[:, k], lhsT=QS[b][:, q], rhs=KD[b][:, k], start=False, stop=False)
                    last = mm(o[:, k], lhsT=QS[b][r, q], rhs=KL[r, k], start=False, stop=True)
                last.then_inc(sc_ready, 1)

            def tr(h, n, o):
                i = TILE_OF[n]
                c = n - CH0[i]
                if c == 0:
                    pe.wait_ge(exp_done, T * h + i + 1)
                for j in range(4 * c, min(4 * c + 4, i + 1)):
                    last = pe.transpose(o[:, tile(j - 4 * c)], Pb[i % 2][:, tile(j)], ident[:, :])
                return last

            def pv(h, b, g, o):
                if g == 0:
                    pe.wait_ge(done["v"], 2 * h + 2)
                pe.wait_ge(pt_lo, NCH * h + CH0[2 * g + 2])
                for j in range(2 * g + 2):
                    q = slice(0, 256) if j <= 2 * g else slice(128, 256)
                    last = three(o[:, q], Vh[:, j, :], Vl[:, j, :], PTh[:, j, q], PTl[:, j, q], j == 0, j == 2 * g + 1)
                return last

            def side(c, o):
                w = done["side"]
                if c == 0 or c == 1:
                    if c == 0:
                        pe.wait_ge(done["qc"], T)
                    for t in range(4):
                        last = pe.transpose(o[0:8, tile(t)], gts[:, 4 * c + t, :], ident[:, :])
                    return last
                if c == 2:
                    pe.wait_ge(side_dve, 4)
                    return mm(o[:, 0:64], lhsT=ones8, rhs=i8d[:, :], start=True, stop=True)
                if c == 3:
                    pe.wait_ge(side_dve, 5)
                    for k in range(K):
                        for t in range(T):
                            last = mm(o[:, 64 * k:64 * k + 64], lhsT=acc[:, t, tile(k)], rhs=oneh[:, t, :],
                                      start=t == 0, stop=t == T - 1)
                    return last
                pe.wait_ge(w, c)
                if c == 4:
                    for h in range(IH):
                        for k in range(K):
                            last = mm(o[:, 8 * h:8 * h + 8], lhsT=wip[:, k, tile(h)], rhs=selT[:, k, 8 * h:8 * h + 8],
                                      start=k == 0, stop=k == K - 1)
                    return last
                if c == 5:
                    mm(o[:, 0:64], lhsT=wside[:, 0, :], rhs=istT, start=True, stop=True)
                    return mm(o[:, 64:128], lhsT=wside[:, 1, :], rhs=istT, start=True, stop=True)
                if c == 6:
                    return mm(o[0:64, 0:128], lhsT=istT, rhs=wside[:, 2, :], start=True, stop=True)
                if c == 7:
                    return mm(o[0:64, 0:64], lhsT=sqT, rhs=skT, start=True, stop=True)
                if c == 8:
                    pe.wait_ge(side_dve, 9)
                    return mm(o[0:64, 0:8], lhsT=sp_s, rhs=mean8[:, :], start=True, stop=True)
                if c == 9:
                    return mm(o[:, 0:8], lhsT=svs, rhs=pms[:, :], start=True, stop=True)
                return mm(o[:, 0:8], lhsT=wside[:, 3, :], rhs=soT[:, :], start=True, stop=True)

            def use(kind, off, c, bank, p):
                u, o = unit(kind, off, p), J[bank]
                b = off % 2
                if kind == "xt":
                    if c == 0:
                        pe.wait_ge(ld_x, 32)
                    for t in range(4):
                        last = pe.transpose(o[:, tile(t)], acc[:, 4 * (c % 2) + t, tile(c // 2)], ident[:, :])
                if kind == "qc":
                    if c == 0:
                        pe.wait_ge(w0_ready, 1)
                        pe.wait_ge(done["xt"], 4)
                    for k in range(K):
                        last = three(o[:, 0:200], xTh[:, k, tile(c)], xTl[:, k, tile(c)], Wcqh[:, k, :], Wcql[:, k, :],
                                     k == 0, k == K - 1)
                if kind == "qm":
                    if c == 0:
                        pe.wait_ge(qc_norm, 1)
                    for t in range(4):
                        src = (qcm, qct)[c // 2][:, 4 * (c % 2) + t, :]
                        last = pe.transpose(o[:, tile(t)], src, ident[:, :])
                if kind == "kv":
                    if c == 0:
                        pe.wait_ge(wkv_ready, u + 1)
                    for k in range(K):
                        last = three(o[:, 0:2 * HD], xTh[:, k, tile(c)], xTl[:, k, tile(c)], Wckh[:, k, :], Wckl[:, k, :],
                                     k == 0, k == K - 1)
                if kind == "qp":
                    if c == 0:
                        pe.wait_ge(wqp_ready, u + 1)
                        if isinstance(u, int) and u == 0:
                            pe.wait_ge(done["qm"], 4)
                    for t in range(4):
                        tok = tile(4 * c + t)
                        w = [Wqph[:, r, :, :].rearrange("p h n -> p (h n)") for r in range(2)]
                        wl = [Wqpl[:, r, :, :].rearrange("p h n -> p (h n)") for r in range(2)]
                        ot = o[:, tile(t)]
                        three(ot, qch[:, tok], qcl[:, tok], w[0], wl[0], True, False)
                        mm(ot, lhsT=qcs[:, tok], rhs=w[1], start=False, stop=False)
                        last = mm(ot, lhsT=qcs[:, tok], rhs=wl[1], start=False, stop=True)
                if kind == "kt":
                    pe.wait_ge(kvn_done, 4 * (p + off // 2) + 2 * b + c + 1)
                    for t in range(4):
                        last = pe.transpose(o[:, tile(t)], kvraw[:, 4 * c + t, b * HD + ROPE:b * HD + HD], ident[:, :])
                if kind == "kp" or kind == "qt":
                    src, rdy = (Rk, rk_ready) if kind == "kp" else (Rq, rq_ready)
                    if c == 0:
                        pe.wait_ge(rdy, 2 * (p + off // 2) + 2)
                    for t in range(4):
                        a = src[:, 4 * c + t, b, :, :].rearrange("p a d -> p (a d)")
                        last = pe.transpose(o[:, tile(t)], a, ident[:, :])
                if kind == "kn":
                    if isinstance(u, int) and u == 0 and c == 0:
                        pe.wait_ge(w0_ready, 2)
                    pe.wait_ge(done["kt"], count("kt", u, c))
                    last = three(o[:, :], Wkh[:, 0:NOPE], Wkl[:, 0:NOPE], kvTh[:, half(c)], kvTl[:, half(c)], True, True)
                if kind == "qn":
                    if c == 0:
                        pe.wait_ge(wqn_ready, u + 1)
                    three(o[:, :], Wqnh[b][:, 0, :], Wqnl[b][:, 0, :], qch[:, half(c)], qcl[:, half(c)], True, False)
                    mm(o[:, :], lhsT=Wqnh[b][:, 1, :], rhs=qcs[:, half(c)], start=False, stop=False)
                    last = mm(o[:, :], lhsT=Wqnl[b][:, 1, :], rhs=qcs[:, half(c)], start=False, stop=True)
                if kind == "v":
                    pe.wait_ge(done["kt"], count("kt", u, 1))
                    for t in range(4):
                        tok = tile(4 * c + t)
                        last = three(o[:, tile(t)], kvTh[:, tok], kvTl[:, tok], Wkh[:, NOPE:], Wkl[:, NOPE:], True, True)
                if kind == "wb":
                    pe.wait_ge(ld_w0, LD_W0)
                    mm(o[:, 0:1], lhsT=r_wkv[:, 0:NOPE], rhs=kvb[:, :], start=True, stop=True)
                    last = mm(o[:, 1:2], lhsT=r_wkv[:, NOPE:], rhs=kvb[:, :], start=True, stop=True)
                if kind == "rw":
                    pe.wait_ge(io_ready, u + 1)
                    pe.wait_ge(wo_split, 2 * u + 2)
                    for hh in range(2):
                        mm(o[:, 0:D], lhsT=iobh[:, :], rhs=Woh[hh][:, :], start=hh == 0, stop=False)
                        mm(o[:, 0:D], lhsT=iobh[:, :], rhs=Wol[hh][:, :], start=False, stop=False)
                        last = mm(o[:, 0:D], lhsT=iobl[:, :], rhs=Woh[hh][:, :], start=False, stop=hh == 1)
                if kind == "wtot":
                    pe.wait_ge(abs_done, 2 * c + 2)
                    last = mm(o[:, 0:2], lhsT=onesf[:, :], rhs=asum[:, 2 * c:2 * c + 2], start=True, stop=True)
                if kind == "wt":
                    w, q = c // 4, c % 4
                    pe.wait_ge(tern_done, 4 * (w + 1))
                    for m in range(4):
                        if w < 2:
                            src = raw[w][:, 4 * (q % 2) + m, tile(q // 2)]
                        else:
                            src = raw[w][:, m % 2, tile(2 * q + m // 2)]
                        last = pe.transpose(o[:, tile(m)], src, ident[:, :])
                if kind == "ht":
                    pe.wait_ge(ln_done, c + 1)
                    for m in range(4):
                        last = pe.transpose(o[:, tile(m)], acc[:, 2 * c + m % 2, tile(m // 2)], ident[:, :])
                if kind == "tc":
                    last = tr(u, c, o)
                if kind == "pv":
                    last = pv(u, b, c, o)
                if kind == "wo":
                    pe.wait_ge(done["pv"], count("pv", u, c))
                    if c == 0:
                        pe.wait_ge(wo_split, u + 1)
                    for t in range(2):
                        last = three(o[:, 256 * t:256 * t + 256], ATh[c % 2][:, tile(t)], ATl[c % 2][:, tile(t)],
                                     Woh[b][:, :], Wol[b][:, :], True, True)
                if kind == "side":
                    if c == 0:
                        pe.wait_ge(ld_side, LD_SIDE)
                    last = side(c, o)
                last.then_inc(ready[kind], 1)

            def run(steps, p, before):
                prev = list(before)
                for kind, off, c, bank in steps:
                    if kind == "qk":
                        qk(unit(kind, off, p), off % 2, c)
                    elif kind in BANKED_ALL:
                        free = prev[-NB]
                        if free is not None and kind != "skip":
                            pe.wait_ge(done[free[0]], count(*free))
                        if kind == "skip":
                            prev.append(prev[-NB])
                        else:
                            use(kind, off, c, bank, p)
                            prev.append((kind, unit(kind, off, p), c))
                return prev[-NB:]

            def at(uses, p):
                return [(k, unit(k, off, p), c) for k, off, c in uses]

            def last_uses(steps):
                prev = [None] * NB
                for s in steps:
                    if s[0] in BANKED:
                        prev.append(s)
                    elif s[0] == "skip":
                        prev.append(prev[-NB])
                return prev[-NB:]

            run(numbered(PROLOGUE), 0, [None] * NB)
            run(numbered(FIRST), 0, at(last_uses(PROLOGUE), 0))
            assert last_uses(FIRST) == last_uses(MID)
            with pe.Fori(1, NP - 1) as p:
                run(numbered(MID), p, at(last_uses(MID), p - 1))
            run(numbered(LAST), NP - 1, at(last_uses(MID), NP - 2))
            run(EPI, 0, at(last_uses(LAST), NP - 1))

        @blk1.scalar
        def _(act):
            def copy(o, i):
                return act.activation(o, i, ACT.Copy)

            def run(steps, p):
                for kind, off, c, bank in steps:
                    u, b = unit(kind, off, p), off % 2
                    o = J[bank] if bank is not None else None
                    if kind == "exp":
                        i = c
                        act.wait_ge(nm_ready, T * u + i + 1)
                        wait(act, tp_ready, NCH * u + (CH0[i - 1] if i >= 2 else (CH0[i + 7] - NCH)))
                        if isinstance(u, int) and u == 0 and i == 0:
                            act.wait_ge(done["side"], 11)
                        w = slice(0, 128 * (i + 1))
                        act.activation(Pb[i % 2][:, w], SC[i % 2][:, w], ACT.Exp, bias=nm[:, i % 2:i % 2 + 1],
                                       scale=SCALE, accum_out=sm[:, b, i:i + 1]).then_inc(exp_done, 1)
                    if kind in ready and kind not in ("side", "wb", "wtot", "wo", "rw"):
                        act.wait_ge(ready[kind], count(kind, u, c))
                    if kind == "tc":
                        i = TILE_OF[c]
                        k = 4 * (c - CH0[i])
                        nb = min(4, i + 1 - k)
                        copy(PTh[:, k:k + nb, tile(i % 2)],
                             o[:, 0:128 * nb].rearrange("p (j q) -> p j q", j=nb)).then_inc(hi["tc"], 1)
                    if kind == "wabs":
                        w, j = c // 2, c % 2
                        if j == 0:
                            act.wait_ge(ld_mlp[w], 16)
                        if w == 2:
                            src, o = raw[2][:, j, :], junk
                        else:
                            src, o = raw[w][:, 4 * j:4 * j + 4, :], junk.rearrange("p (t d) -> p t d", t=4)
                        act.wait_ge(rq_ready, 2 * NP)
                        if c:
                            act.wait_ge(abs_done, c)
                        act.activation(o, src, ACT.Abs, accum_out=asum[:, c:c + 1]).then_inc(abs_done, 1)
                    if kind == "wt":
                        w, q = c // 4, c % 4
                        if w < 2:
                            dst = (xTh, xTl)[w][:, q // 2, half(q % 2)]
                        else:
                            dst = (KNh, KNl)[q // 2][0][:, half(q % 2)]
                        copy(dst, o[:, :]).then_inc(done["wt"], 1)
                    if kind == "ht":
                        for k in range(K):
                            ins = copy((QNh, QNl)[k][0][:, 256 * c:256 * c + 256], o[:, 256 * k:256 * k + 256])
                        ins.then_inc(hi["ht"], 1)
                    if kind == "xt":
                        copy(xTh[:, c // 2, half(c % 2)], o[:, :]).then_inc(hi["xt"], 1)
                    if kind == "qc":
                        copy(qcm[:, c, :], o[:, 0:128])
                        copy(qct[:, c, :].rearrange("p (a n) -> p a n", a=2),
                             o[:, 128:QL].rearrange("p (a n) -> p a n", a=1).to_broadcast([128, 2, QLT]))
                        copy(gts[:, c, :], o[:, QL:QL + IH]).then_inc(hi["qc"], 1)
                    if kind == "qm":
                        if c == 0:
                            act.wait_ge(ld_c, LD_C)
                        w, bb = (0, 1) if c < 2 else (2, 3)
                        act.activation(o[:, :], o[:, :], ACT.Identity, bias=qnwb[:, bb:bb + 1],
                                       scale=qnwb[:, w:w + 1]).then_inc(qm_scaled, 1)
                        act.wait_ge(qm_scaled, c + 1)
                        copy((qch if c < 2 else qcs)[:, half(c % 2)], o[:, :]).then_inc(hi["qm"], 1)
                    if kind == "kv":
                        if c == 0:
                            wait(act, rk_ready, 2 * u)
                        copy(kvraw[:, c, :], o[:, 0:2 * HD]).then_inc(done["kv"], 1)
                    if kind == "qp":
                        if c == 0 and isinstance(u, int) and u == 0:
                            act.wait_ge(side_dve, 2)
                        elif c == 0:
                            act.wait_ge(rq_ready, 2 * u)
                        copy(qraw[:, 4 * c:4 * c + 4, :, :].rearrange("p t h n -> p (t h n)"), o[:, :]).then_inc(done["qp"], 1)
                    if kind == "kt":
                        copy(kvTh[:, half(c)], o[:, :]).then_inc(hi["kt"], 1)
                    if kind == "kp":
                        copy(KD[b][:, half(c)], o[:, :]).then_inc(hi["kp"], 1)
                    if kind == "qt":
                        copy(QS[b][:, half(c)], o[:, :]).then_inc(hi["qt"], 1)
                    if kind == "kn":
                        if isinstance(u, int) and u == 0 and c == 0:
                            act.wait_ge(done["wb"], 1)
                        act.activation(KNh[b][:, half(c)], o[:, :], ACT.Identity, bias=kvbias[:, 0:1]).then_inc(hi["kn"], 1)
                    if kind == "qn":
                        copy(QNh[b][:, half(c)], o[:, :]).then_inc(hi["qn"], 1)
                    if kind == "v":
                        copy(Vh[:, 4 * c:4 * c + 4, :].rearrange("p t n -> p (t n)"), o[:, :]).then_inc(hi["v"], 1)
                    if kind == "pv":
                        wait(act, ready["wo"], 4 * u + c - 1)
                        copy(ATh[c % 2][:, :], o[:, 0:256]).then_inc(hi["pv"], 1)
                    if kind == "side" and c == 7:
                        act.wait_ge(side_dve, 7)
                        act.activation(sp_s, o[0:64, 0:64], ACT.Exp, bias=smx[:, 1:2], scale=SCALE_SIDE,
                                       accum_out=smx[:, 2:3]).then_inc(side_exp, 1)

            run(numbered(PROLOGUE), 0)
            run(numbered(FIRST), 0)
            with act.Fori(1, NP - 1) as p:
                run(numbered(MID), p)
            run(numbered(LAST), NP - 1)
            run(EPI, 0)

        @blk1.vector
        def _(dve):
            def lo(kind, u, c, o, i, h):
                dve.wait_ge(hi[kind], count(kind, u, c))
                dve.tensor_tensor(o, i, h.bitcast(F32), ALU.subtract).then_inc(done[kind], 1)

            def side(c, o):
                n = count("side", 0, c)
                dve.wait_ge(ready["side"], n)
                cp = dve.tensor_copy
                d = done["side"]
                if c in (0, 1):
                    cp(gT[:, half(c)], o[0:8, :]).then_inc(d, 1)
                if c == 1:
                    dve.wait_ge(d, 2)
                    dve.max(m8[:, :], gT).then_inc(side_dve, 1)
                    dve.wait_ge(side_dve, 1)
                    dve.max_index(i8[:, :], m8[:, :], gT).then_inc(side_dve, 1)
                    dve.wait_ge(side_dve, 2)
                    cp(i8f[:, :], i8[:, :]).then_inc(side_dve, 1)
                    dve.wait_ge(side_dve, 3)
                    a = i8f[:, :].rearrange("p (a k) -> p a k", a=1).to_broadcast([8, 8, 8])
                    dve.wait_ge(ld_side, LD_SIDE)
                    dve.tensor_tensor(i8d[:, :].rearrange("p (h k) -> p h k", h=8), a,
                                      blk[:, :].rearrange("p (h k) -> p h k", h=8), ALU.mult).then_inc(side_dve, 1)
                if c == 2:
                    cp(idxb, o[:, 0:64]).then_inc(d, 1)
                    dve.wait_ge(d, 3)
                    a = idxb.rearrange("p (a n) -> p a n", a=1).to_broadcast([128, T, 64])
                    bb = tokid[:, :].rearrange("p (t a) -> p t a", a=1).to_broadcast([128, T, 64])
                    dve.tensor_tensor(oneh[:, :, :], a, bb, ALU.is_equal).then_inc(side_dve, 1)
                if c == 3:
                    cp(selT[:, :, :].rearrange("p k n -> p (k n)"), o[:, 0:128]).then_inc(d, 1)
                if c == 4:
                    cp(istT, o[:, 0:64]).then_inc(d, 1)
                if c == 5:
                    cp(sqT, o[:, 0:64])
                    cp(skT, o[:, 64:128]).then_inc(d, 1)
                if c == 6:
                    cp(svs, o[0:64, 0:128]).then_inc(d, 1)
                if c == 7:
                    dve.tensor_tensor_reduce(out=o[0:64, 0:64], in0=o[0:64, 0:64], in1=off64[:, :], scale=1.0, scalar=LOW,
                                             op0=ALU.add, op1=ALU.max, accum_out=smx[:, 0:1]).then_inc(side_dve, 1)
                    dve.wait_ge(side_dve, 6)
                    dve.tensor_scalar(smx[:, 1:2], smx[:, 0:1], -SCALE_SIDE, None, ALU.mult).then_inc(side_dve, 1)
                    dve.wait_ge(side_exp, 1)
                    dve.reciprocal(smx[:, 3:4], smx[:, 2:3]).then_inc(side_dve, 1)
                    dve.wait_ge(side_dve, 8)
                    dve.tensor_scalar(sp_s, sp_s, smx[:, 3:4], None, ALU.mult).then_inc(side_dve, 1)
                    dve.wait_ge(side_dve, 9)
                    dve.sem_inc(d, 1)
                if c == 8:
                    cp(pms[:, :], o[0:64, 0:8]).then_inc(d, 1)
                if c == 9:
                    cp(soT[:, :], o[:, 0:8]).then_inc(d, 1)
                if c == 10:
                    dve.wait_ge(done["wb"], 1)
                    dve.tensor_scalar(ioT[:, :], o[:, 0:8], kvbias[:, 1:2], None, ALU.add).then_inc(d, 1)

            def run(steps, p):
                for kind, off, c, bank in steps:
                    u, b = unit(kind, off, p), off % 2
                    o = J[bank] if bank is not None else None
                    if kind == "qk":
                        i = c
                        w = slice(0, 128 * (i + 1))
                        hold(dve, sc_ready, T * u + i + 1)
                        dve.tensor_tensor_reduce(out=SC[i % 2][:, w], in0=SC[i % 2][:, w], in1=mask[:, 128 * (7 - i):S],
                                                 scale=1.0, scalar=LOW, op0=ALU.add, op1=ALU.max,
                                                 accum_out=mx[:, i % 2:i % 2 + 1]).then_inc(mx_ready, 1)
                        dve.wait_ge(mx_ready, T * u + i + 1)
                        dve.tensor_scalar(nm[:, i % 2:i % 2 + 1], mx[:, i % 2:i % 2 + 1], -SCALE, None, ALU.mult).then_inc(nm_ready, 1)
                    if kind == "tc":
                        i = TILE_OF[c]
                        k = 4 * (c - CH0[i])
                        nb = min(4, i + 1 - k)
                        dst = (slice(None), slice(k, k + nb), tile(i % 2))
                        lo("tc", u, c, PTl[dst], o[:, 0:128 * nb].rearrange("p (j q) -> p j q", j=nb), PTh[dst])
                    if kind == "xt":
                        d = (slice(None), c // 2, half(c % 2))
                        lo("xt", 0, c, xTl[d], o[:, :], xTh[d])
                    if kind == "qc":
                        dve.wait_ge(hi["qc"], c + 1)
                        dve.bn_stats(qst[:, c, :], o[:, 0:QL]).then_inc(done["qc"], 1)
                        if c == T - 1:
                            dve.wait_ge(done["qc"], T)
                            for t in range(T):
                                ins = dve.bn_aggr(qmv[:, t, :], qst[:, t, :])
                            ins.then_inc(qc_aggr, 1)
                    if kind == "qnorm":
                        dve.wait_ge(qc_rstd, 1)
                        dve.wait_ge(qc_aggr, 1)
                        for t in range(T):
                            for v in (qcm, qct):
                                ins = dve.tensor_scalar(v[:, t, :], v[:, t, :], qmv[:, t, 0:1], rsd[:, t:t + 1],
                                                        ALU.subtract, ALU.mult)
                        ins.then_inc(qc_norm, 1)
                    if kind == "qm":
                        q = half(c % 2)
                        if c < 2:
                            lo("qm", 0, c, qcl[:, q], o[:, :], qch[:, q])
                        else:
                            lo("qm", 0, c, qcs[64:128, q], o[64:128, :], qcs[64:128, q])
                    if kind == "kv":
                        dve.wait_ge(done["kv"], count("kv", u, c))
                        for hh in range(2):
                            ins = dve.bn_stats(bst[:, c, hh, :], kvraw[:, c, hh * HD + ROPE:hh * HD + HD])
                        ins.then_inc(bn_done, 1)
                    if kind == "ropeq" and isinstance(u, int) and u == 0:
                        rope_q(dve, u, c)
                    if kind == "kvn":
                        hold(dve, bn_done, T * (u + 1))
                        for t in range(T):
                            for hh in range(2):
                                ins = dve.bn_aggr(mv[:, 2 * t + hh, :], bst[:, t, hh, :])
                        ins.then_inc(aggr_done, 1)
                    if kind == "kvn2":
                        dve.wait_ge(rstd_done, u + 1)
                        hh = c // 2
                        for t in range(4 * (c % 2), 4 * (c % 2) + 4):
                            v = kvraw[:, t, hh * HD + ROPE:hh * HD + HD]
                            n = 2 * t + hh
                            ins = dve.tensor_scalar(v, v, mv[:, n, 0:1], rstd[:, n:n + 1], ALU.subtract, ALU.mult)
                        ins.then_inc(kvn_done, 1)
                    if kind == "wtot":
                        w = slice(c, c + 1)
                        dve.wait_ge(ready["wtot"], c + 1)
                        dve.tensor_copy(asum[:, 2 * c:2 * c + 2], o[:, 0:2]).then_inc(done["wtot"], 1)
                        dve.wait_ge(done["wtot"], c + 1)
                        dve.tensor_tensor(scl[:, w], asum[:, 2 * c:2 * c + 1], asum[:, 2 * c + 1:2 * c + 2],
                                          ALU.add).then_inc(tot_done, 1)
                        dve.wait_ge(tot_done, c + 1)
                        dve.tensor_scalar(scl[:, w], scl[:, w], 1.0 / (D * E), 1e-8, ALU.mult, ALU.add).then_inc(scl_ready, 1)
                        dve.wait_ge(scl_ready, c + 1)
                        dve.tensor_scalar(thr[:, w], scl[:, w], 0.5, None, ALU.mult)
                        dve.tensor_scalar(nthr[:, w], scl[:, w], -0.5, None, ALU.mult).then_inc(thr_ready, 1)
                    if kind == "tern":
                        w, j = c // 4, c % 4
                        if w == 2:
                            v, lw = raw[2][:, j // 2, half(j % 2)], low[c % 2]
                        else:
                            v, lw = raw[w][:, 2 * j:2 * j + 2, :], low[c % 2].rearrange("p (t d) -> p t d", t=2)
                        if j == 0:
                            dve.wait_ge(thr_ready, w + 1)
                        if c == 0:
                            dve.wait_ge(rq_ready, 2 * NP)
                        if c >= 2:
                            dve.wait_ge(tern_done, c - 1)
                        dve.tensor_scalar(lw, v, nthr[:, w:w + 1], None, ALU.is_lt).then_inc(low_done, 1)
                        dve.wait_ge(low_done, c + 1)
                        dve.scalar_tensor_tensor(v, v, thr[:, w:w + 1], lw, ALU.is_gt, ALU.subtract).then_inc(tern_done, 1)
                    if kind == "ln1":
                        dve.wait_ge(done["wo"], count("wo", NH - 1, c))
                        for t in range(2 * c, 2 * c + 2):
                            ins = dve.bn_stats(st[:, t, :], acc[:, t, :])
                        ins.then_inc(ln_st, 1)
                        dve.wait_ge(ln_st, c + 1)
                        for t in range(2 * c, 2 * c + 2):
                            ins = dve.bn_aggr(mvl[:, t, :], st[:, t, :])
                        ins.then_inc(ln_ag, 1)
                    if kind == "ln1n":
                        dve.wait_ge(ln_rsd, c + 1)
                        for t in range(2 * c, 2 * c + 2):
                            ins = dve.tensor_scalar(acc[:, t, :], acc[:, t, :], mvl[:, t, 0:1], rsd[:, t:t + 1],
                                                    ALU.subtract, ALU.mult)
                        ins.then_inc(ln_done, 1)
                    if kind == "ht":
                        dve.wait_ge(hi["ht"], c + 1)
                        for k in range(K):
                            q = slice(256 * c, 256 * c + 256)
                            ins = dve.tensor_tensor((QS, KD)[k][0][:, q], o[:, 256 * k:256 * k + 256],
                                                    (QNh, QNl)[k][0][:, q].bitcast(F32), ALU.subtract)
                        ins.then_inc(done["ht"], 1)
                    if kind == "wb":
                        dve.wait_ge(ready["wb"], 1)
                        dve.tensor_copy(kvbias[:, :], o[:, 0:2]).then_inc(done["wb"], 1)
                    if kind == "kt":
                        lo("kt", u, c, kvTl[:, half(c)], o[:, :], kvTh[:, half(c)])
                    if kind == "v":
                        lo("v", u, c, Vl[:, 4 * c:4 * c + 4, :].rearrange("p t n -> p (t n)"), o[:, :],
                           Vh[:, 4 * c:4 * c + 4, :].rearrange("p t n -> p (t n)"))
                    if kind == "kn":
                        if isinstance(u, int) and u == 0 and c == 0:
                            dve.wait_ge(done["wb"], 1)
                        dve.wait_ge(hi["kn"], count("kn", u, c))
                        dve.scalar_tensor_tensor(KNl[b][:, half(c)], o[:, :], kvbias[:, 0:1], KNh[b][:, half(c)].bitcast(F32),
                                                 ALU.add, ALU.subtract).then_inc(done["kn"], 1)
                    if kind == "qn":
                        lo("qn", u, c, QNl[b][:, half(c)], o[:, :], QNh[b][:, half(c)])
                    if kind == "kp":
                        r = slice(64 * b, 64 * b + 64)
                        lo("kp", u, c, KL[r, half(c)], o[r, :], KD[b][r, half(c)])
                    if kind == "qt":
                        r = slice(64 * (1 - b), 64 * (1 - b) + 64)
                        lo("qt", u, c, QS[b][r, half(c)], o[r, :], QS[b][r, half(c)])
                    if kind == "io":
                        if isinstance(p, int):
                            if p == 0:
                                dve.wait_ge(done["side"], 11)
                            col = ioT[:, p:p + 1].to_broadcast([128, 128])
                        else:
                            col = ioT[:, bass.ds(p, 1)].to_broadcast([128, 128])
                        dve.tensor_copy(iobh[:, :], col).then_inc(io_hi, 1)
                        dve.wait_ge(io_hi, u + 1)
                        dve.tensor_tensor(iobl[:, :], col, iobh[:, :].bitcast(F32), ALU.subtract).then_inc(io_ready, 1)
                    if kind == "rw":
                        if isinstance(u, int) and u == 0:
                            dve.wait_ge(const_ready, 3)
                        dve.wait_ge(ready["rw"], u + 1)
                        dve.tensor_tensor(row[:, :], o[:, 0:D], row[:, :], ALU.add).then_inc(done["rw"], 1)
                    if kind == "rowadd":
                        dve.wait_ge(done["rw"], NP)
                        a = acc[:, 2 * c:2 * c + 2, :]
                        rb = row[:, :].rearrange("p (a n) -> p a n", a=1).to_broadcast([128, 2, D])
                        dve.tensor_tensor(a, a, rb, ALU.add).then_inc(row_added, 1)
                    if kind == "pv":
                        lo("pv", u, c, ATl[c % 2][:, :], o[:, 0:256], ATh[c % 2][:, :])
                    if kind == "wo":
                        dve.wait_ge(ready["wo"], count("wo", u, c))
                        dve.reciprocal(rs[:, b, 2 * c:2 * c + 2], sm[:, b, 2 * c:2 * c + 2]).then_inc(rs_ready, 1)
                        if isinstance(u, int) and u == NH - 1:
                            dve.wait_ge(row_added, c + 1)
                        dve.wait_ge(rs_ready, count("wo", u, c))
                        for t in range(2):
                            a = acc[:, 2 * c + t, :]
                            ins = dve.scalar_tensor_tensor(a, o[:, D * t:D * t + D], rs[:, b, 2 * c + t:2 * c + t + 1], a,
                                                           ALU.mult, ALU.add)
                        ins.then_inc(done["wo"], 1)
                    if kind == "side":
                        side(c, o)

            run(numbered(PROLOGUE), 0)
            run(numbered(FIRST), 0)
            with dve.Fori(1, NP - 1) as p:
                run(numbered(MID), p)
            run(numbered(LAST), NP - 1)
            run(EPI, 0)

        block.close()
        stack.pop()
        attn.close()

        down = [(KNh, KNl)[e // 4][0][:, D * (e % 4):D * (e % 4) + D] for e in range(E // 128)]
        mlp(nc, top, SC, J, acc, ident, mhalf, epst, (xTh, xTl), down, (QNh[0], QNl[0]), (QS[0], KD[0]),
            scl, st, mvl, ve, rsd, out)


def mlp(nc, top, SC, J, acc, ident, mhalf, epst, upgateT, downT, hTh, hTl, scl, st, mvl, ve, rsd, out):
    def sb(name, shape, dt=F32):
        return top.enter_context(nc.sbuf_tensor(name, shape, dt))

    def sem(name):
        return top.enter_context(nc.semaphore(name))

    ET = E // 128
    N = 2 * ET
    LAG = 3
    HB = 4
    sg = [sb(f"sg{i}", [128, 512]) for i in range(2)]
    tt = [sb(f"tt{i}", [128, 512]) for i in range(2)]
    hid = [sb(f"hid{i}", [128, 512]) for i in range(2)]
    Hh, Hl = [sb(f"Hh{i}", [128, 512], F32R) for i in range(HB)], [sb(f"Hl{i}", [128, 512], F32R) for i in range(HB)]
    st2, mv2 = sb("st2", [128, T, 6]), sb("mv2", [128, T, 2])
    ve2, rsd2 = sb("ve2", [128, T]), sb("rsd2", [128, T])
    yo = sb("yo", [128, T, D])

    st_done, ag_done, ve_done, rsd_ready, ln_done = (sem("st_done"), sem("ag_done"), sem("ve_done"),
                                                     sem("rsd_ready"), sem("ln2_done"))
    ht_ready, ht_hi, ht_done = sem("ht2_ready"), sem("ht2_hi"), sem("ht2_done")
    ug_ready, sg_done, tt_done, hid_done, hh_done, hl_done = (sem("ug_ready"), sem("sg_done"), sem("tt_done"),
                                                              sem("hid_done"), sem("hh_done"), sem("hl_done"))
    dn_ready, y_done, y_st, y_ag, y_ve, y_rsd, y_ln, stored = (sem("dn_ready"), sem("y_done"), sem("y_st"), sem("y_ag"),
                                                               sem("y_ve"), sem("y_rsd"), sem("y_ln"), sem("stored"))

    def tile(t):
        return slice(128 * t, 128 * t + 128)

    UG = [(SC[0][:, 0:512], SC[0][:, 512:1024]), (SC[1][:, 0:512], SC[1][:, 512:1024])]
    DN = [J[t][:, 0:D] for t in range(4)]

    with nc.Block() as blk2:
        @blk2.sync
        def _(sp):
            for c in range(4):
                sp.wait_ge(y_ln, c + 1)
                sp.dma_start(out[256 * c:256 * c + 256, :].rearrange("(t p) d -> p t d", p=128),
                             yo[:, 2 * c:2 * c + 2, :]).then_inc(stored, 16)
            sp.wait_ge(stored, 64)

        @blk2.gpsimd
        def _(gp):
            gp.wait_ge(ag_done, 1)
            gp.tensor_tensor(ve[:, 4:T], mvl[:, 4:T, 1], epst[:, 0:4], ALU.add).then_inc(ve_done, 1)
            gp.wait_ge(ve_done, 1)
            gp.tensor_tensor(rsd[:, 4:T], ve[:, 4:T], mhalf[:, 0:4], ALU.pow).then_inc(rsd_ready, 1)
            for n in range(N):
                gp.wait_ge(hh_done, n + 1)
                gp.tensor_tensor(Hl[n % HB][:, :], hid[n % 2][:, :], Hh[n % HB][:, :].bitcast(F32),
                                 ALU.subtract).then_inc(hl_done, 1)
                if n == ET + LAG or n == N - 1:
                    c = n // (N - 1)
                    gp.wait_ge(y_ag, c + 1)
                    q = slice(4 * c, 4 * c + 4)
                    gp.tensor_tensor(ve2[:, q], mv2[:, q, 1], epst[:, 0:4], ALU.add).then_inc(y_ve, 1)
                    gp.wait_ge(y_ve, c + 1)
                    gp.tensor_tensor(rsd2[:, q], ve2[:, q], mhalf[:, 0:4], ALU.pow).then_inc(y_rsd, 1)

        @blk2.tensor
        def _(pe):
            mm = pe.matmul

            def up_gate(n):
                tok, e = slice(512 * (n // ET), 512 * (n // ET) + 512), n % ET
                if n >= 2:
                    pe.wait_ge(hid_done, n - 1)
                if n == ET:
                    pe.wait_ge(ht_done, 2)
                for w in range(2):
                    for k in range(K):
                        wt = upgateT[w][:, k, tile(e)]
                        mm(UG[n % 2][w], lhsT=wt, rhs=hTh[k][:, tok], start=k == 0, stop=False)
                        last = mm(UG[n % 2][w], lhsT=wt, rhs=hTl[k][:, tok], start=False, stop=k == K - 1)
                last.then_inc(ug_ready, 1)

            def down(n):
                e = n % ET
                pe.wait_ge(hl_done, n + 1)
                if n == 0:
                    pe.wait_ge(ht_done, 2)
                if n == ET:
                    pe.wait_ge(y_done, 4)
                for t in range(4):
                    mm(DN[t], lhsT=Hh[n % HB][:, tile(t)], rhs=downT[e], start=e == 0, stop=False)
                    last = mm(DN[t], lhsT=Hl[n % HB][:, tile(t)], rhs=downT[e], start=False, stop=e == ET - 1)
                last.then_inc(dn_ready, 1)

            for n in range(N):
                up_gate(n)
                if n == 1:
                    pe.wait_ge(ln_done, 1)
                    for c in range(2):
                        for m in range(4):
                            last = pe.transpose(J[c][:, tile(m)], acc[:, 4 + 2 * c + m % 2, tile(m // 2)], ident[:, :])
                        last.then_inc(ht_ready, 1)
                if n >= LAG:
                    down(n - LAG)
            for n in range(N - LAG, N):
                down(n)

        @blk2.scalar
        def _(act):
            def hidden_hi(n):
                act.wait_ge(hid_done, n + 1)
                if n >= HB:
                    act.wait_ge(dn_ready, n - HB + 1)
                act.activation(Hh[n % HB][:, :], hid[n % 2][:, :], ACT.Copy).then_inc(hh_done, 1)

            for n in range(N):
                if n == 2:
                    for c in range(2):
                        act.wait_ge(ht_ready, c + 1)
                        for k in range(K):
                            ins = act.activation(hTh[k][:, 512 + 256 * c:768 + 256 * c], J[c][:, 256 * k:256 * k + 256], ACT.Copy)
                        ins.then_inc(ht_hi, 1)
                act.wait_ge(ug_ready, n + 1)
                if n >= 2:
                    act.wait_ge(tt_done, n - 1)
                act.activation(sg[n % 2][:, :], UG[n % 2][0], ACT.Sigmoid, scale=scl[:, 0:1]).then_inc(sg_done, 1)
                if n >= 1:
                    hidden_hi(n - 1)
            hidden_hi(N - 1)

        @blk2.vector
        def _(dve):
            for t in range(4, T):
                ins = dve.bn_stats(st[:, t, :], acc[:, t, :])
            ins.then_inc(st_done, 1)
            dve.wait_ge(st_done, 1)
            for t in range(4, T):
                ins = dve.bn_aggr(mvl[:, t, :], st[:, t, :])
            ins.then_inc(ag_done, 1)
            dve.wait_ge(rsd_ready, 1)
            dve.wait_ge(ag_done, 1)
            for t in range(4, T):
                ins = dve.tensor_scalar(acc[:, t, :], acc[:, t, :], mvl[:, t, 0:1], rsd[:, t:t + 1], ALU.subtract, ALU.mult)
            ins.then_inc(ln_done, 1)

            def residual(c):
                dve.wait_ge(dn_ready, ET * (c + 1))
                for t in range(4):
                    dve.scalar_tensor_tensor(yo[:, 4 * c + t, :], DN[t], scl[:, 2:3], acc[:, 4 * c + t, :], ALU.mult,
                                             ALU.add).then_inc(y_done, 1)

            def out_stats(c):
                for t in range(4 * c, 4 * c + 4):
                    dve.wait_ge(y_done, t + 1)
                    dve.bn_stats(st2[:, t, :], yo[:, t, :]).then_inc(y_st, 1)
                dve.wait_ge(y_st, 4 * c + 4)
                for t in range(4 * c, 4 * c + 4):
                    ins = dve.bn_aggr(mv2[:, t, :], st2[:, t, :])
                ins.then_inc(y_ag, 1)

            def out_norm(c):
                dve.wait_ge(y_rsd, c + 1)
                dve.wait_ge(y_ag, c + 1)
                for t in range(4 * c, 4 * c + 4):
                    ins = dve.tensor_scalar(yo[:, t, :], yo[:, t, :], mv2[:, t, 0:1], rsd2[:, t:t + 1], ALU.subtract,
                                            ALU.mult)
                    if t % 2 == 1:
                        ins.then_inc(y_ln, 1)

            for n in range(N):
                if n == 2:
                    for c in range(2):
                        dve.wait_ge(ht_hi, c + 1)
                        for k in range(K):
                            q = slice(512 + 256 * c, 768 + 256 * c)
                            ins = dve.tensor_tensor(hTl[k][:, q], J[c][:, 256 * k:256 * k + 256], hTh[k][:, q].bitcast(F32),
                                                    ALU.subtract)
                        ins.then_inc(ht_done, 1)
                dve.wait_ge(sg_done, n + 1)
                dve.scalar_tensor_tensor(tt[n % 2][:, :], UG[n % 2][0], scl[:, 0:1], sg[n % 2][:, :], ALU.mult,
                                         ALU.mult).then_inc(tt_done, 1)
                dve.wait_ge(tt_done, n + 1)
                if n >= 2:
                    dve.wait_ge(hl_done, n - 1)
                dve.scalar_tensor_tensor(hid[n % 2][:, :], UG[n % 2][1], scl[:, 1:2], tt[n % 2][:, :], ALU.mult,
                                         ALU.mult).then_inc(hid_done, 1)
                if n == ET + LAG - 1:
                    residual(0)
                if n == ET + LAG:
                    out_stats(0)
                if n == ET + LAG + 2:
                    out_norm(0)
            residual(1)
            out_stats(1)
            out_norm(1)


INPUTS = ["L0_attn_x", "L0_attn_W_cq", "L0_attn_q_norm_w", "L0_attn_q_norm_b", "L0_attn_W_q", "L0_attn_W_ckv",
          "L0_attn_kv_norm_w", "L0_attn_kv_norm_b", "L0_attn_W_kv", "L0_attn_W_o", "L0_attn_W_ip", "L0_attn_W_ig",
          "L0_attn_W_sq", "L0_attn_W_sk", "L0_attn_W_sv", "L0_attn_W_io", "L0_ffn_W_up", "L0_ffn_W_gate",
          "L0_ffn_W_down"]


def constants():
    import numpy as np
    freqs = (1.0 / np.power(np.float32(10000.0), np.arange(0, ROPE, 2, dtype=np.float32) / np.float32(ROPE))).astype(np.float32)
    f = np.outer(np.arange(S, dtype=np.float32), freqs).astype(np.float32)
    cos, sin = np.cos(f).astype(np.float32), np.sin(f).astype(np.float32)
    col = np.arange(64)
    return {
        "c_ident": np.eye(128, dtype=np.float32),
        "c_cos": np.repeat(cos, 2, axis=1),
        "c_sin": np.stack([-sin, sin], axis=-1).reshape(S, ROPE),
        "c_tok": (np.arange(128)[:, None] + 128 * np.arange(T)[None, :]).astype(np.float32),
        "c_blk": (np.arange(8)[:, None] == col[None, :] // TOPK).astype(np.float32),
        "c_off": np.where(col[:, None] // TOPK == col[None, :] // TOPK, 0.0, -1e30).astype(np.float32),
        "c_mean": ((col[:, None] // TOPK == np.arange(8)[None, :]) / TOPK).astype(np.float32),
    }


def kernel(**inputs):
    import numpy as np
    import concourse.bacc as bacc
    from concourse.bass_utils import run_bass_kernel_spmd

    nc = bacc.Bacc("TRN2", target_bir_lowering=False, num_devices=1)
    arrays, args = {}, []
    for name in INPUTS:
        a = np.ascontiguousarray(inputs[name])
        if name == "L0_attn_x":
            a = a.reshape(S, D)
        arrays[f"in_{name}"] = a
    for name, a in constants().items():
        arrays[f"in_{name}"] = np.ascontiguousarray(a)
    for name, a in arrays.items():
        args.append(nc.dram_tensor(name, a.shape, mybir.dt.from_np(a.dtype), kind="ExternalInput").ap())
    args.append(nc.dram_tensor("out", (S, D), F32, kind="ExternalOutput").ap())
    attention_and_mlp(nc, *args)
    r = run_bass_kernel_spmd(nc, [arrays], core_ids=[0])
    return r.results[0]["out"].reshape(1, S, D)
```
